# Optimizing a Trainium2 kernel written in Bass

```python
import numpy as np
import jax
import jax.numpy as jnp

def _softmax(x, axis=-1):
    return jax.nn.softmax(x, axis=axis)

def _gelu(x):
    return jax.nn.gelu(x, approximate=True)

def _silu(x):
    return jax.nn.silu(x)

def _sigmoid(x):
    return jax.nn.sigmoid(x)

def _layernorm(x, axis=-1, eps=1e-05):
    m = jnp.mean(x, axis=axis, keepdims=True)
    v = jnp.var(x, axis=axis, keepdims=True)
    return (x - m) / jnp.sqrt(v + eps)

def _scatter_add(tgt, idx, src, axis=0):
    return tgt.at[idx].add(src)

def _segment_sum(src, seg, n):
    return jax.ops.segment_sum(src, seg, n)
kernel_name = 'mk_xattn_ffn_d2_seqx_r8_981202'

def setup_inputs(seed: int=0):
    np.random.seed(seed)
    _w = jnp.asarray

    def _rec_inputs():
        import jax
        import jax.numpy as jnp
        _rk = jax.random.key(seed)
        x = 7.22e-05 + 1 * jax.random.normal(jax.random.fold_in(_rk, 1), (8, 128, 512), jnp.float32)
        _lenS = 128 - jax.random.randint(jax.random.fold_in(_rk, 7), (8,), 0, max(1, 128 // 4) + 1, jnp.int32)
        _lenS2 = 128 - jax.random.randint(jax.random.fold_in(_rk, 8), (8,), 0, max(1, 128 // 4) + 1, jnp.int32)
        _ctx_4096P = jax.random.normal(jax.random.fold_in(_rk, 11), (8, 16, 512), jnp.float32)
        _ctx_4096c = jax.random.dirichlet(jax.random.fold_in(_rk, 511), 0.3 * jnp.ones((16,), jnp.float32), (8, 128))
        _ctx_4096t = jnp.einsum('bsk,bkd->bsd', _ctx_4096c, _ctx_4096P)
        _ctx_4096t = _ctx_4096t * jax.lax.rsqrt(jnp.mean(jnp.square(_ctx_4096t)) + 1e-12) * 0.953939
        ctx_4096 = 4.13588e-05 + 0.999923 * (_ctx_4096t + 0.3 * jax.random.normal(jax.random.fold_in(_rk, 611), (8, 128, 512), jnp.float32))
        return (x, ctx_4096)
    x, ctx_4096 = _rec_inputs()

    def _L0_xattn_setup():
        import jax, jax.numpy as jnp
        import numpy as np
        DIM = 512
        NUM_HEADS = 32
        NUM_KV_HEADS = 8
        HEAD_DIM = DIM // NUM_HEADS
        KV_DIM = DIM // (NUM_HEADS // NUM_KV_HEADS)
        B, S = (1, 256)
        key = jax.random.key(seed)
        ks = jax.random.split(key, 7)
        w_scale = DIM ** (-0.5)
        return {'query': jax.random.normal(ks[0], (B, S, DIM), jnp.float32), 'key': jax.random.normal(ks[1], (B, S, DIM), jnp.float32), 'value': jax.random.normal(ks[2], (B, S, DIM), jnp.float32), 'Wq': jax.random.normal(ks[3], (DIM, DIM), jnp.float32) * w_scale, 'Wk': jax.random.normal(ks[4], (DIM, KV_DIM), jnp.float32) * w_scale, 'Wv': jax.random.normal(ks[5], (DIM, KV_DIM), jnp.float32) * w_scale, 'Wo': jax.random.normal(ks[6], (DIM, DIM), jnp.float32) * w_scale}
    _L0_xattn_all = _L0_xattn_setup()
    _L0_xattn_in = {k: v for k, v in _L0_xattn_all.items() if k in ('Wq', 'Wk', 'Wv', 'Wo')}
    del _L0_xattn_all

    def _L0_ffn_setup():
        import jax, jax.numpy as jnp
        import numpy as np
        LORA_RANK = 16
        LORA_ALPHA = 16
        LORA_SCALE = LORA_ALPHA / LORA_RANK
        key = jax.random.key(seed)
        k1, k2, k3, k4, k5 = jax.random.split(key, 5)
        B, S, D_IN, D_OUT, N_LORA, R = (8, 256, 512, 512, 3, LORA_RANK)
        std = 1.0 / np.sqrt(D_IN)
        x = jax.random.normal(k1, (B, S, D_IN), dtype=jnp.float32)
        weight = jax.random.truncated_normal(k2, -3.0, 3.0, (D_OUT, D_IN), dtype=jnp.float32) * std
        bias = jax.random.normal(k3, (D_OUT,), dtype=jnp.float32) * 0.01
        lora_A = jax.random.normal(k4, (N_LORA, R, D_IN), dtype=jnp.float32) * std
        lora_B = jax.random.normal(k5, (N_LORA, D_OUT, R), dtype=jnp.float32) * 0.02
        lora_start_indices = jnp.arange(4, dtype=jnp.int64) * 2
        return {'x': x, 'weight': weight, 'bias': bias, 'lora_A': lora_A, 'lora_B': lora_B, 'lora_start_indices': lora_start_indices}
    _L0_ffn_all = _L0_ffn_setup()
    _L0_ffn_in = {k: v for k, v in _L0_ffn_all.items() if k in ('weight', 'bias', 'lora_A', 'lora_B', 'lora_start_indices')}
    del _L0_ffn_all

    def _L1_xattn_setup():
        import jax, jax.numpy as jnp
        import numpy as np
        B, S, D = (2, 197, 512)
        HEADS = 16
        key = jax.random.key(seed)
        ks = jax.random.split(key, 9)
        inp = {'q': jax.random.normal(ks[0], (B, S, D), dtype=jnp.float32), 'v': jax.random.normal(ks[1], (B, S, D), dtype=jnp.float32), 'k': jax.random.normal(ks[2], (B, S, D), dtype=jnp.float32), 'Wq': jax.random.normal(ks[3], (D, D), dtype=jnp.float32) * 0.02, 'bq': jax.random.normal(ks[4], (D,), dtype=jnp.float32) * 0.02, 'Wk': jax.random.normal(ks[5], (D, D), dtype=jnp.float32) * 0.02, 'bk': jax.random.normal(ks[6], (D,), dtype=jnp.float32) * 0.02, 'Wv': jax.random.normal(ks[7], (D, D), dtype=jnp.float32) * 0.02, 'bv': jax.random.normal(ks[8], (D,), dtype=jnp.float32) * 0.02, 'head_num': HEADS}
        return inp
    _L1_xattn_all = _L1_xattn_setup()
    _L1_xattn_in = {k: v for k, v in _L1_xattn_all.items() if k in ('Wq', 'bq', 'Wk', 'bk', 'Wv', 'bv')}
    del _L1_xattn_all

    def _L1_ffn_setup():
        import math
        import jax, jax.numpy as jnp
        import numpy as np
        SCALING = 16.0 / 32.0

        def real_fourier_orthogonal_multiply(c):
            n = c.shape[-1]
            sqrt_n = math.sqrt(n)
            pair_scale = math.sqrt(n / 2.0)
            max_f = (n - 1) // 2
            work = c.astype(jnp.float32)
            dc = (work[..., 0] * sqrt_n)[..., None].astype(jnp.complex64)
            cos = work[..., 1:1 + 2 * max_f:2] * pair_scale
            sin = work[..., 2:2 + 2 * max_f:2] * pair_scale
            mid = (cos - 1j * sin).astype(jnp.complex64)
            parts = [dc, mid]
            if n % 2 == 0:
                parts.append((work[..., -1] * sqrt_n)[..., None].astype(jnp.complex64))
            spectrum = jnp.concatenate(parts, axis=-1)
            return jnp.fft.irfft(spectrum, n=n, axis=-1).astype(c.dtype)
        key = jax.random.key(seed)
        ks = jax.random.split(key, 9)
        B, S, D_in, D_out, R0, R1, E = (4, 256, 512, 512, 32, 8, 3)
        x = jax.random.normal(ks[0], (B, S, D_in), dtype=jnp.float32)
        W_base = jax.random.normal(ks[1], (D_out, D_in), dtype=jnp.float32) * 0.02
        b_base = jax.random.normal(ks[2], (D_out,), dtype=jnp.float32) * 0.02
        enc0 = jax.random.normal(ks[3], (R0, D_in), dtype=jnp.float32) * 0.02
        enc1 = jax.random.normal(ks[4], (R1, D_in), dtype=jnp.float32) * 0.02
        coefs0 = jax.random.normal(ks[5], (E, D_out, R0), dtype=jnp.float32) * 0.02
        coefs1 = jax.random.normal(ks[6], (E, D_out, R1), dtype=jnp.float32) * 0.02
        mask0 = jax.random.randint(ks[7], (E, D_out, R0), 0, 2).astype(bool)
        mask1 = jax.random.randint(ks[8], (E, D_out, R1), 0, 2).astype(bool)
        return dict(x=x, W_base=W_base, b_base=b_base, enc0=enc0, enc1=enc1, coefs0=coefs0, coefs1=coefs1, mask0=mask0, mask1=mask1)
    _L1_ffn_all = _L1_ffn_setup()
    _L1_ffn_in = {k: v for k, v in _L1_ffn_all.items() if k in ('W_base', 'b_base', 'enc0', 'enc1', 'coefs0', 'coefs1', 'mask0', 'mask1')}
    del _L1_ffn_all
    return {'x': x, 'ctx_4096': ctx_4096, 'L0_xattn_Wq': _L0_xattn_in['Wq'], 'L0_xattn_Wk': _L0_xattn_in['Wk'], 'L0_xattn_Wv': _L0_xattn_in['Wv'], 'L0_xattn_Wo': _L0_xattn_in['Wo'], 'L0_ffn_weight': _L0_ffn_in['weight'], 'L0_ffn_bias': _L0_ffn_in['bias'], 'L0_ffn_lora_A': _L0_ffn_in['lora_A'], 'L0_ffn_lora_B': _L0_ffn_in['lora_B'], 'L0_ffn_lora_start_indices': _L0_ffn_in['lora_start_indices'], 'L1_xattn_Wq': _L1_xattn_in['Wq'], 'L1_xattn_bq': _L1_xattn_in['bq'], 'L1_xattn_Wk': _L1_xattn_in['Wk'], 'L1_xattn_bk': _L1_xattn_in['bk'], 'L1_xattn_Wv': _L1_xattn_in['Wv'], 'L1_xattn_bv': _L1_xattn_in['bv'], 'L1_ffn_W_base': _L1_ffn_in['W_base'], 'L1_ffn_b_base': _L1_ffn_in['b_base'], 'L1_ffn_enc0': _L1_ffn_in['enc0'], 'L1_ffn_enc1': _L1_ffn_in['enc1'], 'L1_ffn_coefs0': _L1_ffn_in['coefs0'], 'L1_ffn_coefs1': _L1_ffn_in['coefs1'], 'L1_ffn_mask0': _L1_ffn_in['mask0'], 'L1_ffn_mask1': _L1_ffn_in['mask1']}

def reference(x, ctx_4096, L0_xattn_Wq, L0_xattn_Wk, L0_xattn_Wv, L0_xattn_Wo, L0_ffn_weight, L0_ffn_bias, L0_ffn_lora_A, L0_ffn_lora_B, L0_ffn_lora_start_indices, L1_xattn_Wq, L1_xattn_bq, L1_xattn_Wk, L1_xattn_bk, L1_xattn_Wv, L1_xattn_bv, L1_ffn_W_base, L1_ffn_b_base, L1_ffn_enc0, L1_ffn_enc1, L1_ffn_coefs0, L1_ffn_coefs1, L1_ffn_mask0, L1_ffn_mask1):
    import jax
    import jax.numpy as jnp

    def _L0_xattn_ref(query, key, value, Wq, Wk, Wv, Wo):
        import jax, jax.numpy as jnp
        import numpy as np
        DIM = 512
        NUM_HEADS = 32
        NUM_KV_HEADS = 8
        HEAD_DIM = DIM // NUM_HEADS
        KV_DIM = DIM // (NUM_HEADS // NUM_KV_HEADS)
        B, S = (1, 256)
        b, sq, _ = query.shape
        _, sk, _ = key.shape
        rep = NUM_HEADS // NUM_KV_HEADS
        q = (query @ Wq).reshape(b, sq, NUM_HEADS, HEAD_DIM).transpose(0, 2, 1, 3)
        k = (key @ Wk).reshape(b, sk, NUM_KV_HEADS, HEAD_DIM).transpose(0, 2, 1, 3)
        v = (value @ Wv).reshape(b, sk, NUM_KV_HEADS, HEAD_DIM).transpose(0, 2, 1, 3)
        k = jnp.repeat(k, rep, axis=1)
        v = jnp.repeat(v, rep, axis=1)
        scale = HEAD_DIM ** (-0.5)
        scores = jnp.einsum('bhqd,bhkd->bhqk', q, k) * scale
        probs = jax.nn.softmax(scores, axis=-1)
        out = jnp.einsum('bhqk,bhkd->bhqd', probs, v)
        out = out.transpose(0, 2, 1, 3).reshape(b, sq, DIM)
        return out @ Wo

    def _L0_ffn_ref(x, weight, bias, lora_A, lora_B, lora_start_indices):
        import jax, jax.numpy as jnp
        import numpy as np
        LORA_RANK = 16
        LORA_ALPHA = 16
        LORA_SCALE = LORA_ALPHA / LORA_RANK
        y = jnp.einsum('bsd,od->bso', x, weight) + bias
        B = x.shape[0]
        seg = jnp.searchsorted(lora_start_indices, jnp.arange(B), side='right') - 1
        adapter_idx = jnp.clip(seg - 1, 0, lora_A.shape[0] - 1)
        A = lora_A[adapter_idx]
        Bw = lora_B[adapter_idx]
        lo = jnp.einsum('bsr,bor->bso', jnp.einsum('bsd,brd->bsr', x, A), Bw) * LORA_SCALE
        use_lora = (seg > 0)[:, None, None]
        return y + jnp.where(use_lora, lo, jnp.zeros((), dtype=y.dtype))

    def _L1_xattn_ref(q, v, k, Wq, bq, Wk, bk, Wv, bv, head_num):
        import jax, jax.numpy as jnp
        import numpy as np
        B, S, D = (2, 197, 512)
        HEADS = 16
        b, s, _ = q.shape
        hide = Wq.shape[0]
        hd = hide // head_num

        def proj(x, W, bias):
            y = x @ W.T + bias
            return y.reshape(b, s, head_num, hd).transpose(0, 2, 1, 3).reshape(b * head_num, s, hd)
        Q = proj(q, Wq, bq)
        K = proj(k, Wk, bk)
        V = proj(v, Wv, bv)
        scores = jnp.einsum('bqd,bkd->bqk', Q, K) / jnp.sqrt(jnp.asarray(hd, jnp.float32))
        attn = jax.nn.softmax(scores, axis=0)
        res = jnp.einsum('bqk,bkd->bqd', attn, V)
        out = res.reshape(b, head_num, s, hd).transpose(0, 2, 3, 1).reshape(b, s, hd * head_num)
        return out

    def _L1_ffn_ref(x, W_base, b_base, enc0, enc1, coefs0, coefs1, mask0, mask1):
        import math
        import jax, jax.numpy as jnp
        import numpy as np
        SCALING = 16.0 / 32.0

        def real_fourier_orthogonal_multiply(c):
            n = c.shape[-1]
            sqrt_n = math.sqrt(n)
            pair_scale = math.sqrt(n / 2.0)
            max_f = (n - 1) // 2
            work = c.astype(jnp.float32)
            dc = (work[..., 0] * sqrt_n)[..., None].astype(jnp.complex64)
            cos = work[..., 1:1 + 2 * max_f:2] * pair_scale
            sin = work[..., 2:2 + 2 * max_f:2] * pair_scale
            mid = (cos - 1j * sin).astype(jnp.complex64)
            parts = [dc, mid]
            if n % 2 == 0:
                parts.append((work[..., -1] * sqrt_n)[..., None].astype(jnp.complex64))
            spectrum = jnp.concatenate(parts, axis=-1)
            return jnp.fft.irfft(spectrum, n=n, axis=-1).astype(c.dtype)
        base = jnp.einsum('bsd,od->bso', x, W_base) + b_base
        e0 = jnp.einsum('bsd,rd->bsr', x, enc0)
        e1 = jnp.einsum('bsd,rd->bsr', x, enc1)
        w0 = coefs0 * mask0.astype(coefs0.dtype)
        w1 = coefs1 * mask1.astype(coefs1.dtype)
        decoded = jnp.einsum('bsr,eor->ebso', e0, w0) + jnp.einsum('bsr,eor->ebso', e1, w1)
        transformed = real_fourier_orthogonal_multiply(decoded)
        update = transformed.sum(axis=0)
        return base + update * SCALING
    x = x + _L0_xattn_ref(_layernorm(x, axis=-1), ctx_4096, ctx_4096, L0_xattn_Wq, L0_xattn_Wk, L0_xattn_Wv, L0_xattn_Wo)
    x = x + _L0_ffn_ref(_layernorm(x, axis=-1), L0_ffn_weight, L0_ffn_bias, L0_ffn_lora_A, L0_ffn_lora_B, L0_ffn_lora_start_indices)
    x = x + _L1_xattn_ref(_layernorm(x, axis=-1), ctx_4096, ctx_4096, L1_xattn_Wq, L1_xattn_bq, L1_xattn_Wk, L1_xattn_bk, L1_xattn_Wv, L1_xattn_bv, 16)
    x = x + _L1_ffn_ref(_layernorm(x, axis=-1), L1_ffn_W_base, L1_ffn_b_base, L1_ffn_enc0, L1_ffn_enc1, L1_ffn_coefs0, L1_ffn_coefs1, L1_ffn_mask0, L1_ffn_mask1)
    return x

_drawn_inputs = setup_inputs


def setup_inputs(seed=0):
    import zlib

    import numpy as np

    out = dict(_drawn_inputs(seed))
    spreads = {}
    factors = {'L0_ffn_bias': 8.0,
     'L1_xattn_Wq': 3.465,
     'L1_xattn_bq': 8.0,
     'L1_xattn_Wk': 3.514,
     'L1_xattn_bk': 8.0,
     'L1_xattn_bv': 5.56,
     'L1_ffn_b_base': 5.55,
     'L1_ffn_enc0': 3.49,
     'L1_ffn_enc1': 7.06,
     'L1_ffn_coefs0': 3.52,
     'L1_ffn_coefs1': 7.108}
    for name, (base, spread) in spreads.items():
        noise = np.random.default_rng([zlib.crc32(name.encode()), seed]).standard_normal(out[name].shape)
        drawn = base * np.exp(spread * noise) if base else spread * noise
        out[name] = jnp.asarray(drawn.astype(out[name].dtype))
    for name, factor in factors.items():
        out[name] = (out[name] * factor).astype(out[name].dtype)
    return out
```

```python
from contextlib import ExitStack

import concourse.bass as bass
from concourse import mybir

F32 = mybir.dt.float32
F32R = mybir.dt.float32r
U8 = mybir.dt.uint8
I32 = mybir.dt.int32
ALU = mybir.AluOpType
ACT = mybir.ActivationFunctionType
AX_X = mybir.AxisListType.X

B, S, D = 8, 128, 512
P = 128
C = D // P
PAIRS = B // 2
KVH, REP, HD0 = 8, 4, 16
H1, HD1 = 16, 32
JH = P // HD1
GROUPS = PAIRS * C
T = 2 * JH
RANK = 48
TOP = 64
ENC = 40
EXP = 3
EPS = 1e-5
SCALE0 = HD0 ** -0.5
SCALE1 = HD1 ** -0.5
NG = 4
NSTG = 4

CHUNKS = ([("wkv", 0), ("wkv", 1)] + [("wq0", c) for c in range(C)] + [("wo", c) for c in range(C)]
          + [("la", 0), ("lb", 0)] + [("w0", c) for c in range(C)]
          + [("wk1", c) for c in range(C)] + [("wq1", c) for c in range(C)]
          + [("wv1", c) for c in range(C)] + [("dft", c) for c in range(C)]
          + [("wbase", c) for c in range(C)])
CHUNK = {key: n for n, key in enumerate(CHUNKS)}
BY_POOL = ("wk1", "wq1", "wv1")


def plan():
    order = []

    def weights(name):
        return [("W", name, c) for n, c in CHUNKS if n == name]

    def prepare(p):
        out = []
        for b in (2 * p, 2 * p + 1):
            out += [("LNs", 0, b), ("CT", 0, b), ("LNn", 0, b)]
        out += [("K0", p), ("KM", 2 * p), ("V0", 2 * p), ("XT", 0, 2 * p), ("V0", 2 * p + 1), ("KM", 2 * p + 1),
                ("XT", 0, 2 * p + 1), ("Q0", p, 0), ("Q0", p, 1)]
        return out

    def output(b):
        return [("OB", b, 0), ("OB", b, 1), ("OX", b), ("WO", b), ("LNs", 1, b), ("LNn", 1, b)]

    def feed(p):
        return [("XT", 1, 2 * p), ("XT", 1, 2 * p + 1), ("LT", p), ("F0", 2 * p), ("F0", 2 * p + 1)]

    def weave(front, back):
        out, done = [], 0
        for n, step in enumerate(front):
            out.append(step)
            upto = (n + 1) * len(back) // len(front)
            out += back[done:upto]
            done = upto
        return out

    order += weights("wkv") + prepare(0)[:-2] + weights("wq0") + prepare(0)[-2:]
    order += [("MX", 0, r) for r in range(REP)] + [("MT", 0)] + weights("wo")
    order += weights("la") + weights("lb") + weights("w0")
    for b in range(B):
        front = []
        for i in range(4):
            front.append(("ST", b, i))
            if b + 1 < B:
                front.append(("MX", b + 1, i))
            if i == 2:
                front.append(("PV", b, 0))
        if b + 1 < B:
            front.append(("MT", b + 1))
        front.append(("PV", b, 1))
        back = output(b - 1) if b else []
        p = b // 2
        if b % 2 == 0 and p + 1 < PAIRS:
            back = back + prepare(p + 1)
        if b % 2 == 1 and p:
            back = back[:2] + feed(p - 1) + back[2:]
        if b == B - 2:
            back = back + weights("wk1")
        order += weave(front, back)
    order += output(B - 1) + weights("wq1") + feed(PAIRS - 1) + weights("wv1")

    def prepare1(p):
        out = []
        for b in (2 * p, 2 * p + 1):
            out += [("LNs", 2, b), ("CT", 1, b), ("LNn", 2, b)]
        return out + [("XT", 2, 2 * p), ("XT", 2, 2 * p + 1)]

    order += [("PH2",)]
    for g in range(GROUPS):
        if g % C == 0:
            order += prepare1(g // C)
        order += [("K1", g)]
        if g:
            order += [("SM", g - 1)]
        order += [("Q1", g), ("S1", g)]
        if g == C:
            order += [("WC",), ("WM",)]
    order += [("SM", GROUPS - 1)]
    order += [("CT", 2, 0), ("V1", 0), ("CT", 2, 1)]
    order += [("FA",)]
    order += [("WE", c) for c in range(C)]
    for b in range(B):
        if b % 2 == 0:
            order += [("NM", b // 2 * C + c) for c in range(C)]
        order += [("PV1", b)]
        if b + 1 < B:
            order += [("V1", b + 1)]
        if b:
            order += [("XT", 3, b - 1)]
        order += [("OX1", b), ("LNs", 3, b)]
        if b + 2 < B:
            order += [("CT", 2, b + 2)]
        if b:
            order += [("F1", b - 1)]
        order += [("LNn", 3, b)]
    order += [("XT", 3, B - 1), ("F1", B - 1)]
    return order


ORDER = plan()
BANK_STEPS = ("CT", "K0", "V0", "XT", "Q0", "MT", "PV", "OB", "OX", "WO", "LT", "F0", "K1", "Q1", "V1",
              "PV1", "OX1", "F1", "WM", "WE")
SPLIT_STEPS = ("CT", "K0", "XT", "Q0", "OX", "LT", "K1", "Q1")


def numbered(kinds):
    return {step: n for n, step in enumerate(s for s in ORDER if s[0] in kinds)}


BANK = numbered(BANK_STEPS)
WIDE = numbered(("MX", "ST", "S1"))
SPLIT = numbered(SPLIT_STEPS)
NORM = numbered(("LNs",))
XN_SLOT = {s: s[1] % 2 * 2 + s[2] % 2 for s in NORM}


def earlier_norm(step):
    same = [s for s in NORM if XN_SLOT[s] == XN_SLOT[step] and NORM[s] < NORM[step]]
    return same[-1] if same else None


CTX = numbered(("CT",))


def build(nc, x, ctx, wkv, wq0, wo, la, lb, w0, starts, wk1, wq1, wv1, biases, bv1, wbase, bbase, enc,
          coefs, masks, dft, eye, table, out):
    with ExitStack() as always:
        def sb(name, shape, dt=F32, where=always):
            return where.enter_context(nc.sbuf_tensor(name, [P] + list(shape), dt))

        def sem(name):
            return always.enter_context(nc.semaphore(name))

        X = sb("X", [B, D])
        slot_h = [sb(f"slot{k}_h", [C, D], F32R) for k in range(3)]
        slot_l = [sb(f"slot{k}_l", [C, D], F32R) for k in range(3)]
        stg = sb("stg", [NSTG, D])
        ident = sb("ident", [P])
        ident_r = sb("ident_r", [P], F32R)
        ctx_in = sb("ctx_in", [2, D])
        ctxT_h, ctxT_l = sb("ctxT_h", [C, 2, P], F32R), sb("ctxT_l", [C, 2, P], F32R)
        xT_h, xT_l = sb("xT_h", [C, 2, P], F32R), sb("xT_l", [C, 2, P], F32R)
        xn = sb("xn", [4, D])
        stats = sb("stats", [4, 6])
        moments = sb("moments", [4, 2])
        var_eps = sb("var_eps", [4, 1])
        rstd = sb("rstd", [4, 1])
        minus_half = sb("minus_half", [1])
        bias_qk = sb("bias_qk", [2, C])
        tab = sb("tab", [KVH + B + 2])
        with ExitStack() as first:
            def s1(name, shape, dt=F32):
                return sb(name, shape, dt, first)
            wkv_h, wkv_l = s1("wkv_h", [C, 256], F32R), s1("wkv_l", [C, 256], F32R)
            la_h, la_l = s1("la_h", [C, P], F32R), s1("la_l", [C, P], F32R)
            lb_h, lb_l = s1("lb_h", [D], F32R), s1("lb_l", [D], F32R)
            K_h, K_l = s1("K_h", [2, 2, P], F32R), s1("K_l", [2, 2, P], F32R)
            KM_h, KM_l = s1("KM_h", [2, KVH, P], F32R), s1("KM_l", [2, KVH, P], F32R)
            V0 = s1("V0", [4, KVH, 32])
            Q_h, Q_l = s1("Q_h", [2, 2, REP, P], F32R), s1("Q_l", [2, 2, REP, P], F32R)
            mx = s1("mx", [2, REP, KVH])
            negmax = s1("negmax", [2, D], F32R)
            select = s1("select", [KVH, P], F32R)
            PT = s1("PT", [4, 2 * D])
            OTs = s1("OTs", [2, D])
            rec = s1("rec", [2, REP, 4])
            O = s1("O", [2, D])
            OT_h, OT_l = s1("OT_h", [2, C, P], F32R), s1("OT_l", [2, C, P], F32R)
            fT_h, fT_l = s1("fT_h", [C, 2, P], F32R), s1("fT_l", [C, 2, P], F32R)
            lora_t = s1("lora_t", [2, P], F32R)
            starts_i = s1("starts_i", [4], I32)
            starts_f = s1("starts_f", [4])
            started = s1("started", [B, 4])
            n_started = s1("n_started", [B])
            use_lora = s1("use_lora", [B])
        with ExitStack() as second:
            def s2(name, shape, dt=F32):
                return sb(name, shape, dt, second)
            P1 = s2("P1", [GROUPS, T, P])
            K1_h, K1_l = s2("K1_h", [2, 2, P], F32R), s2("K1_l", [2, 2, P], F32R)
            Q1_h, Q1_l = s2("Q1_h", [2, 2, JH, P], F32R), s2("Q1_l", [2, 2, JH, P], F32R)
            mneg = s2("mneg", [GROUPS, P], F32R)
            Z = s2("Z", [GROUPS, P])
            enc_sb = s2("enc_sb", [D])
            mt = s2("mt", [D])
            bias_out = s2("bias_out", [D])
            nmin = s2("nmin", [P])
        with ExitStack() as early:
            sb("under_early", [(GROUPS - 1) * T * P], F32, early)
            cf = sb("cf", [C, EXP, ENC], F32, early)
            mk = sb("mk", [C * EXP * ENC // 4], I32, early)
            cs = sb("cs", [C, ENC], F32, early)
        with ExitStack() as third:
            sb("under_third", [GROUPS * T * P], F32, third)
            fac = sb("fac", [GROUPS, P], F32, third)
            V1 = sb("V1", [2, D], F32, third)
            O1T = sb("O1T", [D], F32, third)
            XB = sb("XB", [2, D], F32, third)
            bias_v = sb("bias_v", [D], F32, third)
        ps = always.enter_context(nc.psum_tensor("ps", [P, 8, D], F32))

        x_loaded = [sem(f"x_loaded{b}") for b in range(B)]
        ctx_loaded = [sem(f"ctx_loaded{k}") for k in range(2)]
        stg_loaded = [sem(f"stg_loaded{k}") for k in range(NSTG)]
        small_loaded = sem("small_loaded")
        late_loaded = sem("late_loaded")
        out_stored = [sem(f"out_stored{k}") for k in range(2)]
        bias_v_loaded = sem("bias_v_loaded")
        bank_full = sem("bank_full")
        bank_free = [sem(f"bank_free{k}") for k in range(NG)]
        wide_full = sem("wide_full")
        wide_free = [sem(f"wide_free{k}") for k in range(2)]
        split_hi = sem("split_hi")
        w_hi = sem("w_hi")
        w_lo = sem("w_lo")
        w_lo_pool = sem("w_lo_pool")
        w_sum = sem("w_sum")
        km_ready = sem("km_ready")
        consts_pool = sem("consts_pool")
        consts_dve = sem("consts_dve")
        lora_ready = sem("lora_ready")
        stat_done, moments_ready = sem("stat_done"), sem("moments_ready")
        eps_done, rstd_ready = sem("eps_done"), sem("rstd_ready")
        xn_ready = sem("xn_ready")
        rec_ready = sem("rec_ready")
        cs_step = sem("cs_step")
        m1_ready = sem("m1_ready")
        shifted = sem("shifted")
        z_ready = sem("z_ready")
        zero_q1 = sem("zero_q1")
        fac_dve, fac_act = sem("fac_dve"), sem("fac_act")
        nm_dve, nm_pool = sem("nm_dve"), sem("nm_pool")
        xb_ready = sem("xb_ready")

        def filled(eng, step):
            eng.wait_ge(bank_full, BANK[step] + 1)

        def consumed(eng, step):
            n = BANK[step]
            eng.wait_ge(bank_free[n % NG], n // NG + 1)

        def bank(step):
            return ps[:, BANK[step] % NG, :]

        def free(step):
            return bank_free[BANK[step] % NG]

        def take_bank(eng, step):
            n = BANK[step]
            if n >= NG:
                eng.wait_ge(bank_free[n % NG], n // NG)
            return bank(step)

        def wide(step):
            k = NG + 2 * (WIDE[step] % 2)
            return ps[:, k:k + 2, :]

        def wide_filled(eng, step):
            eng.wait_ge(wide_full, WIDE[step] + 1)

        def wide_consumed(eng, step):
            n = WIDE[step]
            eng.wait_ge(wide_free[n % 2], n // 2 + 1)

        def take_wide(eng, step):
            n = WIDE[step]
            if n >= 2:
                eng.wait_ge(wide_free[n % 2], n // 2)
            return wide(step)

        def hi_written(eng, step):
            eng.wait_ge(split_hi, SPLIT[step] + 1)

        def weight_ready(eng, name):
            mine = [k for k, (n, _) in enumerate(CHUNKS) if n == name]
            if name in BY_POOL:
                eng.wait_ge(w_lo_pool, sum(n in BY_POOL for n, _ in CHUNKS[:mine[-1] + 1]))
            else:
                eng.wait_ge(w_lo, sum(n not in BY_POOL + ("dft",) for n, _ in CHUNKS[:mine[-1] + 1]))

        def hi_count(key):
            return sum(n != "dft" for n, _ in CHUNKS[:CHUNK[key] + 1])

        def stage_loaded(eng, key):
            n = CHUNK[key]
            eng.wait_ge(stg_loaded[n % NSTG], 16 * (n // NSTG + 1))

        def stage(key):
            return stg[:, CHUNK[key] % NSTG, :]

        def parts(key):
            name, c = key
            src = stage(key)
            if name == "wkv":
                return (wkv_h[:, 2 * c:2 * c + 2, :], wkv_l[:, 2 * c:2 * c + 2, :],
                        src.rearrange("p (c n) -> p c n", c=2))
            if name == "la":
                return la_h[:, :, :], la_l[:, :, :], src.rearrange("p (c n) -> p c n", c=C)
            if name == "lb":
                return lb_h[:, :], lb_l[0:TOP, :], src
            k = {"wq0": 0, "wk1": 0, "wo": 1, "wq1": 1, "wbase": 1, "w0": 2, "wv1": 2}[name]
            return slot_h[k][:, c, :], slot_l[k][:, c, :], src

        last_reader = {"wk1": ("Q0", PAIRS - 1, 1), "wq1": ("WO", B - 1), "wv1": ("F0", B - 1),
                       "wbase": ("Q1", GROUPS - 1)}

        def passes(eng, dst, left, right, start=True, stop=True):
            eng.matmul(dst, left[0], right[0], start=start, stop=False)
            eng.matmul(dst, left[0], right[1], start=False, stop=False)
            return eng.matmul(dst, left[1], right[0], start=False, stop=stop)

        def project(eng, dst, left, right):
            for c in range(C):
                last = passes(eng, dst, left(c), right(c), start=(c == 0), stop=(c == C - 1))
            return last

        block = always.enter_context(nc.Block())

        @block.sync
        def _(sp):
            def load_ctx(n):
                step = [s for s in CTX if CTX[s] == n][0]
                if n >= 2:
                    filled(sp, [s for s in CTX if CTX[s] == n - 2][0])
                sp.dma_start(ctx_in[:, n % 2, :], ctx[step[2]]).then_inc(ctx_loaded[n % 2], 16)

            def load_chunk(n):
                name, c = CHUNKS[n]
                if n >= NSTG:
                    old = CHUNKS[n - NSTG]
                    if old[0] == "dft":
                        filled(sp, ("WM",))
                    elif old[0] in BY_POOL:
                        sp.wait_ge(w_lo_pool, sum(k in BY_POOL for k, _ in CHUNKS[:n - NSTG + 1]))
                    else:
                        sp.wait_ge(w_lo, sum(k not in BY_POOL + ("dft",) for k, _ in CHUNKS[:n - NSTG + 1]))
                dst = stg[:, n % NSTG, :]
                w = {"wkv": wkv, "wq0": wq0, "wo": wo, "la": la, "lb": lb, "w0": w0, "wk1": wk1, "wq1": wq1,
                     "wv1": wv1, "dft": dft, "wbase": wbase}[name]
                if name == "wkv":
                    src = w.rearrange("(c p) n -> p c n", p=P)[:, 2 * c:2 * c + 2, :]
                    dst = dst.rearrange("p (c n) -> p c n", c=2)
                elif name == "la":
                    src = w.rearrange("(c p) n -> p c n", p=P)
                    dst = dst.rearrange("p (c n) -> p c n", c=C)
                elif name == "lb":
                    src = w
                else:
                    src = w[c * P:(c + 1) * P, :]
                sp.dma_start(dst, src).then_inc(stg_loaded[n % NSTG], 16)

            def load_x(b):
                sp.dma_start(X[:, b, :], x[b]).then_inc(x_loaded[b], 16)

            sp.dma_start(ident[:, :], eye).then_inc(small_loaded, 16)
            load_ctx(0)
            load_chunk(0)
            load_chunk(1)
            load_ctx(1)
            load_x(0)
            load_x(1)
            sp.dma_start(tab[:, :], table).then_inc(small_loaded, 16)
            load_chunk(2)
            load_chunk(3)
            sp.dma_start(starts_i[:, :], starts.partition_broadcast(P)).then_inc(small_loaded, 16)
            sp.dma_start(bias_qk[:, :, :], biases).then_inc(small_loaded, 16)
            for b in range(2, B):
                load_x(b)
            done_chunks, done_ctx, n_w = 4, 2, 0
            for step in ORDER:
                if step[0] == "CT" and done_ctx < len(CTX):
                    load_ctx(done_ctx)
                    done_ctx += 1
                elif step[0] == "W" or step[0] == "WE":
                    n_w += 1
                    while done_chunks < min(n_w + NSTG, len(CHUNKS)) and CHUNKS[done_chunks][0] != "dft":
                        load_chunk(done_chunks)
                        done_chunks += 1
                elif step[0] == "WC":
                    for _ in range(C):
                        load_chunk(done_chunks)
                        done_chunks += 1
                elif step[0] == "PH2":
                    consumed(sp, ("F0", B - 1))
                    sp.dma_start(cf[:, :, :, :], coefs).then_inc(late_loaded, 16)
                    sp.dma_start(mk[:, :], masks).then_inc(late_loaded, 16)
                    sp.dma_start(enc_sb[0:ENC, :], enc).then_inc(late_loaded, 16)
                    sp.dma_start(bias_out[:, :], bbase.partition_broadcast(P)).then_inc(late_loaded, 16)
                elif step[0] == "WM":
                    n_w += C
                    while done_chunks < len(CHUNKS):
                        load_chunk(done_chunks)
                        done_chunks += 1
                elif step[0] == "F1":
                    b = step[1]
                    consumed(sp, step)
                    sp.dma_start(out[b], XB[:, b % 2, :]).then_inc(out_stored[b % 2], 16)
                elif step[0] == "V1" and step[1] == 0:
                    filled(sp, step)
                    sp.dma_start(bias_v[:, :], bv1.partition_broadcast(P)).then_inc(bias_v_loaded, 16)
            for k in range(2):
                sp.wait_ge(out_stored[k], 16 * (B // 2))

        @block.tensor
        def _(pe):
            pe.wait_ge(small_loaded, 16 * 4)
            pe.wait_ge(consts_dve, 2)
            pe.wait_ge(consts_pool, 4)
            for step in ORDER:
                kind = step[0]
                if kind == "CT":
                    n = CTX[step]
                    dst = take_bank(pe, step)
                    pe.wait_ge(ctx_loaded[n % 2], 16 * (n // 2 + 1))
                    for c in range(C):
                        last = pe.transpose(dst[:, c * P:(c + 1) * P], ctx_in[:, n % 2, c * P:(c + 1) * P],
                                            ident[:, :])
                    last.then_inc(bank_full, 1)
                elif kind == "XT":
                    layer, b = step[1:]
                    n, k = NORM[("LNs", layer, b)], XN_SLOT[("LNs", layer, b)]
                    dst = take_bank(pe, step)
                    pe.wait_ge(xn_ready, n + 1)
                    for c in range(C):
                        last = pe.transpose(dst[:, c * P:(c + 1) * P], xn[:, k, c * P:(c + 1) * P],
                                            ident[:, :])
                    last.then_inc(bank_full, 1)
                elif kind == "K0":
                    p = step[1]
                    dst = take_bank(pe, step)
                    weight_ready(pe, "wkv")
                    consumed(pe, ("CT", 0, 2 * p))
                    consumed(pe, ("CT", 0, 2 * p + 1))
                    last = project(pe, dst[:, 0:2 * P],
                                   lambda c: (wkv_h[:, c, 0:P], wkv_l[:, c, 0:P]),
                                   lambda c: (ctxT_h[:, c, :, :].rearrange("p b t -> p (b t)"),
                                              ctxT_l[:, c, :, :].rearrange("p b t -> p (b t)")))
                    last.then_inc(bank_full, 1)
                elif kind == "V0":
                    b = step[1]
                    dst = take_bank(pe, step)
                    last = project(pe, dst[:, 0:2 * P],
                                   lambda c: (ctxT_h[:, c, b % 2, :], ctxT_l[:, c, b % 2, :]),
                                   lambda c: (wkv_h[:, c, :], wkv_l[:, c, :]))
                    last.then_inc(bank_full, 1)
                elif kind == "Q0":
                    p, half = step[1:]
                    dst = take_bank(pe, step)
                    weight_ready(pe, "wq0")
                    consumed(pe, ("XT", 0, 2 * p))
                    consumed(pe, ("XT", 0, 2 * p + 1))
                    for k in range(2):
                        r = 2 * half + k
                        last = project(pe, dst[:, k * 2 * P:(k + 1) * 2 * P],
                                       lambda c: (slot_h[0][:, c, r * P:(r + 1) * P],
                                                  slot_l[0][:, c, r * P:(r + 1) * P]),
                                       lambda c: (xT_h[:, c, :, :].rearrange("p b t -> p (b t)"),
                                                  xT_l[:, c, :, :].rearrange("p b t -> p (b t)")))
                    last.then_inc(bank_full, 1)
                elif kind == "MX":
                    b, r = step[1:]
                    p = b // 2
                    dst = take_wide(pe, step)
                    consumed(pe, ("Q0", p, r // 2))
                    pe.wait_ge(km_ready, 2 * b + 2)
                    for k in range(2):
                        last = pe.matmul(dst[:, k, :], Q_h[:, p % 2, b % 2, r, :],
                                         KM_h[:, b % 2, 4 * k:4 * k + 4, :].rearrange("p g k -> p (g k)"),
                                         start=True, stop=True)
                    last.then_inc(wide_full, 1)
                elif kind == "MT":
                    b = step[1]
                    dst = take_bank(pe, step)
                    wide_consumed(pe, ("MX", b, REP - 1))
                    wide_consumed(pe, ("MX", b, REP - 2))
                    for r in range(REP):
                        last = pe.transpose(dst[0:KVH, r * P:(r + 1) * P], mx[:, b % 2, r, :], ident[:, :])
                    last.then_inc(bank_full, 1)
                elif kind == "ST":
                    b, g2 = step[1:]
                    p = b // 2
                    dst = take_wide(pe, step)
                    consumed(pe, ("MT", b))
                    consumed(pe, ("Q0", p, 0))
                    consumed(pe, ("Q0", p, 1))
                    q = [t[:, p % 2, b % 2, :, :].rearrange("p r q -> p (r q)") for t in (Q_h, Q_l)]
                    for k in range(2):
                        g = 2 * g2 + k
                        passes(pe, dst[:, k, :], (KM_h[:, b % 2, g, :], KM_l[:, b % 2, g, :]), q, stop=False)
                        last = pe.matmul(dst[:, k, :], select[:, g, :], negmax[:, b % 2, :],
                                         start=False, stop=True)
                    last.then_inc(wide_full, 1)
                elif kind == "PV":
                    b, gq = step[1:]
                    dst = take_bank(pe, step)
                    consumed(pe, ("V0", b))
                    wide_consumed(pe, ("ST", b, 2 * gq))
                    wide_consumed(pe, ("ST", b, 2 * gq + 1))
                    for j in range(4):
                        n = 4 * b + 2 * gq + j // 2
                        last = pe.matmul(dst[32 * j:32 * j + 32, :], V0[:, b % 4, 4 * gq + j, :],
                                         PT[:, n % 4, (j % 2) * D:(j % 2 + 1) * D], start=True, stop=True)
                    last.then_inc(bank_full, 1)
                elif kind == "OB":
                    b, gq = step[1:]
                    dst = take_bank(pe, step)
                    consumed(pe, ("PV", b, gq))
                    for r in range(REP):
                        last = pe.transpose(dst[:, r * P:(r + 1) * P], OTs[:, gq, r * P:(r + 1) * P],
                                            ident[:, :])
                    last.then_inc(bank_full, 1)
                elif kind == "OX":
                    b = step[1]
                    dst = take_bank(pe, step)
                    consumed(pe, ("OB", b, 0))
                    consumed(pe, ("OB", b, 1))
                    for c in range(C):
                        last = pe.transpose(dst[:, c * P:(c + 1) * P], O[:, b % 2, c * P:(c + 1) * P],
                                            ident[:, :])
                    last.then_inc(bank_full, 1)
                elif kind == "WO":
                    b = step[1]
                    dst = take_bank(pe, step)
                    weight_ready(pe, "wo")
                    consumed(pe, ("OX", b))
                    last = project(pe, dst, lambda c: (OT_h[:, b % 2, c, :], OT_l[:, b % 2, c, :]),
                                   lambda c: (slot_h[1][:, c, :], slot_l[1][:, c, :]))
                    last.then_inc(bank_full, 1)
                elif kind == "LT":
                    p = step[1]
                    dst = take_bank(pe, step)
                    weight_ready(pe, "la")
                    consumed(pe, ("XT", 1, 2 * p))
                    consumed(pe, ("XT", 1, 2 * p + 1))
                    last = project(pe, dst[:, 0:2 * P], lambda c: (la_h[:, c, :], la_l[:, c, :]),
                                   lambda c: (fT_h[:, c, :, :].rearrange("p b t -> p (b t)"),
                                              fT_l[:, c, :, :].rearrange("p b t -> p (b t)")))
                    last.then_inc(bank_full, 1)
                elif kind == "F0":
                    b = step[1]
                    dst = take_bank(pe, step)
                    weight_ready(pe, "w0")
                    consumed(pe, ("LT", b // 2))
                    for c in range(C):
                        passes(pe, dst, (fT_h[:, c, b % 2, :], fT_l[:, c, b % 2, :]),
                               (slot_h[2][:, c, :], slot_l[2][:, c, :]), start=(c == 0), stop=False)
                    pe.matmul(dst, lora_t[:, b % 2, :], lb_h[:, :], start=False, stop=False)
                    pe.matmul(dst, lora_t[:, b % 2, :], lb_l[:, :], start=False, stop=True).then_inc(bank_full, 1)
                elif kind in ("K1", "Q1"):
                    g = step[1]
                    p, c1 = g // C, g % C
                    dst = take_bank(pe, step)
                    src, k = ((ctxT_h, ctxT_l), 0) if kind == "K1" else ((xT_h, xT_l), 1)
                    weight_ready(pe, "wk1" if kind == "K1" else "wq1")
                    for b in (2 * p, 2 * p + 1):
                        consumed(pe, ("CT", 1, b) if kind == "K1" else ("XT", 2, b))
                    last = project(pe, dst[:, 0:2 * P],
                                   lambda c: (slot_h[k][:, c, c1 * P:(c1 + 1) * P],
                                              slot_l[k][:, c, c1 * P:(c1 + 1) * P]),
                                   lambda c: [t[:, c, :, :].rearrange("p b t -> p (b t)") for t in src])
                    last.then_inc(bank_full, 1)
                elif kind == "S1":
                    g = step[1]
                    dst = take_wide(pe, step)
                    consumed(pe, ("K1", g))
                    consumed(pe, ("Q1", g))
                    for b in range(2):
                        last = passes(pe, dst[:, b, :], (K1_h[:, g % 2, b, :], K1_l[:, g % 2, b, :]),
                                      [t[:, g % 2, b, :, :].rearrange("p j q -> p (j q)") for t in (Q1_h, Q1_l)])
                    last.then_inc(wide_full, 1)
                elif kind == "SM":
                    g = step[1]
                    dst = wide(("S1", g))
                    pe.wait_ge(m1_ready, g + 1)
                    for b in range(2):
                        last = pe.matmul(dst[:, b, :], ident_r[:, :],
                                         mneg[:, g, :].unsqueeze(1).broadcast_to([P, JH, P]),
                                         start=False, stop=True, skip_group_check=True)
                    last.then_inc(shifted, 1)
                elif kind == "V1":
                    b = step[1]
                    dst = take_bank(pe, step)
                    weight_ready(pe, "wv1")
                    consumed(pe, ("CT", 2, b))
                    last = project(pe, dst, lambda c: (ctxT_h[:, c, b % 2, :], ctxT_l[:, c, b % 2, :]),
                                   lambda c: (slot_h[2][:, c, :], slot_l[2][:, c, :]))
                    last.then_inc(bank_full, 1)
                elif kind == "PV1":
                    b = step[1]
                    dst = take_bank(pe, step)
                    consumed(pe, ("V1", b))
                    pe.wait_ge(nm_dve, 3 * (b // 2 + 1))
                    pe.wait_ge(nm_pool, b // 2 + 1)
                    for c in range(C):
                        for j in range(JH):
                            h = c * JH + j
                            last = pe.matmul(dst[32 * j:32 * j + 32, c * P:(c + 1) * P],
                                             V1[:, b % 2, h * HD1:(h + 1) * HD1],
                                             P1[:, b // 2 * C + c, (b % 2) * JH + j, :], start=True, stop=True)
                    last.then_inc(bank_full, 1)
                elif kind == "OX1":
                    b = step[1]
                    dst = take_bank(pe, step)
                    consumed(pe, ("PV1", b))
                    for c in range(C):
                        last = pe.transpose(dst[:, c * P:(c + 1) * P], O1T[:, c * P:(c + 1) * P], ident[:, :])
                    last.then_inc(bank_full, 1)
                elif kind == "F1":
                    b = step[1]
                    dst = take_bank(pe, step)
                    weight_ready(pe, "wbase")
                    consumed(pe, ("XT", 3, b))
                    last = project(pe, dst, lambda c: (xT_h[:, c, b % 2, :], xT_l[:, c, b % 2, :]),
                                   lambda c: (slot_h[1][:, c, :], slot_l[1][:, c, :]))
                    last.then_inc(bank_full, 1)
                elif kind == "WM":
                    dst = take_bank(pe, step)
                    pe.wait_ge(cs_step, 3)
                    for c in range(C):
                        stage_loaded(pe, ("dft", c))
                        last = pe.matmul(dst[0:ENC, :], cs[:, c, :], stage(("dft", c)),
                                         start=(c == 0), stop=(c == C - 1))
                    last.then_inc(bank_full, 1)
                elif kind == "WE":
                    c = step[1]
                    dst = take_bank(pe, step)
                    consumed(pe, ("WM",))
                    pe.wait_ge(late_loaded, 64)
                    pe.matmul(dst, enc_sb[0:ENC, c * P:(c + 1) * P], mt[0:ENC, :],
                              start=True, stop=True).then_inc(bank_full, 1)

        @block.scalar
        def _(act):
            act.wait_ge(small_loaded, 16 * 4)
            for step in ORDER:
                kind = step[0]
                if kind == "W":
                    key = step[1:]
                    hi, _, src = parts(key)
                    stage_loaded(act, key)
                    if key[0] in last_reader:
                        filled(act, last_reader[key[0]])
                    act.activation(hi, src, ACT.Copy).then_inc(w_hi, 1)
                elif kind == "WE":
                    key = ("wbase", step[1])
                    hi, _, src = parts(key)
                    consumed(act, step)
                    filled(act, last_reader["wbase"])
                    act.activation(hi, src, ACT.Copy).then_inc(w_hi, 1)
                elif kind == "CT":
                    filled(act, step)
                    act.activation(ctxT_h[:, :, step[2] % 2, :],
                                   bank(step).rearrange("p (c t) -> p c t", c=C), ACT.Copy).then_inc(split_hi, 1)
                elif kind == "XT":
                    filled(act, step)
                    dst = fT_h if step[1] == 1 else xT_h
                    act.activation(dst[:, :, step[2] % 2, :],
                                   bank(step).rearrange("p (c t) -> p c t", c=C), ACT.Copy).then_inc(split_hi, 1)
                elif kind == "K0":
                    p = step[1]
                    filled(act, step)
                    if p >= 2:
                        act.wait_ge(km_ready, 4 * (p - 1))
                    act.activation(K_h[:, p % 2, :, :], bank(step)[:, 0:2 * P].rearrange("p (b t) -> p b t", b=2),
                                   ACT.Copy).then_inc(split_hi, 1)
                elif kind == "V0":
                    b = step[1]
                    filled(act, step)
                    act.wait_ge(consts_pool, 4)
                    act.activation(V0[:, b % 4, :, 0:HD0],
                                   bank(step)[:, P:2 * P].rearrange("p (g d) -> p g d", g=KVH),
                                   ACT.Copy).then_inc(free(step), 1)
                elif kind == "Q0":
                    p, half = step[1:]
                    filled(act, step)
                    act.activation(Q_h[:, p % 2, :, 2 * half:2 * half + 2, :],
                                   bank(step).rearrange("p (r b q) -> p b r q", r=2, b=2),
                                   ACT.Copy).then_inc(split_hi, 1)
                elif kind == "ST":
                    b, g2 = step[1:]
                    n = 4 * b + g2
                    wide_filled(act, step)
                    if n >= 4:
                        filled(act, ("PV", (n - 4) // 4, (n - 4) % 4 // 2))
                    act.activation(PT[:, n % 4, :], wide(step).rearrange("p k n -> p (k n)"), ACT.Exp,
                                   scale=SCALE0).then_inc(wide_free[WIDE[step] % 2], 1)
                elif kind == "PV":
                    b, gq = step[1:]
                    filled(act, step)
                    act.activation(OTs[:, gq, :], bank(step), ACT.Copy).then_inc(free(step), 1)
                elif kind == "OX":
                    b = step[1]
                    filled(act, step)
                    act.activation(OT_h[:, b % 2, :, :], bank(step).rearrange("p (c t) -> p c t", c=C),
                                   ACT.Copy).then_inc(split_hi, 1)
                elif kind == "LT":
                    p = step[1]
                    filled(act, step)
                    act.wait_ge(lora_ready, 5)
                    for k in range(2):
                        b = 2 * p + k
                        last = act.activation(lora_t[:, k, :], bank(step)[:, k * P:(k + 1) * P], ACT.Identity,
                                              scale=use_lora[:, b:b + 1], bias=tab[:, KVH + B + 1:KVH + B + 2])
                    last.then_inc(split_hi, 1)
                elif kind == "K1":
                    g = step[1]
                    filled(act, step)
                    act.activation(K1_h[:, g % 2, :, :], bank(step)[:, 0:2 * P].rearrange("p (b t) -> p b t", b=2),
                                   ACT.Identity, bias=bias_qk[:, 0, g % C:g % C + 1]).then_inc(split_hi, 1)
                elif kind == "Q1":
                    g = step[1]
                    filled(act, step)
                    act.wait_ge(zero_q1, 4)
                    for j in range(JH):
                        rows = slice(j * HD1, (j + 1) * HD1)
                        last = act.activation(Q1_h[rows, g % 2, :, j, :],
                                              bank(step)[rows, 0:2 * P].rearrange("p (b t) -> p b t", b=2),
                                              ACT.Identity, bias=bias_qk[rows, 1, g % C:g % C + 1])
                    last.then_inc(split_hi, 1)
                elif kind == "SM":
                    g = step[1]
                    act.wait_ge(shifted, g + 1)
                    act.activation(P1[:, g, :, :].rearrange("p t q -> p (t q)"),
                                   wide(("S1", g)).rearrange("p k n -> p (k n)"),
                                   ACT.Exp, scale=SCALE1).then_inc(wide_free[WIDE[("S1", g)] % 2], 1)
                elif kind == "FA":
                    act.wait_ge(fac_dve, 2)
                    act.activation(fac[:, :, :], fac[:, :, :], ACT.Exp, scale=SCALE1).then_inc(fac_act, 1)
                elif kind == "PV1":
                    b = step[1]
                    filled(act, step)
                    act.activation(O1T[:, :], bank(step), ACT.Copy).then_inc(free(step), 1)

        @block.vector
        def _(dve):
            dve.wait_ge(small_loaded, 16 * 4)
            dve.tensor_copy(ident_r[:, :], ident[:, :]).then_inc(consts_dve, 1)
            dve.tensor_copy(select[:, :, :],
                            ident[:, 0:KVH].unsqueeze(2).broadcast_to([P, KVH, P])).then_inc(consts_dve, 1)
            dve.tensor_copy(starts_f[:, :], starts_i[:, :]).then_inc(lora_ready, 1)
            dve.wait_ge(lora_ready, 1)
            dve.tensor_tensor(started[:, :, :], starts_f[:, :].unsqueeze(1).broadcast_to([P, B, 4]),
                              tab[:, KVH:KVH + B].unsqueeze(2).broadcast_to([P, B, 4]),
                              ALU.is_le).then_inc(lora_ready, 1)
            dve.wait_ge(lora_ready, 2)
            dve.tensor_reduce(n_started[:, :], started[:, :, :], AX_X, ALU.add).then_inc(lora_ready, 1)
            dve.wait_ge(lora_ready, 3)
            dve.tensor_scalar(use_lora[:, :], n_started[:, :], tab[:, KVH + B:KVH + B + 1], None,
                              ALU.is_equal).then_inc(lora_ready, 1)
            dve.wait_ge(lora_ready, 4)
            dve.memset(lb_l[TOP:P, :].bitcast(F32), 0.0).then_inc(lora_ready, 1)
            for step in ORDER:
                kind = step[0]
                if kind == "W" and step[1] not in BY_POOL:
                    key = step[1:]
                    hi, lo, src = parts(key)
                    if key[0] == "lb":
                        hi, src = hi[0:TOP, :], src[0:TOP, :]
                    dve.wait_ge(w_hi, hi_count(key))
                    dve.tensor_tensor(lo, src, hi.bitcast(F32), ALU.subtract).then_inc(w_lo, 1)
                elif kind == "WE":
                    key = ("wbase", step[1])
                    filled(dve, step)
                    stage_loaded(dve, key)
                    hi, lo, src = parts(key)
                    dve.tensor_tensor(src, bank(step), src, ALU.add).then_inc(free(step), 1)
                    dve.wait_ge(w_hi, hi_count(key))
                    dve.tensor_tensor(lo, src, hi.bitcast(F32), ALU.subtract).then_inc(w_lo, 1)
                elif kind == "LNs":
                    layer, b = step[1:]
                    n = NORM[step]
                    if layer == 0:
                        dve.wait_ge(x_loaded[b], 16)
                    else:
                        consumed(dve, [None, ("WO", b), ("F0", b), ("OX1", b)][layer])
                    if n >= 4:
                        dve.wait_ge(rstd_ready, n - 3)
                    dve.bn_stats(stats[:, n % 4, :], X[:, b, :]).then_inc(stat_done, 1)
                    dve.wait_ge(stat_done, n + 1)
                    dve.bn_aggr(moments[:, n % 4, :], stats[:, n % 4, :]).then_inc(moments_ready, 1)
                elif kind == "LNn":
                    layer, b = step[1:]
                    n = NORM[("LNs", layer, b)]
                    old = earlier_norm(("LNs", layer, b))
                    if old:
                        filled(dve, ("XT",) + old[1:])
                    dve.wait_ge(rstd_ready, n + 1)
                    dve.tensor_scalar(xn[:, XN_SLOT[("LNs", layer, b)], :], X[:, b, :], moments[:, n % 4, 0:1], rstd[:, n % 4, 0:1],
                                      ALU.subtract, ALU.mult).then_inc(xn_ready, 1)
                elif kind in ("CT", "XT", "OX"):
                    hi_written(dve, step)
                    if kind == "OX":
                        lo, hi = [t[:, step[1] % 2, :, :] for t in (OT_l, OT_h)]
                    else:
                        ts = (ctxT_l, ctxT_h) if kind == "CT" else (fT_l, fT_h) if step[1] == 1 else (xT_l, xT_h)
                        lo, hi = [t[:, :, step[2] % 2, :] for t in ts]
                    dve.tensor_tensor(lo, bank(step).rearrange("p (c t) -> p c t", c=C), hi.bitcast(F32),
                                      ALU.subtract).then_inc(free(step), 1)
                elif kind == "K0":
                    p = step[1]
                    hi_written(dve, step)
                    dve.tensor_tensor(K_l[:, p % 2, :, :], bank(step)[:, 0:2 * P].rearrange("p (b t) -> p b t", b=2),
                                      K_h[:, p % 2, :, :].bitcast(F32), ALU.subtract).then_inc(free(step), 1)
                elif kind == "Q0":
                    p, half = step[1:]
                    rs = slice(2 * half, 2 * half + 2)
                    hi_written(dve, step)
                    dve.tensor_tensor(Q_l[:, p % 2, :, rs, :], bank(step).rearrange("p (r b q) -> p b r q", r=2, b=2),
                                      Q_h[:, p % 2, :, rs, :].bitcast(F32), ALU.subtract).then_inc(free(step), 1)
                elif kind == "MX":
                    b, r = step[1:]
                    wide_filled(dve, step)
                    dve.tensor_reduce(mx[:, b % 2, r, :], wide(step).rearrange("p k (g t) -> p (k g) t", g=4),
                                      AX_X, ALU.max).then_inc(wide_free[WIDE[step] % 2], 1)
                elif kind == "MT":
                    b = step[1]
                    filled(dve, step)
                    dve.wait_ge(consts_pool, 4)
                    dve.tensor_scalar(negmax[0:KVH, b % 2, :], bank(step)[0:KVH, :], -1.0, None,
                                      ALU.mult).then_inc(free(step), 1)
                elif kind == "OB":
                    b, gq = step[1:]
                    filled(dve, step)
                    src = bank(step).rearrange("p (r j e) -> p r j e", r=REP, j=4)
                    dve.reciprocal(rec[:, gq, :, :], src[:, :, :, HD0]).then_inc(rec_ready, 1)
                    dve.wait_ge(rec_ready, 2 * b + gq + 1)
                    dst = O[:, b % 2, :].rearrange("p (g r d) -> p r g d", g=KVH, r=REP)[:, :, 4 * gq:4 * gq + 4, :]
                    dve.tensor_tensor(dst, src[:, :, :, 0:HD0],
                                      rec[:, gq, :, :].unsqueeze(3).broadcast_to([P, REP, 4, HD0]),
                                      ALU.mult).then_inc(free(step), 1)
                elif kind in ("WO", "F0"):
                    b = step[1]
                    filled(dve, step)
                    dve.tensor_tensor(X[:, b, :], bank(step), X[:, b, :], ALU.add).then_inc(free(step), 1)
                elif kind == "LT":
                    p = step[1]
                    hi_written(dve, step)
                    for k in range(2):
                        b = 2 * p + k
                        last = dve.scalar_tensor_tensor(
                            out=lora_t[TOP:P, k, :], in0=bank(step)[TOP:P, k * P:(k + 1) * P],
                            scalar=use_lora[TOP:P, b:b + 1], in1=lora_t[TOP:P, k, :].bitcast(F32),
                            op0=ALU.mult, op1=ALU.subtract)
                    last.then_inc(free(step), 1)
                elif kind == "K1":
                    g = step[1]
                    hi_written(dve, step)
                    dve.scalar_tensor_tensor(
                        out=K1_l[:, g % 2, :, :], in0=bank(step)[:, 0:2 * P].rearrange("p (b t) -> p b t", b=2),
                        scalar=bias_qk[:, 0, g % C:g % C + 1], in1=K1_h[:, g % 2, :, :].bitcast(F32),
                        op0=ALU.add, op1=ALU.subtract).then_inc(free(step), 1)
                elif kind == "Q1":
                    g = step[1]
                    hi_written(dve, step)
                    dve.wait_ge(zero_q1, 4)
                    for j in range(JH):
                        rows = slice(j * HD1, (j + 1) * HD1)
                        last = dve.scalar_tensor_tensor(
                            out=Q1_l[rows, g % 2, :, j, :],
                            in0=bank(step)[rows, 0:2 * P].rearrange("p (b t) -> p b t", b=2),
                            scalar=bias_qk[rows, 1, g % C:g % C + 1], in1=Q1_h[rows, g % 2, :, j, :].bitcast(F32),
                            op0=ALU.add, op1=ALU.subtract)
                    last.then_inc(free(step), 1)
                elif kind == "S1":
                    g = step[1]
                    wide_filled(dve, step)
                    dve.tensor_reduce(mneg[:, g, :], wide(step).rearrange("p k (j q) -> p q (k j)", j=JH),
                                      AX_X, ALU.max, negate=True).then_inc(m1_ready, 1)
                elif kind == "SM":
                    g = step[1]
                    wide_consumed(dve, ("S1", g))
                    dve.tensor_reduce(Z[:, g, :], P1[:, g, :, :].rearrange("p t q -> p q t"),
                                      AX_X, ALU.add).then_inc(z_ready, 1)
                elif kind == "FA":
                    dve.wait_ge(z_ready, GROUPS)
                    dve.wait_ge(m1_ready, GROUPS)
                    neg = mneg[:, :, :].bitcast(F32)
                    dve.tensor_reduce(nmin[:, :], neg.rearrange("p g q -> p q g"), AX_X, ALU.min).then_inc(fac_dve, 1)
                    dve.wait_ge(fac_dve, 1)
                    dve.tensor_tensor(fac[:, :, :], nmin[:, :].unsqueeze(1).broadcast_to([P, GROUPS, P]), neg,
                                      ALU.subtract).then_inc(fac_dve, 1)
                    dve.wait_ge(fac_act, 1)
                    dve.tensor_tensor(Z[:, :, :], Z[:, :, :], fac[:, :, :], ALU.mult).then_inc(fac_dve, 1)
                    dve.wait_ge(fac_dve, 3)
                    dve.tensor_reduce(nmin[:, :], Z[:, :, :].rearrange("p g q -> p q g"), AX_X,
                                      ALU.add).then_inc(fac_dve, 1)
                    dve.wait_ge(fac_dve, 4)
                    dve.reciprocal(nmin[:, :], nmin[:, :]).then_inc(fac_dve, 1)
                    dve.wait_ge(fac_dve, 5)
                    dve.tensor_tensor(fac[:, :, :], fac[:, :, :], nmin[:, :].unsqueeze(1).broadcast_to([P, GROUPS, P]),
                                      ALU.mult).then_inc(fac_dve, 1)
                elif kind == "NM" and step[1] % C != C - 1:
                    g = step[1]
                    dve.wait_ge(fac_dve, 6)
                    dve.tensor_tensor(P1[:, g, :, :], P1[:, g, :, :],
                                      fac[:, g, :].unsqueeze(1).broadcast_to([P, T, P]),
                                      ALU.mult).then_inc(nm_dve, 1)
                elif kind == "V1":
                    b = step[1]
                    filled(dve, step)
                    dve.wait_ge(bias_v_loaded, 16)
                    dve.tensor_tensor(V1[:, b % 2, :], bank(step), bias_v[:, :], ALU.add).then_inc(free(step), 1)
                elif kind == "OX1":
                    b = step[1]
                    filled(dve, step)
                    dst = X[:, b, :].rearrange("p (d h) -> p h d", h=H1)
                    dve.tensor_tensor(dst, bank(step).rearrange("p (h d) -> p h d", h=H1), dst,
                                      ALU.add).then_inc(free(step), 1)
                elif kind == "F1":
                    b = step[1]
                    filled(dve, step)
                    dve.wait_ge(xb_ready, b + 1)
                    dve.tensor_tensor(XB[:, b % 2, :], bank(step), XB[:, b % 2, :], ALU.add).then_inc(free(step), 1)
                elif kind == "WC":
                    dve.wait_ge(late_loaded, 64)
                    dve.tensor_tensor(cf[:, :, :, :], cf[:, :, :, :],
                                      mk[:, :].bitcast(U8).rearrange("p (c e r) -> p c e r", c=C, e=EXP),
                                      ALU.mult).then_inc(cs_step, 1)
                    dve.wait_ge(cs_step, 1)
                    dve.tensor_tensor(cs[:, :, :], cf[:, :, 0, :], cf[:, :, 1, :], ALU.add).then_inc(cs_step, 1)
                    dve.wait_ge(cs_step, 2)
                    dve.tensor_tensor(cs[:, :, :], cs[:, :, :], cf[:, :, 2, :], ALU.add).then_inc(cs_step, 1)
                elif kind == "WM":
                    filled(dve, step)
                    consumed(dve, ("F0", B - 1))
                    dve.tensor_copy(mt[0:ENC, :], bank(step)[0:ENC, :]).then_inc(free(step), 1)

        @block.gpsimd
        def _(pool):
            pool.memset(minus_half[:, :], -0.5).then_inc(consts_pool, 1)
            pool.memset(V0[:, :, :, :], 0.0).then_inc(consts_pool, 1)
            pool.wait_ge(consts_pool, 2)
            pool.memset(V0[:, :, :, HD0:HD0 + 1], 1.0).then_inc(consts_pool, 1)
            pool.memset(negmax[:, :, :].bitcast(F32), 0.0).then_inc(consts_pool, 1)
            pool.wait_ge(small_loaded, 16 * 4)
            for step in ORDER:
                kind = step[0]
                if kind == "W" and step[1] in BY_POOL:
                    key = step[1:]
                    hi, lo, src = parts(key)
                    pool.wait_ge(w_hi, hi_count(key))
                    pool.tensor_tensor(lo, src, hi.bitcast(F32), ALU.subtract).then_inc(w_lo_pool, 1)
                elif kind == "LNs":
                    n = NORM[step]
                    pool.wait_ge(moments_ready, n + 1)
                    if n >= 4:
                        pool.wait_ge(xn_ready, n - 3)
                    pool.tensor_scalar(var_eps[:, n % 4, :], moments[:, n % 4, 1:2], EPS, None,
                                       ALU.add).then_inc(eps_done, 1)
                    pool.wait_ge(eps_done, n + 1)
                    pool.tensor_tensor(rstd[:, n % 4, :], var_eps[:, n % 4, :], minus_half[:, :],
                                       ALU.pow).then_inc(rstd_ready, 1)
                elif kind == "KM":
                    b = step[1]
                    consumed(pool, ("K0", b // 2))
                    if b >= 2:
                        wide_consumed(pool, ("ST", b - 2, 3))
                    own = tab[:, 0:KVH].unsqueeze(2).broadcast_to([P, KVH, P])
                    for src, dst in ((K_h, KM_h), (K_l, KM_l)):
                        pool.tensor_tensor(dst[:, b % 2, :, :],
                                           src[:, b // 2 % 2, b % 2, :].bitcast(F32).unsqueeze(1).broadcast_to([P, KVH, P]),
                                           own, ALU.mult).then_inc(km_ready, 1)
                elif kind == "PH2":
                    consumed(pool, ("F0", B - 1))
                    for t in (Q1_h, Q1_l):
                        for k in range(2):
                            pool.memset(t[:, k, :, :, :].bitcast(F32), 0.0).then_inc(zero_q1, 1)
                elif kind == "NM" and step[1] % C == C - 1:
                    g = step[1]
                    pool.wait_ge(fac_dve, 6)
                    pool.tensor_tensor(P1[:, g, :, :], P1[:, g, :, :],
                                       fac[:, g, :].unsqueeze(1).broadcast_to([P, T, P]),
                                       ALU.mult).then_inc(nm_pool, 1)
                elif kind == "OX1":
                    b = step[1]
                    consumed(pool, step)
                    pool.wait_ge(late_loaded, 64)
                    if b >= 2:
                        pool.wait_ge(out_stored[b % 2], 16 * (b // 2))
                    pool.tensor_tensor(XB[:, b % 2, :], X[:, b, :], bias_out[:, :], ALU.add).then_inc(xb_ready, 1)


def kernel(**inputs):
    import numpy as np
    import concourse.bacc as bacc
    from concourse import mybir as _mybir
    from concourse.bass_utils import run_bass_kernel_spmd as run

    a = {k: np.asarray(v) for k, v in inputs.items()}
    f = np.float32
    wq0 = a["L0_xattn_Wq"].reshape(D, KVH, REP, HD0).transpose(0, 2, 1, 3).reshape(D, D)
    lora_a = a["L0_ffn_lora_A"].reshape(RANK, D).T
    la = np.zeros((D, P), f)
    la[:, 0:RANK] = lora_a
    la[:, TOP:TOP + RANK] = lora_a
    lora_b = a["L0_ffn_lora_B"].transpose(0, 2, 1).reshape(RANK, D)
    lb = np.zeros((P, D), f)
    lb[0:RANK] = lora_b
    lb[RANK] = a["L0_ffn_bias"]
    lb[TOP:TOP + RANK] = lora_b
    packed = lambda u, v: np.concatenate([u, v], axis=2).reshape(EXP, C, P, ENC).transpose(2, 1, 0, 3)
    n = np.arange(D)
    k = np.arange(1, (D - 1) // 2 + 1)[:, None]
    dft = np.zeros((D, D))
    dft[0] = D ** -0.5
    dft[1:D - 1:2] = np.sqrt(2.0 / D) * np.cos(2 * np.pi * (k * n % D) / D)
    dft[2:D:2][:len(k)] = np.sqrt(2.0 / D) * np.sin(2 * np.pi * (k * n % D) / D)
    dft[D - 1] = np.where(n % 2 == 0, 1.0, -1.0) * D ** -0.5
    dft = (0.5 * dft).astype(f)
    row = np.arange(P)
    table = np.zeros((P, KVH + B + 2), f)
    table[:, 0:KVH] = row[:, None] // HD0 == np.arange(KVH)[None]
    table[:, KVH:KVH + B] = np.arange(B)[None]
    table[:, KVH + B] = np.where(row % TOP < RANK, row % TOP // 16 + 2, -1)
    table[:, KVH + B + 1] = row == RANK
    arrays = {
        "x": a["x"], "ctx": a["ctx_4096"],
        "wkv": np.concatenate([a["L0_xattn_Wk"], a["L0_xattn_Wv"]], axis=1), "wq0": wq0,
        "wo": a["L0_xattn_Wo"], "la": la, "lb": lb, "w0": a["L0_ffn_weight"].T,
        "starts": a["L0_ffn_lora_start_indices"],
        "wk1": a["L1_xattn_Wk"].T, "wq1": a["L1_xattn_Wq"].T, "wv1": a["L1_xattn_Wv"].T,
        "biases": np.stack([a["L1_xattn_bk"], a["L1_xattn_bq"]]).reshape(2, C, P).transpose(2, 0, 1),
        "bv1": a["L1_xattn_bv"],
        "wbase": a["L1_ffn_W_base"].T, "bbase": a["L1_ffn_b_base"],
        "enc": np.concatenate([a["L1_ffn_enc0"], a["L1_ffn_enc1"]], axis=0),
        "coefs": packed(a["L1_ffn_coefs0"], a["L1_ffn_coefs1"]),
        "masks": packed(a["L1_ffn_mask0"], a["L1_ffn_mask1"]).reshape(P, -1).view(np.int32),
        "dft": dft, "eye": np.eye(P, dtype=f), "table": table,
    }
    nc = bacc.Bacc("TRN2", target_bir_lowering=False, num_devices=1)
    feeds, args = {}, []
    for name, v in arrays.items():
        v = np.ascontiguousarray(v)
        feeds[f"in_{name}"] = v
        args.append(nc.dram_tensor(f"in_{name}", v.shape, _mybir.dt.from_np(v.dtype), kind="ExternalInput").ap())
    args.append(nc.dram_tensor("out_0", (B, S, D), F32, kind="ExternalOutput").ap())
    build(nc, *args)
    r = run(nc, [feeds], core_ids=[0])
    return r.results[0]["out_0"]
```

```python
from contextlib import ExitStack

import concourse.bass as bass
from concourse import mybir

F32 = mybir.dt.float32
F32R = mybir.dt.float32r
U8 = mybir.dt.uint8
I32 = mybir.dt.int32
ALU = mybir.AluOpType
ACT = mybir.ActivationFunctionType
AX_X = mybir.AxisListType.X

B, S, D = 8, 128, 512
P = 128
C = D // P
PAIRS = B // 2
KVH, REP, HD0 = 8, 4, 16
H1, HD1 = 16, 32
JH = P // HD1
GROUPS = PAIRS * C
T = 2 * JH
RANK = 48
TOP = 64
LAST = 96
ENC = 40
EXP = 3
EPS = 1e-5
SCALE0 = HD0 ** -0.5
SCALE1 = HD1 ** -0.5
NG = 4
NSTG = 4

CHUNKS = ([("wkv", 0), ("wkv", 1)] + [("wq0", c) for c in range(C)] + [("wo", c) for c in range(C)]
          + [("la", 0), ("lb", 0)] + [("w0", c) for c in range(C)]
          + [("wk1", c) for c in range(C)] + [("wq1", c) for c in range(C)]
          + [("wv1", c) for c in range(C)] + [("dft", c) for c in range(C)]
          + [("wbase", c) for c in range(C)])
CHUNK = {key: n for n, key in enumerate(CHUNKS)}
BY_POOL = ("wk1", "wq1", "wv1")


EVEN = [("LNs", 0, 2), ("MX", 1, 0), ("OB", -1, 0), ("ST", 0, 0), ("OB", -1, 1), ("CT", 0, 2), ("MX", 1, 1),
        ("LNn", 0, 2), ("XT", 1, -2), ("OX", -1), ("ST", 0, 1), ("CT", 0, 3), ("LNs", 0, 3), ("XT", 0, 2), ("MX", 1, 2),
        ("WO", -1), ("K0", 1), ("LNn", 0, 3), ("ST", 0, 2), ("KM", 2), ("MX", 1, 3), ("V0", 2), ("LNs", 1, -1), ("PV", 0, 0),
        ("XT", 0, 3), ("V0", 3), ("LNn", 1, -1), ("ST", 0, 3), ("MT", 1), ("DM", 1), ("Q0", 1, 0), ("PV", 0, 1), ("Q0", 1, 1),
        ("DK", 2), ("DQ", 2)]
ODD = [("KM", 2), ("MX", 1, 0), ("OB", -1, 0), ("ST", 0, 0), ("OB", -1, 1), ("XT", 1, -2), ("MX", 1, 1), ("OX", -1),
       ("ST", 0, 1), ("LT", -1), ("MX", 1, 2), ("WO", -1), ("ST", 0, 2), ("PV", 0, 0), ("MX", 1, 3),
       ("F0", -3), ("LNs", 1, -1), ("ST", 0, 3), ("MT", 1), ("DM", 1), ("LNn", 1, -1), ("F0", -2), ("PV", 0, 1),
       ("DK", 2), ("DQ", 2)]
EXTRA = {0: {0: "first", 4: "wo"}, 1: {8: "wo2"}, 2: {4: "la", 8: "lb", 20: "w0"}, 6: {12: "wk1", 20: "turned"}}


def plan():
    order = []

    def weights(name):
        return [("W", name, c) for n, c in CHUNKS if n == name]

    def norms1(p):
        return [("LNs", 2, 2 * p), ("LNs", 2, 2 * p + 1), ("LNn", 2, 2 * p), ("LNn", 2, 2 * p + 1)]

    def turned1(p):
        return [("CT", 1, 2 * p), ("XT", 2, 2 * p), ("CT", 1, 2 * p + 1), ("XT", 2, 2 * p + 1)]

    def slot(b):
        out = []
        for n, step in enumerate(EVEN if b % 2 == 0 else ODD):
            out += extra(b, n)
            kind = step[0]
            if kind in ("K0", "Q0", "LT"):
                step = (kind, b // 2 + step[1]) + step[2:]
                if 0 <= step[1] < PAIRS:
                    out.append(step)
            elif kind in ("LNs", "LNn", "XT", "CT"):
                step = step[:2] + (b + step[2],)
                if 0 <= step[2] < B:
                    out.append(step)
            else:
                step = (kind, b + step[1]) + step[2:]
                if 0 <= step[1] < B:
                    out.append(step)
        return out

    def extra(b, n):
        name = EXTRA.get(b, {}).get(n)
        if name is None:
            return []
        if name == "first":
            return [("KM", 1), ("DK", 1), ("DQ", 1)]
        if name == "turned":
            return norms1(0) + turned1(0)
        if name in ("wo", "wo2"):
            ws = weights("wo")
            return ws[:2] if name == "wo" else ws[2:]
        return weights(name)

    order += weights("wkv")
    for b in range(2):
        order += [("LNs", 0, b), ("CT", 0, b), ("LNn", 0, b)]
    order += [("K0", 0), ("KM", 0), ("V0", 0), ("XT", 0, 0), ("V0", 1), ("XT", 0, 1)]
    order += weights("wq0") + [("Q0", 0, 0), ("Q0", 0, 1)]
    order += [("DK", 0), ("DQ", 0)] + [("MX", 0, r) for r in range(REP)] + [("MT", 0), ("DM", 0)]
    for b in range(B):
        order += slot(b)

    b = B - 1
    order += [("OB", b, 0), ("OB", b, 1), ("OX", b), ("PH2",), ("K1", 0), ("XT", 1, b - 1), ("WO", b), ("K1", 1),
              ("LNs", 1, b), ("LNn", 1, b)] + weights("wq1") + [("XT", 1, b)]
    order += [("Q1", 0), ("LT", PAIRS - 1), ("Q1", 1), ("F0", B - 2), ("F0", B - 1)]
    for g in range(GROUPS):
        order += [("S1", g)]
        if g + 2 < GROUPS:
            order += [("K1", g + 2), ("Q1", g + 2)]
        p = (g + 3) // C
        if g % C == 0 and p < PAIRS and g + 4 < GROUPS:
            order += norms1(g // C + 1)
        if (g + 3) % C == 0 and p < PAIRS:
            order += turned1(p)
        order += [("SM", g)]
        if g == 0:
            order += weights("wv1")
        if g == C:
            order += [("WC",), ("WM",)]

    order += [("CT", 2, 0), ("FA", 0), ("CT", 2, 1), ("V1", 0), ("CT", 2, 2), ("V1", 1), ("FA", 1)]
    for b in range(2, B):
        if b == 3:
            order += [("NM", c) for c in range(C)]
        if b == 6:
            order += [("WE", c) for c in range(C)]
        if b + 1 < B:
            order += [("CT", 2, b + 1)]
        order += [("V1", b)]
    for b in range(B):
        order += [("PV1", b)]
        if b:
            order += [("XT", 3, b - 1)]
        order += [("OX1", b), ("LNs", 3, b)]
        if b // 2 + 1 < PAIRS:
            order += [("NM", (b // 2 + 1) * C + 2 * (b % 2) + k) for k in range(2)]
        if b:
            order += [("F1", b - 1)]
        order += [("LNn", 3, b)]
    order += [("XT", 3, B - 1), ("F1", B - 1)]
    return order


ORDER = plan()
BANK_STEPS = ("CT", "K0", "V0", "XT", "Q0", "MT", "PV", "OB", "OX", "WO", "LT", "F0", "K1", "Q1", "V1",
              "PV1", "OX1", "F1", "WM", "WE")
SPLIT_STEPS = ("CT", "K0", "XT", "Q0", "OX", "LT", "K1", "Q1")


def numbered(kinds):
    return {step: n for n, step in enumerate(s for s in ORDER if s[0] in kinds)}


BANK = numbered(BANK_STEPS)
WIDE = numbered(("MX", "ST", "S1"))
SPLIT = numbered(SPLIT_STEPS)
NORM = numbered(("LNs",))
XN_SLOT = {s: n % 2 for s, n in NORM.items()}


def earlier_norm(step):
    same = [s for s in NORM if XN_SLOT[s] == XN_SLOT[step] and NORM[s] < NORM[step]]
    return same[-1] if same else None


CTX = numbered(("CT",))


def build(nc, x, ctx, wkv, wq0, wo, la, lb, w0, starts, wk1, wq1, wv1, biases, bv1, wbase, bbase, enc,
          coefs, masks, dft, eye, table, out):
    with ExitStack() as always:
        def sb(name, shape, dt=F32, where=always):
            return where.enter_context(nc.sbuf_tensor(name, [P] + list(shape), dt))

        def sem(name):
            return always.enter_context(nc.semaphore(name))

        X = sb("X", [B, D])
        slot_h = [None] + [sb(f"slot{k}_h", [C, D], F32R) for k in (1, 2)]
        slot_l = [None] + [sb(f"slot{k}_l", [C, D], F32R) for k in (1, 2)]
        stg = sb("stg", [NSTG, D])
        ident = sb("ident", [P])
        ident_r = sb("ident_r", [P], F32R)
        ctx_in = sb("ctx_in", [2, D])
        ctxT_h, ctxT_l = sb("ctxT_h", [C, 2, P], F32R), sb("ctxT_l", [C, 2, P], F32R)
        xT_h, xT_l = sb("xT_h", [C, 2, P], F32R), sb("xT_l", [C, 2, P], F32R)
        xn = sb("xn", [2, D])
        stats = sb("stats", [4, 6])
        moments = sb("moments", [4, 2])
        var_eps = sb("var_eps", [4, 1])
        rstd = sb("rstd", [4, 1])
        minus_half = sb("minus_half", [1])
        bias_qk = sb("bias_qk", [2, C])
        tab = sb("tab", [KVH + B + 2 + KVH])
        with ExitStack() as short:
            slot_h[0] = sb("slot0_h", [C, D], F32R, short)
            slot_l[0] = sb("slot0_l", [C, D], F32R, short)
        V1 = sb("V1", [B, D])
        with ExitStack() as first:
            def s1(name, shape, dt=F32):
                return sb(name, shape, dt, first)
            wkv_h, wkv_l = s1("wkv_h", [C, 256], F32R), s1("wkv_l", [C, 256], F32R)
            KM_h, KM_l = s1("KM_h", [2, KVH, P], F32R), s1("KM_l", [KVH, P], F32R)
            K_h, K_l = s1("K_h", [2, 2, P], F32R), s1("K_l", [2, 2, P], F32R)
            V0 = s1("V0", [4, KVH, 32])
            la_h, la_l = s1("la_h", [C, P], F32R), s1("la_l", [C, P], F32R)
            lb_h, lb_l = s1("lb_h", [D], F32R), s1("lb_l", [D], F32R)
            fT_h, fT_l = s1("fT_h", [C, 2, P], F32R), s1("fT_l", [C, 2, P], F32R)
            lora_t = s1("lora_t", [2, P], F32R)
            OT_h, OT_l = s1("OT_h", [C, P], F32R), s1("OT_l", [C, P], F32R)
            starts_i = s1("starts_i", [4], I32)
            starts_f = s1("starts_f", [4])
            started = s1("started", [B, 4])
            n_started = s1("n_started", [B])
            use_lora = s1("use_lora", [B])
            Q_h, Q_l = s1("Q_h", [2, REP, P], F32R), s1("Q_l", [2, REP, P], F32R)
            QS, KS = s1("QS", [2, KVH // 2, D], F32R), s1("KS", [2, KVH, P], F32R)
            mx = s1("mx", [2, REP, KVH])
            negmax = s1("negmax", [2, D], F32R)
            PT = s1("PT", [4, 2 * D])
            OTs = s1("OTs", [2, D])
            rec = s1("rec", [2, REP, 4])
            O = s1("O", [D])
        with ExitStack() as second:
            def s2(name, shape, dt=F32):
                return sb(name, shape, dt, second)
            P1 = s2("P1", [GROUPS, T, P])
            K1_h, K1_l = s2("K1_h", [2, 2, P], F32R), s2("K1_l", [2, 2, P], F32R)
            Q1_h, Q1_l = s2("Q1_h", [2, 2, JH, P], F32R), s2("Q1_l", [2, 2, JH, P], F32R)
            mneg = s2("mneg", [GROUPS, P], F32R)
            Z = s2("Z", [GROUPS, P])
            enc_sb = s2("enc_sb", [D])
            mt = s2("mt", [D])
            bias_out = s2("bias_out", [D])
            nmin = s2("nmin", [P])
            zpart = s2("zpart", [JH, P])
        with ExitStack() as early:
            sb("under_early", [(GROUPS - 1) * T * P], F32, early)
            cf = sb("cf", [C, EXP, ENC], F32, early)
            mk = sb("mk", [C * EXP * ENC // 4], I32, early)
            cs = sb("cs", [C, ENC], F32, early)
        with ExitStack() as third:
            sb("under_third", [GROUPS * T * P], F32, third)
            fac = sb("fac", [GROUPS, P], F32, third)
            O1T = sb("O1T", [D], F32, third)
            XB = sb("XB", [2, D], F32, third)
            bias_v = sb("bias_v", [D], F32, third)
        ps = always.enter_context(nc.psum_tensor("ps", [P, 8, D], F32))

        x_loaded = [sem(f"x_loaded{b}") for b in range(B)]
        ctx_loaded = [sem(f"ctx_loaded{k}") for k in range(2)]
        stg_loaded = [sem(f"stg_loaded{k}") for k in range(NSTG)]
        small_loaded = sem("small_loaded")
        late_loaded = sem("late_loaded")
        out_stored = [sem(f"out_stored{k}") for k in range(2)]
        bias_v_loaded = sem("bias_v_loaded")
        bank_full = sem("bank_full")
        bank_free = [sem(f"bank_free{k}") for k in range(NG)]
        wide_full = sem("wide_full")
        wide_free = [sem(f"wide_free{k}") for k in range(2)]
        split_hi = sem("split_hi")
        w_hi = sem("w_hi")
        w_lo = sem("w_lo")
        w_lo_pool = sem("w_lo_pool")
        w_sum = sem("w_sum")
        km_ready = sem("km_ready")
        ks_loaded = [sem(f"ks_loaded{k}") for k in range(2)]
        qs_loaded = [sem(f"qs_loaded{k}") for k in range(2)]
        max_loaded = [sem(f"max_loaded{k}") for k in range(2)]
        consts_pool = sem("consts_pool")
        consts_dve = sem("consts_dve")
        lora_ready = sem("lora_ready")
        stat_done, moments_ready = sem("stat_done"), sem("moments_ready")
        eps_done, rstd_ready = sem("eps_done"), sem("rstd_ready")
        xn_ready = sem("xn_ready")
        rec_ready = sem("rec_ready")
        cs_step = sem("cs_step")
        m1_ready = sem("m1_ready")
        shifted = sem("shifted")
        z_ready = sem("z_ready")
        zero_q1 = sem("zero_q1")
        fac_dve, fac_act = sem("fac_dve"), sem("fac_act")
        nm_dve, nm_pool = sem("nm_dve"), sem("nm_pool")
        xb_ready = sem("xb_ready")

        def filled(eng, step):
            eng.wait_ge(bank_full, BANK[step] + 1)

        def consumed(eng, step):
            n = BANK[step]
            eng.wait_ge(bank_free[n % NG], n // NG + 1)

        def bank(step):
            return ps[:, BANK[step] % NG, :]

        def free(step):
            return bank_free[BANK[step] % NG]

        def take_bank(eng, step):
            n = BANK[step]
            if n >= NG:
                eng.wait_ge(bank_free[n % NG], n // NG)
            return bank(step)

        def wide(step):
            k = NG + 2 * (WIDE[step] % 2)
            return ps[:, k:k + 2, :]

        def wide_filled(eng, step):
            eng.wait_ge(wide_full, WIDE[step] + 1)

        def wide_consumed(eng, step):
            n = WIDE[step]
            eng.wait_ge(wide_free[n % 2], n // 2 + 1)

        def take_wide(eng, step):
            n = WIDE[step]
            if n >= 2:
                eng.wait_ge(wide_free[n % 2], n // 2)
            return wide(step)

        def hi_written(eng, step):
            eng.wait_ge(split_hi, SPLIT[step] + 1)

        def weight_ready(eng, name):
            mine = [k for k, (n, _) in enumerate(CHUNKS) if n == name]
            if name in BY_POOL:
                eng.wait_ge(w_lo_pool, sum(n in BY_POOL for n, _ in CHUNKS[:mine[-1] + 1]))
            else:
                eng.wait_ge(w_lo, sum(n not in BY_POOL + ("dft",) for n, _ in CHUNKS[:mine[-1] + 1]))

        def hi_count(key):
            return sum(n != "dft" for n, _ in CHUNKS[:CHUNK[key] + 1])

        def stage_loaded(eng, key):
            n = CHUNK[key]
            eng.wait_ge(stg_loaded[n % NSTG], 16 * (n // NSTG + 1))

        def stage(key):
            return stg[:, CHUNK[key] % NSTG, :]

        def parts(key):
            name, c = key
            src = stage(key)
            if name == "wkv":
                return (wkv_h[:, 2 * c:2 * c + 2, :], wkv_l[:, 2 * c:2 * c + 2, :],
                        src.rearrange("p (c n) -> p c n", c=2))
            if name == "la":
                return la_h[:, :, :], la_l[:, :, :], src.rearrange("p (c n) -> p c n", c=C)
            if name == "lb":
                return lb_h[:, :], lb_l[0:TOP, :], src
            k = {"wq0": 0, "wk1": 0, "wo": 1, "wq1": 1, "wbase": 1, "w0": 2, "wv1": 2}[name]
            return slot_h[k][:, c, :], slot_l[k][:, c, :], src

        last_reader = {"wk1": ("Q0", PAIRS - 1, 1), "wq1": ("WO", B - 1), "wv1": ("F0", B - 1),
                       "wbase": ("Q1", GROUPS - 1)}

        def passes(eng, dst, left, right, start=True, stop=True):
            eng.matmul(dst, left[0], right[0], start=start, stop=False)
            eng.matmul(dst, left[0], right[1], start=False, stop=False)
            return eng.matmul(dst, left[1], right[0], start=False, stop=stop)

        def project(eng, dst, left, right):
            for c in range(C):
                last = passes(eng, dst, left(c), right(c), start=(c == 0), stop=(c == C - 1))
            return last

        block = always.enter_context(nc.Block())

        @block.sync
        def _(sp):
            def load_ctx(n):
                step = [s for s in CTX if CTX[s] == n][0]
                if n >= 2:
                    filled(sp, [s for s in CTX if CTX[s] == n - 2][0])
                sp.dma_start(ctx_in[:, n % 2, :], ctx[step[2]]).then_inc(ctx_loaded[n % 2], 16)

            def load_chunk(n):
                name, c = CHUNKS[n]
                if n >= NSTG:
                    old = CHUNKS[n - NSTG]
                    if old[0] == "dft":
                        filled(sp, ("WM",))
                    elif old[0] in BY_POOL:
                        sp.wait_ge(w_lo_pool, sum(k in BY_POOL for k, _ in CHUNKS[:n - NSTG + 1]))
                    else:
                        sp.wait_ge(w_lo, sum(k not in BY_POOL + ("dft",) for k, _ in CHUNKS[:n - NSTG + 1]))
                dst = stg[:, n % NSTG, :]
                w = {"wkv": wkv, "wq0": wq0, "wo": wo, "la": la, "lb": lb, "w0": w0, "wk1": wk1, "wq1": wq1,
                     "wv1": wv1, "dft": dft, "wbase": wbase}[name]
                if name == "wkv":
                    src = w.rearrange("(c p) n -> p c n", p=P)[:, 2 * c:2 * c + 2, :]
                    dst = dst.rearrange("p (c n) -> p c n", c=2)
                elif name == "la":
                    src = w.rearrange("(c p) n -> p c n", p=P)
                    dst = dst.rearrange("p (c n) -> p c n", c=C)
                elif name == "lb":
                    src = w
                else:
                    src = w[c * P:(c + 1) * P, :]
                sp.dma_start(dst, src).then_inc(stg_loaded[n % NSTG], 16)

            def load_x(b):
                sp.dma_start(X[:, b, :], x[b]).then_inc(x_loaded[b], 16)

            sp.dma_start(ident[:, :], eye).then_inc(small_loaded, 16)
            load_ctx(0)
            load_chunk(0)
            load_chunk(1)
            load_ctx(1)
            load_x(0)
            load_x(1)
            sp.dma_start(tab[:, :], table).then_inc(small_loaded, 16)
            load_chunk(2)
            load_chunk(3)
            sp.dma_start(starts_i[:, :], starts.partition_broadcast(P)).then_inc(small_loaded, 16)
            sp.dma_start(bias_qk[:, :, :], biases).then_inc(small_loaded, 16)
            for b in range(2, B):
                load_x(b)
            done_chunks, done_ctx, n_w = 4, 2, 0
            for step in ORDER:
                if step[0] == "CT" and done_ctx < len(CTX):
                    load_ctx(done_ctx)
                    done_ctx += 1
                elif step[0] == "W" or step[0] == "WE":
                    n_w += 1
                    while done_chunks < min(n_w + NSTG, len(CHUNKS)) and CHUNKS[done_chunks][0] != "dft":
                        load_chunk(done_chunks)
                        done_chunks += 1
                elif step[0] == "WC":
                    for _ in range(C):
                        load_chunk(done_chunks)
                        done_chunks += 1
                elif step[0] in ("DK", "DQ", "DM"):
                    kind, b = step
                    k = b % 2
                    if b >= 2 and kind != "DM":
                        wide_filled(sp, ("ST", b - 2, 3))
                    if kind == "DK":
                        sp.wait_ge(km_ready, 2 * b + 2)
                    elif kind == "DQ":
                        consumed(sp, ("Q0", b // 2, 0))
                        consumed(sp, ("Q0", b // 2, 1))
                    else:
                        consumed(sp, ("MT", b))
                    for g2 in range(KVH // 2):
                        mine, own = slice(32 * g2, 32 * g2 + 32), slice(2 * g2, 2 * g2 + 2)
                        if kind == "DK":
                            for to, src in ((0, KM_h[mine, k, own, :]), (32, KM_h[mine, k, own, :]),
                                            (64, KM_l[mine, own, :])):
                                sp.dma_start(KS[to:to + 32, k, own, :].bitcast(F32), src.bitcast(F32)).then_inc(ks_loaded[k], 16)
                        elif kind == "DQ":
                            for to, src in ((0, Q_h), (32, Q_l), (64, Q_h)):
                                sp.dma_start(QS[to:to + 32, k, g2, :].bitcast(F32),
                                             src[mine, k, :, :].rearrange("p r q -> p (r q)").bitcast(F32)).then_inc(qs_loaded[k], 16)
                        else:
                            sp.dma_start(QS[LAST:LAST + 2, k, g2, :].bitcast(F32),
                                         negmax[own, k, :].bitcast(F32)).then_inc(max_loaded[k], 16)
                elif step[0] == "PH2":
                    filled(sp, ("OX", B - 1))
                    sp.dma_start(cf[:, :, :, :], coefs).then_inc(late_loaded, 16)
                    sp.dma_start(mk[:, :], masks).then_inc(late_loaded, 16)
                    sp.dma_start(enc_sb[0:ENC, :], enc).then_inc(late_loaded, 16)
                    sp.dma_start(bias_out[:, :], bbase.partition_broadcast(P)).then_inc(late_loaded, 16)
                elif step[0] == "WM":
                    n_w += C
                    while done_chunks < len(CHUNKS):
                        load_chunk(done_chunks)
                        done_chunks += 1
                elif step[0] == "F1":
                    b = step[1]
                    consumed(sp, step)
                    sp.dma_start(out[b], XB[:, b % 2, :]).then_inc(out_stored[b % 2], 16)
                elif step[0] == "V1" and step[1] == 0:
                    filled(sp, step)
                    sp.dma_start(bias_v[:, :], bv1.partition_broadcast(P)).then_inc(bias_v_loaded, 16)
            for k in range(2):
                sp.wait_ge(out_stored[k], 16 * (B // 2))

        @block.tensor
        def _(pe):
            pe.wait_ge(small_loaded, 16 * 4)
            pe.wait_ge(consts_dve, 3)
            pe.wait_ge(consts_pool, 4)
            for step in ORDER:
                kind = step[0]
                if kind == "CT":
                    n = CTX[step]
                    dst = take_bank(pe, step)
                    pe.wait_ge(ctx_loaded[n % 2], 16 * (n // 2 + 1))
                    for c in range(C):
                        last = pe.transpose(dst[:, c * P:(c + 1) * P], ctx_in[:, n % 2, c * P:(c + 1) * P],
                                            ident[:, :])
                    last.then_inc(bank_full, 1)
                elif kind == "XT":
                    layer, b = step[1:]
                    n, k = NORM[("LNs", layer, b)], XN_SLOT[("LNs", layer, b)]
                    dst = take_bank(pe, step)
                    pe.wait_ge(xn_ready, n + 1)
                    for c in range(C):
                        last = pe.transpose(dst[:, c * P:(c + 1) * P], xn[:, k, c * P:(c + 1) * P],
                                            ident[:, :])
                    last.then_inc(bank_full, 1)
                elif kind == "K0":
                    p = step[1]
                    dst = take_bank(pe, step)
                    weight_ready(pe, "wkv")
                    consumed(pe, ("CT", 0, 2 * p))
                    consumed(pe, ("CT", 0, 2 * p + 1))
                    last = project(pe, dst[:, 0:2 * P],
                                   lambda c: (wkv_h[:, c, 0:P], wkv_l[:, c, 0:P]),
                                   lambda c: (ctxT_h[:, c, :, :].rearrange("p b t -> p (b t)"),
                                              ctxT_l[:, c, :, :].rearrange("p b t -> p (b t)")))
                    last.then_inc(bank_full, 1)
                elif kind == "V0":
                    b = step[1]
                    dst = take_bank(pe, step)
                    last = project(pe, dst[:, 0:2 * P],
                                   lambda c: (ctxT_h[:, c, b % 2, :], ctxT_l[:, c, b % 2, :]),
                                   lambda c: (wkv_h[:, c, :], wkv_l[:, c, :]))
                    last.then_inc(bank_full, 1)
                elif kind == "Q0":
                    p, half = step[1:]
                    dst = take_bank(pe, step)
                    weight_ready(pe, "wq0")
                    consumed(pe, ("XT", 0, 2 * p))
                    consumed(pe, ("XT", 0, 2 * p + 1))
                    for k in range(2):
                        r = 2 * half + k
                        last = project(pe, dst[:, k * 2 * P:(k + 1) * 2 * P],
                                       lambda c: (slot_h[0][:, c, r * P:(r + 1) * P],
                                                  slot_l[0][:, c, r * P:(r + 1) * P]),
                                       lambda c: (xT_h[:, c, :, :].rearrange("p b t -> p (b t)"),
                                                  xT_l[:, c, :, :].rearrange("p b t -> p (b t)")))
                    last.then_inc(bank_full, 1)
                elif kind == "MX":
                    b, r = step[1:]
                    p = b // 2
                    dst = take_wide(pe, step)
                    consumed(pe, ("Q0", p, r // 2))
                    pe.wait_ge(km_ready, 2 * b + 2)
                    for k in range(2):
                        last = pe.matmul(dst[:, k, :], Q_h[:, b % 2, r, :],
                                         KM_h[:, b % 2, 4 * k:4 * k + 4, :].rearrange("p g k -> p (g k)"),
                                         start=True, stop=True)
                    last.then_inc(wide_full, 1)
                elif kind == "MT":
                    b = step[1]
                    dst = take_bank(pe, step)
                    wide_consumed(pe, ("MX", b, REP - 1))
                    wide_consumed(pe, ("MX", b, REP - 2))
                    for r in range(REP):
                        last = pe.transpose(dst[0:KVH, r * P:(r + 1) * P], mx[:, b % 2, r, :], ident[:, :])
                    last.then_inc(bank_full, 1)
                elif kind == "ST":
                    b, g2 = step[1:]
                    p = b // 2
                    dst = take_wide(pe, step)
                    pe.wait_ge(ks_loaded[b % 2], 16 * 12 * (b // 2 + 1))
                    pe.wait_ge(qs_loaded[b % 2], 16 * 12 * (b // 2 + 1))
                    pe.wait_ge(max_loaded[b % 2], 16 * 4 * (b // 2 + 1))
                    for k in range(2):
                        last = pe.matmul(dst[:, k, :], KS[:, b % 2, 2 * g2 + k, :], QS[:, b % 2, g2, :],
                                         start=True, stop=True)
                    last.then_inc(wide_full, 1)
                elif kind == "PV":
                    b, gq = step[1:]
                    dst = take_bank(pe, step)
                    consumed(pe, ("V0", b))
                    wide_consumed(pe, ("ST", b, 2 * gq))
                    wide_consumed(pe, ("ST", b, 2 * gq + 1))
                    for j in range(4):
                        n = 4 * b + 2 * gq + j // 2
                        last = pe.matmul(dst[32 * j:32 * j + 32, :], V0[:, b % 4, 4 * gq + j, :],
                                         PT[:, n % 4, (j % 2) * D:(j % 2 + 1) * D], start=True, stop=True)
                    last.then_inc(bank_full, 1)
                elif kind == "OB":
                    b, gq = step[1:]
                    dst = take_bank(pe, step)
                    consumed(pe, ("PV", b, gq))
                    for r in range(REP):
                        last = pe.transpose(dst[:, r * P:(r + 1) * P], OTs[:, gq, r * P:(r + 1) * P],
                                            ident[:, :])
                    last.then_inc(bank_full, 1)
                elif kind == "OX":
                    b = step[1]
                    dst = take_bank(pe, step)
                    consumed(pe, ("OB", b, 0))
                    consumed(pe, ("OB", b, 1))
                    for c in range(C):
                        last = pe.transpose(dst[:, c * P:(c + 1) * P], O[:, c * P:(c + 1) * P],
                                            ident[:, :])
                    last.then_inc(bank_full, 1)
                elif kind == "WO":
                    b = step[1]
                    dst = take_bank(pe, step)
                    weight_ready(pe, "wo")
                    consumed(pe, ("OX", b))
                    last = project(pe, dst, lambda c: (OT_h[:, c, :], OT_l[:, c, :]),
                                   lambda c: (slot_h[1][:, c, :], slot_l[1][:, c, :]))
                    last.then_inc(bank_full, 1)
                elif kind == "LT":
                    p = step[1]
                    dst = take_bank(pe, step)
                    weight_ready(pe, "la")
                    consumed(pe, ("XT", 1, 2 * p))
                    consumed(pe, ("XT", 1, 2 * p + 1))
                    last = project(pe, dst[:, 0:2 * P], lambda c: (la_h[:, c, :], la_l[:, c, :]),
                                   lambda c: (fT_h[:, c, :, :].rearrange("p b t -> p (b t)"),
                                              fT_l[:, c, :, :].rearrange("p b t -> p (b t)")))
                    last.then_inc(bank_full, 1)
                elif kind == "F0":
                    b = step[1]
                    dst = take_bank(pe, step)
                    weight_ready(pe, "w0")
                    consumed(pe, ("LT", b // 2))
                    for c in range(C):
                        passes(pe, dst, (fT_h[:, c, b % 2, :], fT_l[:, c, b % 2, :]),
                               (slot_h[2][:, c, :], slot_l[2][:, c, :]), start=(c == 0), stop=False)
                    pe.matmul(dst, lora_t[:, b % 2, :], lb_h[:, :], start=False, stop=False)
                    pe.matmul(dst, lora_t[:, b % 2, :], lb_l[:, :], start=False, stop=True).then_inc(bank_full, 1)
                elif kind in ("K1", "Q1"):
                    g = step[1]
                    p, c1 = g // C, g % C
                    dst = take_bank(pe, step)
                    src, k = ((ctxT_h, ctxT_l), 0) if kind == "K1" else ((xT_h, xT_l), 1)
                    weight_ready(pe, "wk1" if kind == "K1" else "wq1")
                    for b in (2 * p, 2 * p + 1):
                        consumed(pe, ("CT", 1, b) if kind == "K1" else ("XT", 2, b))
                    last = project(pe, dst[:, 0:2 * P],
                                   lambda c: (slot_h[k][:, c, c1 * P:(c1 + 1) * P],
                                              slot_l[k][:, c, c1 * P:(c1 + 1) * P]),
                                   lambda c: [t[:, c, :, :].rearrange("p b t -> p (b t)") for t in src])
                    last.then_inc(bank_full, 1)
                elif kind == "S1":
                    g = step[1]
                    dst = take_wide(pe, step)
                    consumed(pe, ("K1", g))
                    consumed(pe, ("Q1", g))
                    for b in range(2):
                        last = passes(pe, dst[:, b, :], (K1_h[:, g % 2, b, :], K1_l[:, g % 2, b, :]),
                                      [t[:, g % 2, b, :, :].rearrange("p j q -> p (j q)") for t in (Q1_h, Q1_l)])
                    last.then_inc(wide_full, 1)
                elif kind == "SM":
                    g = step[1]
                    dst = wide(("S1", g))
                    pe.wait_ge(m1_ready, g + 1)
                    for b in range(2):
                        last = pe.matmul(dst[:, b, :], ident_r[:, :],
                                         mneg[:, g, :].unsqueeze(1).broadcast_to([P, JH, P]),
                                         start=False, stop=True, skip_group_check=True)
                    last.then_inc(shifted, 1)
                elif kind == "V1":
                    b = step[1]
                    dst = take_bank(pe, step)
                    weight_ready(pe, "wv1")
                    consumed(pe, ("CT", 2, b))
                    last = project(pe, dst, lambda c: (ctxT_h[:, c, b % 2, :], ctxT_l[:, c, b % 2, :]),
                                   lambda c: (slot_h[2][:, c, :], slot_l[2][:, c, :]))
                    last.then_inc(bank_full, 1)
                elif kind == "PV1":
                    b = step[1]
                    dst = take_bank(pe, step)
                    consumed(pe, ("V1", b))
                    pe.wait_ge(nm_dve, 3 * (b // 2 + 1))
                    pe.wait_ge(nm_pool, b // 2 + 1)
                    for c in range(C):
                        for j in range(JH):
                            h = c * JH + j
                            last = pe.matmul(dst[32 * j:32 * j + 32, c * P:(c + 1) * P],
                                             V1[:, b, h * HD1:(h + 1) * HD1],
                                             P1[:, b // 2 * C + c, (b % 2) * JH + j, :], start=True, stop=True)
                    last.then_inc(bank_full, 1)
                elif kind == "OX1":
                    b = step[1]
                    dst = take_bank(pe, step)
                    consumed(pe, ("PV1", b))
                    for c in range(C):
                        last = pe.transpose(dst[:, c * P:(c + 1) * P], O1T[:, c * P:(c + 1) * P], ident[:, :])
                    last.then_inc(bank_full, 1)
                elif kind == "F1":
                    b = step[1]
                    dst = take_bank(pe, step)
                    weight_ready(pe, "wbase")
                    consumed(pe, ("XT", 3, b))
                    last = project(pe, dst, lambda c: (xT_h[:, c, b % 2, :], xT_l[:, c, b % 2, :]),
                                   lambda c: (slot_h[1][:, c, :], slot_l[1][:, c, :]))
                    last.then_inc(bank_full, 1)
                elif kind == "WM":
                    dst = take_bank(pe, step)
                    pe.wait_ge(cs_step, 3)
                    for c in range(C):
                        stage_loaded(pe, ("dft", c))
                        last = pe.matmul(dst[0:ENC, :], cs[:, c, :], stage(("dft", c)),
                                         start=(c == 0), stop=(c == C - 1))
                    last.then_inc(bank_full, 1)
                elif kind == "WE":
                    c = step[1]
                    dst = take_bank(pe, step)
                    consumed(pe, ("WM",))
                    pe.wait_ge(late_loaded, 64)
                    pe.matmul(dst, enc_sb[0:ENC, c * P:(c + 1) * P], mt[0:ENC, :],
                              start=True, stop=True).then_inc(bank_full, 1)

        @block.scalar
        def _(act):
            act.wait_ge(small_loaded, 16 * 4)
            for step in ORDER:
                kind = step[0]
                if kind == "W":
                    key = step[1:]
                    hi, _, src = parts(key)
                    stage_loaded(act, key)
                    if key[0] in last_reader:
                        filled(act, last_reader[key[0]])
                    act.activation(hi, src, ACT.Copy).then_inc(w_hi, 1)
                elif kind == "WE":
                    key = ("wbase", step[1])
                    hi, _, src = parts(key)
                    consumed(act, step)
                    filled(act, last_reader["wbase"])
                    act.activation(hi, src, ACT.Copy).then_inc(w_hi, 1)
                elif kind == "CT":
                    filled(act, step)
                    act.activation(ctxT_h[:, :, step[2] % 2, :],
                                   bank(step).rearrange("p (c t) -> p c t", c=C), ACT.Copy).then_inc(split_hi, 1)
                elif kind == "XT":
                    filled(act, step)
                    dst = fT_h if step[1] == 1 else xT_h
                    act.activation(dst[:, :, step[2] % 2, :],
                                   bank(step).rearrange("p (c t) -> p c t", c=C), ACT.Copy).then_inc(split_hi, 1)
                elif kind == "K0":
                    p = step[1]
                    filled(act, step)
                    if p >= 2:
                        act.wait_ge(km_ready, 4 * (p - 1))
                    act.activation(K_h[:, p % 2, :, :], bank(step)[:, 0:2 * P].rearrange("p (b t) -> p b t", b=2),
                                   ACT.Copy).then_inc(split_hi, 1)
                elif kind == "V0":
                    b = step[1]
                    filled(act, step)
                    act.wait_ge(consts_pool, 4)
                    act.activation(V0[:, b % 4, :, 0:HD0],
                                   bank(step)[:, P:2 * P].rearrange("p (g d) -> p g d", g=KVH),
                                   ACT.Copy).then_inc(free(step), 1)
                elif kind == "Q0":
                    p, half = step[1:]
                    filled(act, step)
                    if p:
                        for k in range(2):
                            act.wait_ge(qs_loaded[k], 16 * 12 * p)
                    act.activation(Q_h[:, :, 2 * half:2 * half + 2, :],
                                   bank(step).rearrange("p (r b q) -> p b r q", r=2, b=2),
                                   ACT.Copy).then_inc(split_hi, 1)
                elif kind == "ST":
                    b, g2 = step[1:]
                    n = 4 * b + g2
                    wide_filled(act, step)
                    if n >= 4:
                        filled(act, ("PV", (n - 4) // 4, (n - 4) % 4 // 2))
                    act.activation(PT[:, n % 4, :], wide(step).rearrange("p k n -> p (k n)"), ACT.Exp,
                                   scale=SCALE0).then_inc(wide_free[WIDE[step] % 2], 1)
                elif kind == "PV":
                    b, gq = step[1:]
                    filled(act, step)
                    act.activation(OTs[:, gq, :], bank(step), ACT.Copy).then_inc(free(step), 1)
                elif kind == "OX":
                    b = step[1]
                    filled(act, step)
                    act.activation(OT_h[:, :, :], bank(step).rearrange("p (c t) -> p c t", c=C),
                                   ACT.Copy).then_inc(split_hi, 1)
                elif kind == "LT":
                    p = step[1]
                    filled(act, step)
                    act.wait_ge(lora_ready, 5)
                    for k in range(2):
                        b = 2 * p + k
                        last = act.activation(lora_t[:, k, :], bank(step)[:, k * P:(k + 1) * P], ACT.Identity,
                                              scale=use_lora[:, b:b + 1], bias=tab[:, KVH + B + 1:KVH + B + 2])
                    last.then_inc(split_hi, 1)
                elif kind == "K1":
                    g = step[1]
                    filled(act, step)
                    act.activation(K1_h[:, g % 2, :, :], bank(step)[:, 0:2 * P].rearrange("p (b t) -> p b t", b=2),
                                   ACT.Identity, bias=bias_qk[:, 0, g % C:g % C + 1]).then_inc(split_hi, 1)
                elif kind == "Q1":
                    g = step[1]
                    filled(act, step)
                    act.wait_ge(zero_q1, 4)
                    for j in range(JH):
                        rows = slice(j * HD1, (j + 1) * HD1)
                        last = act.activation(Q1_h[rows, g % 2, :, j, :],
                                              bank(step)[rows, 0:2 * P].rearrange("p (b t) -> p b t", b=2),
                                              ACT.Identity, bias=bias_qk[rows, 1, g % C:g % C + 1])
                    last.then_inc(split_hi, 1)
                elif kind == "SM":
                    g = step[1]
                    act.wait_ge(shifted, g + 1)
                    act.activation(P1[:, g, :, :].rearrange("p t q -> p (t q)"),
                                   wide(("S1", g)).rearrange("p k n -> p (k n)"),
                                   ACT.Exp, scale=SCALE1).then_inc(wide_free[WIDE[("S1", g)] % 2], 1)
                elif kind == "FA" and step[1] == 0:
                    act.wait_ge(fac_dve, 2)
                    act.activation(fac[:, :, :], fac[:, :, :], ACT.Exp, scale=SCALE1).then_inc(fac_act, 1)
                elif kind == "PV1":
                    b = step[1]
                    filled(act, step)
                    act.activation(O1T[:, :], bank(step), ACT.Copy).then_inc(free(step), 1)

        @block.vector
        def _(dve):
            dve.wait_ge(small_loaded, 16 * 4)
            dve.tensor_copy(ident_r[:, :], ident[:, :]).then_inc(consts_dve, 1)
            for k in range(2):
                dve.tensor_copy(KS[LAST:P, k, :, :],
                                tab[LAST:P, KVH + B + 2:].unsqueeze(2).broadcast_to([P - LAST, KVH, P])).then_inc(consts_dve, 1)
            dve.tensor_copy(starts_f[:, :], starts_i[:, :]).then_inc(lora_ready, 1)
            dve.wait_ge(lora_ready, 1)
            dve.tensor_tensor(started[:, :, :], starts_f[:, :].unsqueeze(1).broadcast_to([P, B, 4]),
                              tab[:, KVH:KVH + B].unsqueeze(2).broadcast_to([P, B, 4]),
                              ALU.is_le).then_inc(lora_ready, 1)
            dve.wait_ge(lora_ready, 2)
            dve.tensor_reduce(n_started[:, :], started[:, :, :], AX_X, ALU.add).then_inc(lora_ready, 1)
            dve.wait_ge(lora_ready, 3)
            dve.tensor_scalar(use_lora[:, :], n_started[:, :], tab[:, KVH + B:KVH + B + 1], None,
                              ALU.is_equal).then_inc(lora_ready, 1)
            dve.wait_ge(lora_ready, 4)
            dve.memset(lb_l[TOP:P, :].bitcast(F32), 0.0).then_inc(lora_ready, 1)
            for step in ORDER:
                kind = step[0]
                if kind == "W" and step[1] not in BY_POOL:
                    key = step[1:]
                    hi, lo, src = parts(key)
                    if key[0] == "lb":
                        hi, src = hi[0:TOP, :], src[0:TOP, :]
                    dve.wait_ge(w_hi, hi_count(key))
                    dve.tensor_tensor(lo, src, hi.bitcast(F32), ALU.subtract).then_inc(w_lo, 1)
                elif kind == "WE":
                    key = ("wbase", step[1])
                    filled(dve, step)
                    stage_loaded(dve, key)
                    hi, lo, src = parts(key)
                    dve.tensor_tensor(src, bank(step), src, ALU.add).then_inc(free(step), 1)
                    dve.wait_ge(w_hi, hi_count(key))
                    dve.tensor_tensor(lo, src, hi.bitcast(F32), ALU.subtract).then_inc(w_lo, 1)
                elif kind == "LNs":
                    layer, b = step[1:]
                    n = NORM[step]
                    if layer == 0:
                        dve.wait_ge(x_loaded[b], 16)
                    else:
                        consumed(dve, [None, ("WO", b), ("F0", b), ("OX1", b)][layer])
                    if n >= 4:
                        dve.wait_ge(rstd_ready, n - 3)
                    dve.bn_stats(stats[:, n % 4, :], X[:, b, :]).then_inc(stat_done, 1)
                    dve.wait_ge(stat_done, n + 1)
                    dve.bn_aggr(moments[:, n % 4, :], stats[:, n % 4, :]).then_inc(moments_ready, 1)
                elif kind == "LNn":
                    layer, b = step[1:]
                    n = NORM[("LNs", layer, b)]
                    old = earlier_norm(("LNs", layer, b))
                    if old:
                        filled(dve, ("XT",) + old[1:])
                    dve.wait_ge(rstd_ready, n + 1)
                    dve.tensor_scalar(xn[:, XN_SLOT[("LNs", layer, b)], :], X[:, b, :], moments[:, n % 4, 0:1], rstd[:, n % 4, 0:1],
                                      ALU.subtract, ALU.mult).then_inc(xn_ready, 1)
                elif kind in ("CT", "XT", "OX"):
                    hi_written(dve, step)
                    if kind == "OX":
                        lo, hi = [t[:, :, :] for t in (OT_l, OT_h)]
                    else:
                        ts = (ctxT_l, ctxT_h) if kind == "CT" else (fT_l, fT_h) if step[1] == 1 else (xT_l, xT_h)
                        lo, hi = [t[:, :, step[2] % 2, :] for t in ts]
                    dve.tensor_tensor(lo, bank(step).rearrange("p (c t) -> p c t", c=C), hi.bitcast(F32),
                                      ALU.subtract).then_inc(free(step), 1)
                elif kind == "K0":
                    p = step[1]
                    hi_written(dve, step)
                    dve.tensor_tensor(K_l[:, p % 2, :, :], bank(step)[:, 0:2 * P].rearrange("p (b t) -> p b t", b=2),
                                      K_h[:, p % 2, :, :].bitcast(F32), ALU.subtract).then_inc(free(step), 1)
                elif kind == "Q0":
                    p, half = step[1:]
                    rs = slice(2 * half, 2 * half + 2)
                    hi_written(dve, step)
                    dve.tensor_tensor(Q_l[:, :, rs, :], bank(step).rearrange("p (r b q) -> p b r q", r=2, b=2),
                                      Q_h[:, :, rs, :].bitcast(F32), ALU.subtract).then_inc(free(step), 1)
                elif kind == "MX":
                    b, r = step[1:]
                    wide_filled(dve, step)
                    dve.tensor_reduce(mx[:, b % 2, r, :], wide(step).rearrange("p k (g t) -> p (k g) t", g=4),
                                      AX_X, ALU.max).then_inc(wide_free[WIDE[step] % 2], 1)
                elif kind == "MT":
                    b = step[1]
                    filled(dve, step)
                    if b >= 2:
                        dve.wait_ge(max_loaded[b % 2], 16 * 4 * (b // 2))
                    dve.tensor_scalar(negmax[0:KVH, b % 2, :], bank(step)[0:KVH, :], -1.0, None,
                                      ALU.mult).then_inc(free(step), 1)
                elif kind == "OB":
                    b, gq = step[1:]
                    filled(dve, step)
                    src = bank(step).rearrange("p (r j e) -> p r j e", r=REP, j=4)
                    dve.reciprocal(rec[:, gq, :, :], src[:, :, :, HD0]).then_inc(rec_ready, 1)
                    dve.wait_ge(rec_ready, 2 * b + gq + 1)
                    dst = O[:, :].rearrange("p (g r d) -> p r g d", g=KVH, r=REP)[:, :, 4 * gq:4 * gq + 4, :]
                    dve.tensor_tensor(dst, src[:, :, :, 0:HD0],
                                      rec[:, gq, :, :].unsqueeze(3).broadcast_to([P, REP, 4, HD0]),
                                      ALU.mult).then_inc(free(step), 1)
                elif kind in ("WO", "F0"):
                    b = step[1]
                    filled(dve, step)
                    dve.tensor_tensor(X[:, b, :], bank(step), X[:, b, :], ALU.add).then_inc(free(step), 1)
                elif kind == "LT":
                    p = step[1]
                    hi_written(dve, step)
                    for k in range(2):
                        b = 2 * p + k
                        last = dve.scalar_tensor_tensor(
                            out=lora_t[TOP:P, k, :], in0=bank(step)[TOP:P, k * P:(k + 1) * P],
                            scalar=use_lora[TOP:P, b:b + 1], in1=lora_t[TOP:P, k, :].bitcast(F32),
                            op0=ALU.mult, op1=ALU.subtract)
                    last.then_inc(free(step), 1)
                elif kind == "K1":
                    g = step[1]
                    hi_written(dve, step)
                    dve.scalar_tensor_tensor(
                        out=K1_l[:, g % 2, :, :], in0=bank(step)[:, 0:2 * P].rearrange("p (b t) -> p b t", b=2),
                        scalar=bias_qk[:, 0, g % C:g % C + 1], in1=K1_h[:, g % 2, :, :].bitcast(F32),
                        op0=ALU.add, op1=ALU.subtract).then_inc(free(step), 1)
                elif kind == "Q1":
                    g = step[1]
                    hi_written(dve, step)
                    dve.wait_ge(zero_q1, 4)
                    for j in range(JH):
                        rows = slice(j * HD1, (j + 1) * HD1)
                        last = dve.scalar_tensor_tensor(
                            out=Q1_l[rows, g % 2, :, j, :],
                            in0=bank(step)[rows, 0:2 * P].rearrange("p (b t) -> p b t", b=2),
                            scalar=bias_qk[rows, 1, g % C:g % C + 1], in1=Q1_h[rows, g % 2, :, j, :].bitcast(F32),
                            op0=ALU.add, op1=ALU.subtract)
                    last.then_inc(free(step), 1)
                elif kind == "S1":
                    g = step[1]
                    wide_filled(dve, step)
                    dve.tensor_reduce(mneg[:, g, :], wide(step).rearrange("p k (j q) -> p q (k j)", j=JH),
                                      AX_X, ALU.max, negate=True).then_inc(m1_ready, 1)
                elif kind == "FA" and step[1] == 0:
                    dve.wait_ge(m1_ready, GROUPS)
                    neg = mneg[:, :, :].bitcast(F32)
                    dve.tensor_reduce(nmin[:, :], neg.rearrange("p g q -> p q g"), AX_X, ALU.min).then_inc(fac_dve, 1)
                    dve.wait_ge(fac_dve, 1)
                    dve.tensor_tensor(fac[:, :, :], nmin[:, :].unsqueeze(1).broadcast_to([P, GROUPS, P]), neg,
                                      ALU.subtract).then_inc(fac_dve, 1)
                elif kind == "FA":
                    dve.wait_ge(z_ready, 3 * GROUPS)
                    dve.wait_ge(fac_act, 1)
                    dve.tensor_tensor(Z[:, :, :], Z[:, :, :], fac[:, :, :], ALU.mult).then_inc(fac_dve, 1)
                    dve.wait_ge(fac_dve, 3)
                    dve.tensor_reduce(nmin[:, :], Z[:, :, :].rearrange("p g q -> p q g"), AX_X,
                                      ALU.add).then_inc(fac_dve, 1)
                    dve.wait_ge(fac_dve, 4)
                    dve.reciprocal(nmin[:, :], nmin[:, :]).then_inc(fac_dve, 1)
                    dve.wait_ge(fac_dve, 5)
                    dve.tensor_tensor(fac[:, :, :], fac[:, :, :], nmin[:, :].unsqueeze(1).broadcast_to([P, GROUPS, P]),
                                      ALU.mult).then_inc(fac_dve, 1)
                elif kind == "NM" and step[1] % C != C - 1:
                    g = step[1]
                    dve.wait_ge(fac_dve, 6)
                    dve.tensor_tensor(P1[:, g, :, :], P1[:, g, :, :],
                                      fac[:, g, :].unsqueeze(1).broadcast_to([P, T, P]),
                                      ALU.mult).then_inc(nm_dve, 1)
                elif kind == "V1":
                    b = step[1]
                    filled(dve, step)
                    dve.wait_ge(bias_v_loaded, 16)
                    dve.tensor_tensor(V1[:, b, :], bank(step), bias_v[:, :], ALU.add).then_inc(free(step), 1)
                elif kind == "OX1":
                    b = step[1]
                    filled(dve, step)
                    dst = X[:, b, :].rearrange("p (d h) -> p h d", h=H1)
                    dve.tensor_tensor(dst, bank(step).rearrange("p (h d) -> p h d", h=H1), dst,
                                      ALU.add).then_inc(free(step), 1)
                elif kind == "F1":
                    b = step[1]
                    filled(dve, step)
                    dve.wait_ge(xb_ready, b + 1)
                    dve.tensor_tensor(XB[:, b % 2, :], bank(step), XB[:, b % 2, :], ALU.add).then_inc(free(step), 1)
                elif kind == "WC":
                    dve.wait_ge(late_loaded, 64)
                    dve.tensor_tensor(cf[:, :, :, :], cf[:, :, :, :],
                                      mk[:, :].bitcast(U8).rearrange("p (c e r) -> p c e r", c=C, e=EXP),
                                      ALU.mult).then_inc(cs_step, 1)
                    dve.wait_ge(cs_step, 1)
                    dve.tensor_tensor(cs[:, :, :], cf[:, :, 0, :], cf[:, :, 1, :], ALU.add).then_inc(cs_step, 1)
                    dve.wait_ge(cs_step, 2)
                    dve.tensor_tensor(cs[:, :, :], cs[:, :, :], cf[:, :, 2, :], ALU.add).then_inc(cs_step, 1)
                elif kind == "WM":
                    filled(dve, step)
                    consumed(dve, ("F0", B - 1))
                    dve.tensor_copy(mt[0:ENC, :], bank(step)[0:ENC, :]).then_inc(free(step), 1)

        @block.gpsimd
        def _(pool):
            pool.memset(minus_half[:, :], -0.5).then_inc(consts_pool, 1)
            pool.memset(V0[:, :, :, :], 0.0).then_inc(consts_pool, 1)
            pool.wait_ge(consts_pool, 2)
            pool.memset(V0[:, :, :, HD0:HD0 + 1], 1.0).then_inc(consts_pool, 1)
            pool.wait_ge(consts_pool, 3)
            pool.memset(QS[LAST:P, :, :, :].bitcast(F32), 0.0).then_inc(consts_pool, 1)
            pool.wait_ge(consts_pool, 4)
            pool.wait_ge(small_loaded, 16 * 4)
            for step in ORDER:
                kind = step[0]
                if kind == "W" and step[1] in BY_POOL:
                    key = step[1:]
                    hi, lo, src = parts(key)
                    pool.wait_ge(w_hi, hi_count(key))
                    pool.tensor_tensor(lo, src, hi.bitcast(F32), ALU.subtract).then_inc(w_lo_pool, 1)
                elif kind == "LNs":
                    n = NORM[step]
                    pool.wait_ge(moments_ready, n + 1)
                    if n >= 4:
                        pool.wait_ge(xn_ready, n - 3)
                    pool.tensor_scalar(var_eps[:, n % 4, :], moments[:, n % 4, 1:2], EPS, None,
                                       ALU.add).then_inc(eps_done, 1)
                    pool.wait_ge(eps_done, n + 1)
                    pool.tensor_tensor(rstd[:, n % 4, :], var_eps[:, n % 4, :], minus_half[:, :],
                                       ALU.pow).then_inc(rstd_ready, 1)
                elif kind == "KM":
                    b = step[1]
                    consumed(pool, ("K0", b // 2))
                    if b:
                        pool.wait_ge(ks_loaded[(b - 1) % 2], 16 * 12 * ((b - 1) // 2 + 1))
                    if b >= 2:
                        pool.wait_ge(ks_loaded[b % 2], 16 * 12 * (b // 2))
                        wide_consumed(pool, ("MX", b - 2, REP - 1))
                    own = tab[:, 0:KVH].unsqueeze(2).broadcast_to([P, KVH, P])
                    for src, dst in ((K_h, KM_h[:, b % 2, :, :]), (K_l, KM_l[:, :, :])):
                        pool.tensor_tensor(dst,
                                           src[:, b // 2 % 2, b % 2, :].bitcast(F32).unsqueeze(1).broadcast_to([P, KVH, P]),
                                           own, ALU.mult).then_inc(km_ready, 1)
                elif kind == "SM":
                    g = step[1]
                    wide_consumed(pool, ("S1", g))
                    if g:
                        pool.wait_ge(z_ready, 3 * g)
                    pool.tensor_tensor(zpart[:, :, :], P1[:, g, 0:JH, :], P1[:, g, JH:T, :],
                                       ALU.add).then_inc(z_ready, 1)
                    pool.wait_ge(z_ready, 3 * g + 1)
                    pool.tensor_tensor(zpart[:, 0:2, :], zpart[:, 0:2, :], zpart[:, 2:4, :],
                                       ALU.add).then_inc(z_ready, 1)
                    pool.wait_ge(z_ready, 3 * g + 2)
                    pool.tensor_tensor(Z[:, g, :], zpart[:, 0, :], zpart[:, 1, :], ALU.add).then_inc(z_ready, 1)
                elif kind == "PH2":
                    filled(pool, ("OX", B - 1))
                    for t in (Q1_h, Q1_l):
                        for k in range(2):
                            pool.memset(t[:, k, :, :, :].bitcast(F32), 0.0).then_inc(zero_q1, 1)
                elif kind == "NM" and step[1] % C == C - 1:
                    g = step[1]
                    pool.wait_ge(fac_dve, 6)
                    pool.tensor_tensor(P1[:, g, :, :], P1[:, g, :, :],
                                       fac[:, g, :].unsqueeze(1).broadcast_to([P, T, P]),
                                       ALU.mult).then_inc(nm_pool, 1)
                elif kind == "OX1":
                    b = step[1]
                    consumed(pool, step)
                    pool.wait_ge(late_loaded, 64)
                    if b >= 2:
                        pool.wait_ge(out_stored[b % 2], 16 * (b // 2))
                    pool.tensor_tensor(XB[:, b % 2, :], X[:, b, :], bias_out[:, :], ALU.add).then_inc(xb_ready, 1)


def kernel(**inputs):
    import numpy as np
    import concourse.bacc as bacc
    from concourse import mybir as _mybir
    from concourse.bass_utils import run_bass_kernel_spmd as run

    a = {k: np.asarray(v) for k, v in inputs.items()}
    f = np.float32
    wq0 = a["L0_xattn_Wq"].reshape(D, KVH, REP, HD0).transpose(0, 2, 1, 3).reshape(D, D)
    lora_a = a["L0_ffn_lora_A"].reshape(RANK, D).T
    la = np.zeros((D, P), f)
    la[:, 0:RANK] = lora_a
    la[:, TOP:TOP + RANK] = lora_a
    lora_b = a["L0_ffn_lora_B"].transpose(0, 2, 1).reshape(RANK, D)
    lb = np.zeros((P, D), f)
    lb[0:RANK] = lora_b
    lb[RANK] = a["L0_ffn_bias"]
    lb[TOP:TOP + RANK] = lora_b
    packed = lambda u, v: np.concatenate([u, v], axis=2).reshape(EXP, C, P, ENC).transpose(2, 1, 0, 3)
    n = np.arange(D)
    k = np.arange(1, (D - 1) // 2 + 1)[:, None]
    dft = np.zeros((D, D))
    dft[0] = D ** -0.5
    dft[1:D - 1:2] = np.sqrt(2.0 / D) * np.cos(2 * np.pi * (k * n % D) / D)
    dft[2:D:2][:len(k)] = np.sqrt(2.0 / D) * np.sin(2 * np.pi * (k * n % D) / D)
    dft[D - 1] = np.where(n % 2 == 0, 1.0, -1.0) * D ** -0.5
    dft = (0.5 * dft).astype(f)
    row = np.arange(P)
    table = np.zeros((P, KVH + B + 2 + KVH), f)
    table[:, 0:KVH] = row[:, None] // HD0 == np.arange(KVH)[None]
    table[:, KVH:KVH + B] = np.arange(B)[None]
    table[:, KVH + B] = np.where(row % TOP < RANK, row % TOP // 16 + 2, -1)
    table[:, KVH + B + 1] = row == RANK
    table[:, KVH + B + 2:] = row[:, None] == LAST + np.arange(KVH)[None] % 2
    arrays = {
        "x": a["x"], "ctx": a["ctx_4096"],
        "wkv": np.concatenate([a["L0_xattn_Wk"], a["L0_xattn_Wv"]], axis=1), "wq0": wq0,
        "wo": a["L0_xattn_Wo"], "la": la, "lb": lb, "w0": a["L0_ffn_weight"].T,
        "starts": a["L0_ffn_lora_start_indices"],
        "wk1": a["L1_xattn_Wk"].T, "wq1": a["L1_xattn_Wq"].T, "wv1": a["L1_xattn_Wv"].T,
        "biases": np.stack([a["L1_xattn_bk"], a["L1_xattn_bq"]]).reshape(2, C, P).transpose(2, 0, 1),
        "bv1": a["L1_xattn_bv"],
        "wbase": a["L1_ffn_W_base"].T, "bbase": a["L1_ffn_b_base"],
        "enc": np.concatenate([a["L1_ffn_enc0"], a["L1_ffn_enc1"]], axis=0),
        "coefs": packed(a["L1_ffn_coefs0"], a["L1_ffn_coefs1"]),
        "masks": packed(a["L1_ffn_mask0"], a["L1_ffn_mask1"]).reshape(P, -1).view(np.int32),
        "dft": dft, "eye": np.eye(P, dtype=f), "table": table,
    }
    nc = bacc.Bacc("TRN2", target_bir_lowering=False, num_devices=1)
    feeds, args = {}, []
    for name, v in arrays.items():
        v = np.ascontiguousarray(v)
        feeds[f"in_{name}"] = v
        args.append(nc.dram_tensor(f"in_{name}", v.shape, _mybir.dt.from_np(v.dtype), kind="ExternalInput").ap())
    args.append(nc.dram_tensor("out_0", (B, S, D), F32, kind="ExternalOutput").ap())
    build(nc, *args)
    r = run(nc, [feeds], core_ids=[0])
    return r.results[0]["out_0"]
```

```python
from contextlib import ExitStack

import concourse.bass as bass
from concourse import mybir

F32 = mybir.dt.float32
F32R = mybir.dt.float32r
U8 = mybir.dt.uint8
I32 = mybir.dt.int32
ALU = mybir.AluOpType
ACT = mybir.ActivationFunctionType
AX_X = mybir.AxisListType.X

B, S, D = 8, 128, 512
P = 128
C = D // P
PAIRS = B // 2
KVH, REP, HD0 = 8, 4, 16
H1, HD1 = 16, 32
JH = P // HD1
GROUPS = PAIRS * C
T = 2 * JH
RANK = 48
TOP = 64
LAST = 96
ENC = 40
EXP = 3
EPS = 1e-5
SCALE0 = HD0 ** -0.5
SCALE1 = HD1 ** -0.5
NG = 4
NSTG = 4

CHUNKS = ([("wkv", 0), ("wkv", 1)] + [("wq0", c) for c in range(C)] + [("wo", c) for c in range(C)]
          + [("la", 0), ("lb", 0)] + [("w0", c) for c in range(C)]
          + [("wk1", c) for c in range(C)] + [("wq1", c) for c in range(C)]
          + [("wv1", c) for c in range(C)] + [("dft", c) for c in range(C)]
          + [("wbase", c) for c in range(C)])
CHUNK = {key: n for n, key in enumerate(CHUNKS)}
BY_POOL = ("wk1", "wq1", "wv1", "wbase")


EVEN = [
    ("LNs", 0, 2), ("MX", 1, 0), ("OB", -1, 0), ("OB", -1, 1), ("MX", 1, 1), ("CT", 0, 2), ("ST", 0, 0),
    ("XT", 1, -2), ("LNn", 0, 2), ("OX", -1), ("CT", 0, 3), ("LNs", 0, 3), ("ST", 0, 1), ("MX", 1, 2),
    ("LNn", 0, 3), ("MX", 1, 3), ("WO", -1), ("LNs", 1, -1), ("V0", 2), ("XT", 0, 2), ("MT", 1), ("ST", 0, 2),
    ("XT", 0, 3), ("ST", 0, 3), ("V0", 3), ("PV", 0, 0), ("LNn", 1, -1), ("K0", 1), ("DM", 1), ("KM", 2), ("KS", 1),
    ("Q0", 1, 0), ("KL", 1), ("KX", 2), ("Q0", 1, 1), ("QS", 1), ("QL", 2), ("PV", 0, 1)
]
ODD = [
    ("OB", -1, 0), ("MX", 1, 0), ("XT", 1, -2), ("OB", -1, 1), ("MX", 1, 1), ("DM", 1), ("MX", 1, 3), ("OX", -1),
    ("LT", -1), ("ST", 0, 0), ("MX", 1, 2), ("KM", 2), ("WO", -1), ("ST", 0, 1), ("ST", 0, 2), ("MT", 1),
    ("F0", -3), ("KX", 2), ("LNs", 1, -1), ("ST", 0, 3), ("F0", -2), ("LNn", 1, -1), ("PV", 0, 0), ("QL", 2),
    ("PV", 0, 1)
]
EXTRA = {
    (0, 0): [
        ("W", "wo", 0), ("W", "wo", 1)],
    (0, 18): [
        ("W", "wo", 2)],
    (1, 3): [
        ("W", "wo", 3)],
    (1, 9): [
        ("W", "la", 0)],
    (1, 21): [
        ("W", "lb", 0)],
    (2, 34): [
        ("W", "w0", 0), ("W", "w0", 1), ("W", "w0", 2), ("W", "w0", 3)],
    (6, 7): [
        ("LNs", 2, 0), ("LNs", 2, 1), ("LNn", 2, 0), ("LNn", 2, 1)],
    (6, 9): [
        ("CT", 1, 0)],
    (6, 15): [
        ("XT", 2, 0), ("CT", 1, 1), ("XT", 2, 1), ("W", "wk1", 0), ("W", "wk1", 1), ("W", "wk1", 2),
        ("W", "wk1", 3)],
}
START = [
    ("CT", 0, 0), ("W", "wkv", 0), ("LNs", 0, 0), ("W", "wkv", 1), ("CT", 0, 1), ("LNs", 0, 1), ("LNn", 0, 0),
    ("V0", 0), ("LNn", 0, 1), ("XT", 0, 0), ("V0", 1), ("W", "wq0", 0), ("XT", 0, 1), ("K0", 0), ("W", "wq0", 1),
    ("KS", 0), ("W", "wq0", 2), ("W", "wq0", 3), ("Q0", 0, 1), ("C0",), ("KM", 0), ("Q0", 0, 0), ("KL", 0),
    ("MX", 0, 2), ("KX", 1), ("QS", 0), ("KX", 0), ("MX", 0, 1), ("MX", 0, 3), ("MX", 0, 0), ("QL", 0), ("MT", 0),
    ("DM", 0), ("KM", 1), ("QL", 1)
]
MIDDLE = [
    ("PH2",), ("OB", 7, 0), ("OB", 7, 1), ("OX", 7), ("K1", 0), ("W", "wq1", 0), ("W", "wq1", 1), ("WO", 7),
    ("W", "wq1", 2), ("LNs", 1, 7), ("K1", 1), ("W", "wq1", 3), ("LNn", 1, 7), ("XT", 1, 6), ("XT", 1, 7),
    ("Q1", 0), ("LT", 3), ("Q1", 1), ("F0", 7), ("F0", 6)
]
CYCLE = [
    ("S1", 0), ("LNs", 2, 3), ("LNs", 2, 2), ("K1", 2), ("S1", 1), ("LNn", 2, 2), ("LNn", 2, 3), ("K1", 3),
    ("SM", 0), ("CT", 1, 3), ("Q1", 2), ("Q1", 3), ("XT", 2, 2), ("XT", 2, 3), ("CT", 1, 2), ("SM", 1), ("S1", 2),
    ("S1", 3), ("Q1", 4), ("K1", 4), ("SM", 2), ("Q1", 5), ("K1", 5), ("SM", 3)
]
CYCLE_EXTRA = {
    (0, 3): [
        ("W", "wv1", 0)],
    (0, 5): [
        ("W", "wv1", 1)],
    (0, 17): [
        ("W", "wv1", 2), ("W", "wv1", 3), ("WC",)],
    (2, 10): [
        ("WM",)],
}
CYCLES = 3
VALUES = [
    ("S1", 12), ("Q1", 14), ("SM", 12), ("S1", 13), ("K1", 14), ("Q1", 15), ("SM", 13), ("S1", 14), ("K1", 15),
    ("CT", 2, 0), ("SM", 14), ("S1", 15), ("SM", 15), ("V1", 0), ("CT", 2, 1), ("FA", 0), ("CT", 2, 2), ("V1", 1),
    ("CT", 2, 3), ("V1", 2), ("CT", 2, 4), ("FA", 1), ("FA", 2), ("V1", 3), ("V1", 4), ("FA", 3), ("CT", 2, 5),
    ("CT", 2, 6), ("WE", 0), ("FA", 4), ("NM", 3), ("V1", 5), ("NM", 2), ("NM", 1), ("WE", 1), ("CT", 2, 7),
    ("WE", 3), ("WE", 2), ("V1", 6), ("NM", 0), ("V1", 7)
]
LAST_EVEN = [
    ("F1", -1), ("NM", 8), ("XT", 3, 0), ("OX1", 1), ("LNs", 3, 1), ("PV1", 2), ("NM", 9), ("LNn", 3, 1)
]
LAST_ODD = [
    ("F1", -1), ("OX1", 1), ("LNs", 3, 1), ("XT", 3, 0), ("NM", 10), ("PV1", 2), ("NM", 11), ("LNn", 3, 1)
]


def plan():
    order = list(START)

    def place(step, b):
        kind = step[0]
        base = {"K0": b // 2, "KS": b // 2, "KL": b // 2, "Q0": b // 2, "QS": b // 2, "LT": b // 2, "S1": 2 * b, "SM": 2 * b, "K1": 2 * b, "Q1": 2 * b,
                "NM": 2 * (b - b % 2)}.get(kind, b)
        count = PAIRS if kind in ("K0", "KS", "KL", "Q0", "QS", "LT") else GROUPS if kind in ("S1", "SM", "K1", "Q1", "NM") else B
        at = 2 if kind in ("LNs", "LNn", "XT", "CT") else 1
        k = base + step[at]
        step = step[:at] + (k,) + step[at + 1:]
        return [step] if 0 <= k < count and step not in order else []

    for b in range(B):
        for n, step in enumerate(EVEN if b % 2 == 0 else ODD):
            order += EXTRA.get((b, n), []) + place(step, b)
    order += MIDDLE
    for p in range(CYCLES):
        for n, step in enumerate(CYCLE):
            order += CYCLE_EXTRA.get((p, n), []) + place(step, 2 * p)
    order += VALUES
    for b in range(-2, B + 2):
        for step in LAST_EVEN if b % 2 == 0 else LAST_ODD:
            order += place(step, b)
    return order


ORDER = plan()
BANK_STEPS = ("K0", "V0", "XT", "Q0", "MT", "PV", "OB", "OX", "WO", "LT", "F0", "K1", "Q1", "V1",
              "PV1", "OX1", "F1", "WM", "WE")
SPLIT_STEPS = ("CT", "K0", "XT", "Q0", "OX", "LT", "K1", "Q1")


def numbered(kinds):
    return {step: n for n, step in enumerate(s for s in ORDER if s[0] in kinds)}


BANK = numbered(BANK_STEPS)
WIDE = numbered(("MX", "ST", "S1"))
SPLIT = numbered(SPLIT_STEPS)
NORM = numbered(("LNs",))
NORMED = numbered(("LNn",))


def turn_of(turns, n):
    return list(turns)[n]


CTX = numbered(("CT",))
CT_BY_POOL = [s for s in CTX if s[1] > 0]


def previous_ctx(step):
    same = [s for s in CTX if CTX[s] < CTX[step] and s[2] % 2 == step[2] % 2]
    return same[-1] if same else None


def build(nc, x, ctx, wkv, wq0, wo, la, lb, w0, starts, wk1, wq1, wv1, biases, bv1, wbase, bbase, enc,
          coefs, masks, dft, eye, table, out):
    with ExitStack() as always:
        def sb(name, shape, dt=F32, where=always):
            return where.enter_context(nc.sbuf_tensor(name, [P] + list(shape), dt))

        def sem(name):
            return always.enter_context(nc.semaphore(name))

        X = sb("X", [B, D])
        slot_h = [None] + [sb(f"slot{k}_h", [C, D], F32R) for k in (1, 2)]
        slot_l = [None] + [sb(f"slot{k}_l", [C, D], F32R) for k in (1, 2)]
        stg = sb("stg", [NSTG, D])
        ident = sb("ident", [P])
        ident_r = sb("ident_r", [P], F32R)
        ctx_in = sb("ctx_in", [2, D])
        ctxT_h, ctxT_l = sb("ctxT_h", [C, 2, P], F32R), sb("ctxT_l", [C, 2, P], F32R)
        xT_h, xT_l = sb("xT_h", [C, 2, P], F32R), sb("xT_l", [C, 2, P], F32R)
        xn = sb("xn", [2, D])
        stats = sb("stats", [4, 6])
        moments = sb("moments", [4, 2])
        var_eps = sb("var_eps", [4, 1])
        rstd = sb("rstd", [4, 1])
        minus_half = sb("minus_half", [1])
        bias_qk = sb("bias_qk", [2, C])
        with ExitStack() as short:
            slot_h[0] = sb("slot0_h", [C, D], F32R, short)
            slot_l[0] = sb("slot0_l", [C, D], F32R, short)
        V1 = sb("V1", [B, D])
        with ExitStack() as first:
            def s1(name, shape, dt=F32):
                return sb(name, shape, dt, first)
            wkv_h, wkv_l = s1("wkv_h", [C, 256], F32R), s1("wkv_l", [C, 256], F32R)
            KM_h = s1("KM_h", [2, KVH, P], F32R)
            K_raw = s1("K_raw", [2, P])
            KR = s1("KR", [KVH // 2, 2, P])
            K_h, K_l = s1("K_h", [2, 2, P], F32R), s1("K_l", [2, 2, P], F32R)
            V0 = s1("V0", [4, KVH, 32])
            la_h, la_l = s1("la_h", [C, P], F32R), s1("la_l", [C, P], F32R)
            lb_h, lb_l = s1("lb_h", [D], F32R), s1("lb_l", [D], F32R)
            fT_h, fT_l = s1("fT_h", [C, 2, P], F32R), s1("fT_l", [C, 2, P], F32R)
            lora_t = s1("lora_t", [2, P], F32R)
            OT_h, OT_l = s1("OT_h", [C, P], F32R), s1("OT_l", [C, P], F32R)
            starts_i = s1("starts_i", [4], I32)
            starts_f = s1("starts_f", [4])
            started = s1("started", [B, 4])
            n_started = s1("n_started", [B])
            use_lora = s1("use_lora", [B])
            tab = s1("tab", [KVH + B + 2 + KVH + 2])
            Q_h, Q_l = s1("Q_h", [2, REP, P], F32R), s1("Q_l", [2, REP, P], F32R)
            QS, KS = s1("QS", [2, KVH // 2, D], F32R), s1("KS", [2, KVH, P], F32R)
            mx = s1("mx", [2, REP, KVH])
            negmax = s1("negmax", [2, D], F32R)
            PT = s1("PT", [4, 2 * D])
            OTs = s1("OTs", [2, D])
            rec = s1("rec", [2, REP, 4])
            O = s1("O", [D])
        with ExitStack() as second:
            def s2(name, shape, dt=F32):
                return sb(name, shape, dt, second)
            P1 = s2("P1", [GROUPS, T, P])
            K1_h, K1_l = s2("K1_h", [2, 2, P], F32R), s2("K1_l", [2, 2, P], F32R)
            Q1_h, Q1_l = s2("Q1_h", [2, 2, JH, P], F32R), s2("Q1_l", [2, 2, JH, P], F32R)
            mneg = s2("mneg", [GROUPS, P], F32R)
            Z = s2("Z", [GROUPS, P])
            enc_sb = s2("enc_sb", [D])
            mt = s2("mt", [D])
            bias_out = s2("bias_out", [D])
            nmin = s2("nmin", [P])
            zpart = s2("zpart", [JH, P])
            bias_v = s2("bias_v", [D])
        with ExitStack() as early:
            sb("under_early", [(GROUPS - 1) * T * P], F32, early)
            cf = sb("cf", [C, EXP, ENC], F32, early)
            mk = sb("mk", [C * EXP * ENC // 4], I32, early)
            cs = sb("cs", [C, ENC], F32, early)
        with ExitStack() as third:
            sb("under_third", [GROUPS * T * P], F32, third)
            fac = sb("fac", [GROUPS, P], F32, third)
            zsum = sb("zsum", [P], F32, third)
            O1T = sb("O1T", [2, D], F32, third)
            XB = sb("XB", [2, D], F32, third)
        ps = always.enter_context(nc.psum_tensor("ps", [P, 8, D], F32))
        k_dram = [nc.dram_tensor(f"k_dram{p}", [2, P, 2 * P], F32).ap() for p in range(PAIRS)]
        q_dram = [nc.dram_tensor(f"q_dram{p}", [2, P, 2, REP * P], F32).ap() for p in range(PAIRS)]
        max_dram = [nc.dram_tensor(f"max_dram{b}", [KVH, D], F32).ap() for b in range(B)]

        x_loaded = [sem(f"x_loaded{b}") for b in range(B)]
        ctx_loaded = [sem(f"ctx_loaded{k}") for k in range(2)]
        stg_loaded = [sem(f"stg_loaded{k}") for k in range(NSTG)]
        ident_loaded = sem("ident_loaded")
        small_loaded = sem("small_loaded")
        late_loaded = sem("late_loaded")
        out_stored = [sem(f"out_stored{k}") for k in range(2)]
        bank_full = sem("bank_full")
        bank_free = [sem(f"bank_free{k}") for k in range(NG)]
        wide_full = sem("wide_full")
        wide_free = [sem(f"wide_free{k}") for k in range(2)]
        split_hi = sem("split_hi")
        ctx_lo, ctx_lo_pool = sem("ctx_lo"), sem("ctx_lo_pool")
        w_hi = sem("w_hi")
        w_lo = sem("w_lo")
        w_lo_pool = sem("w_lo_pool")
        w_sum = sem("w_sum")
        km_ready = sem("km_ready")
        k_spilled, q_spilled = sem("k_spilled"), sem("q_spilled")
        kr_loaded = sem("kr_loaded")
        ks_ready = sem("ks_ready")
        max_spilled = sem("max_spilled")
        qs_loaded = [sem(f"qs_loaded{k}") for k in range(2)]
        max_loaded = [sem(f"max_loaded{k}") for k in range(2)]
        consts_pool = sem("consts_pool")
        consts_dve = sem("consts_dve")
        lora_ready = sem("lora_ready")
        stat_done, moments_ready = sem("stat_done"), sem("moments_ready")
        eps_done, rstd_ready = sem("eps_done"), sem("rstd_ready")
        xn_ready = sem("xn_ready")
        rec_ready = sem("rec_ready")
        cs_step = sem("cs_step")
        m1_ready = sem("m1_ready")
        nmin_ready = sem("nmin_ready")
        v1_ready = sem("v1_ready")
        shifted = sem("shifted")
        z_ready = sem("z_ready")
        zero_q1 = sem("zero_q1")
        fac_dve, fac_act = sem("fac_dve"), sem("fac_act")
        nm_dve, nm_pool = sem("nm_dve"), sem("nm_pool")
        xb_ready = sem("xb_ready")

        def filled(eng, step):
            eng.wait_ge(bank_full, BANK[step] + 1)

        def consumed(eng, step):
            n = BANK[step]
            eng.wait_ge(bank_free[n % NG], n // NG + 1)

        def bank(step):
            return ps[:, BANK[step] % NG, :]

        def free(step):
            return bank_free[BANK[step] % NG]

        def take_bank(eng, step):
            n = BANK[step]
            if n >= NG:
                eng.wait_ge(bank_free[n % NG], n // NG)
            return bank(step)

        def wide(step):
            k = NG + 2 * (WIDE[step] % 2)
            return ps[:, k:k + 2, :]

        def wide_filled(eng, step):
            eng.wait_ge(wide_full, WIDE[step] + 1)

        def wide_consumed(eng, step):
            n = WIDE[step]
            eng.wait_ge(wide_free[n % 2], n // 2 + 1)

        def stacks_read(eng, b):
            for g2 in range(KVH // 2):
                wide_filled(eng, ("ST", b, g2))

        def take_wide(eng, step):
            n = WIDE[step]
            if n >= 2:
                eng.wait_ge(wide_free[n % 2], n // 2)
            return wide(step)

        def ctx_split(eng, step):
            mine = step in CT_BY_POOL
            n = sum((s in CT_BY_POOL) == mine for s in CTX if CTX[s] <= CTX[step])
            eng.wait_ge(ctx_lo_pool if mine else ctx_lo, n)

        def ctx_read(eng, step):
            b = step[2]
            if step[1] == 1:
                for c in range(C):
                    filled(eng, ("K1", b // 2 * C + c))
            else:
                filled(eng, ("V0" if step[1] == 0 else "V1", b))

        def hi_written(eng, step):
            eng.wait_ge(split_hi, SPLIT[step] + 1)

        def weight_ready(eng, name):
            mine = [k for k, (n, _) in enumerate(CHUNKS) if n == name]
            if name in BY_POOL:
                eng.wait_ge(w_lo_pool, sum(n in BY_POOL for n, _ in CHUNKS[:mine[-1] + 1]))
            else:
                eng.wait_ge(w_lo, sum(n not in BY_POOL + ("dft",) for n, _ in CHUNKS[:mine[-1] + 1]))

        def hi_count(key):
            return sum(n != "dft" for n, _ in CHUNKS[:CHUNK[key] + 1])

        def stage_loaded(eng, key):
            n = CHUNK[key]
            eng.wait_ge(stg_loaded[n % NSTG], 16 * (n // NSTG + 1))

        def stage(key):
            return stg[:, CHUNK[key] % NSTG, :]

        def parts(key):
            name, c = key
            src = stage(key)
            if name == "wkv":
                return (wkv_h[:, 2 * c:2 * c + 2, :], wkv_l[:, 2 * c:2 * c + 2, :],
                        src.rearrange("p (c n) -> p c n", c=2))
            if name == "la":
                return la_h[:, :, :], la_l[:, :, :], src.rearrange("p (c n) -> p c n", c=C)
            if name == "lb":
                return lb_h[:, :], lb_l[0:TOP, :], src
            k = {"wq0": 0, "wk1": 0, "wo": 1, "wq1": 1, "wbase": 1, "w0": 2, "wv1": 2}[name]
            return slot_h[k][:, c, :], slot_l[k][:, c, :], src

        last_readers = {"wk1": [("Q0", PAIRS - 1, half) for half in range(2)], "wq1": [("WO", B - 1)],
                        "wv1": [("F0", B - 2), ("F0", B - 1)], "wbase": [("Q1", GROUPS - 2), ("Q1", GROUPS - 1)]}

        def passes(eng, dst, left, right, start=True, stop=True):
            eng.matmul(dst, left[0], right[0], start=start, stop=False)
            eng.matmul(dst, left[0], right[1], start=False, stop=False)
            return eng.matmul(dst, left[1], right[0], start=False, stop=stop)

        def project(eng, dst, left, right):
            for c in range(C):
                last = passes(eng, dst, left(c), right(c), start=(c == 0), stop=(c == C - 1))
            return last

        block = always.enter_context(nc.Block())

        @block.sync
        def _(sp):
            def load_ctx(n):
                step = turn_of(CTX, n)
                if n >= 2:
                    ctx_split(sp, turn_of(CTX, n - 2))
                sp.dma_start(ctx_in[:, n % 2, :], ctx[step[2]]).then_inc(ctx_loaded[n % 2], 16)

            def load_chunk(n):
                name, c = CHUNKS[n]
                if n >= NSTG:
                    old = CHUNKS[n - NSTG]
                    if old[0] == "dft":
                        filled(sp, ("WM",))
                    elif old[0] in BY_POOL:
                        sp.wait_ge(w_lo_pool, sum(k in BY_POOL for k, _ in CHUNKS[:n - NSTG + 1]))
                    else:
                        sp.wait_ge(w_lo, sum(k not in BY_POOL + ("dft",) for k, _ in CHUNKS[:n - NSTG + 1]))
                dst = stg[:, n % NSTG, :]
                w = {"wkv": wkv, "wq0": wq0, "wo": wo, "la": la, "lb": lb, "w0": w0, "wk1": wk1, "wq1": wq1,
                     "wv1": wv1, "dft": dft, "wbase": wbase}[name]
                if name == "wkv":
                    src = w.rearrange("(c p) n -> p c n", p=P)[:, 2 * c:2 * c + 2, :]
                    dst = dst.rearrange("p (c n) -> p c n", c=2)
                elif name == "la":
                    src = w.rearrange("(c p) n -> p c n", p=P)
                    dst = dst.rearrange("p (c n) -> p c n", c=C)
                elif name == "lb":
                    src = w
                else:
                    src = w[c * P:(c + 1) * P, :]
                sp.dma_start(dst, src).then_inc(stg_loaded[n % NSTG], 16)

            def load_x(b):
                sp.dma_start(X[:, b, :], x[b]).then_inc(x_loaded[b], 16)

            load_ctx(0)
            sp.dma_start(ident[:, :], eye).then_inc(ident_loaded, 16)
            load_chunk(0)
            load_chunk(1)
            load_x(0)
            load_ctx(1)
            load_x(1)
            sp.dma_start(tab[:, :], table).then_inc(small_loaded, 16)
            load_chunk(2)
            load_chunk(3)
            sp.dma_start(starts_i[:, :], starts.partition_broadcast(P)).then_inc(small_loaded, 16)
            sp.dma_start(bias_qk[:, :, :], biases).then_inc(small_loaded, 16)
            for b in range(2, B):
                load_x(b)
            done_chunks, done_ctx, n_w = 4, 2, 0
            for step in ORDER:
                if step[0] == "CT" and done_ctx < len(CTX):
                    load_ctx(done_ctx)
                    done_ctx += 1
                elif step[0] == "W" or step[0] == "WE":
                    n_w += 1
                    while done_chunks < min(n_w + NSTG, len(CHUNKS)) and CHUNKS[done_chunks][0] != "dft":
                        load_chunk(done_chunks)
                        done_chunks += 1
                elif step[0] == "WC":
                    for _ in range(C):
                        load_chunk(done_chunks)
                        done_chunks += 1
                elif step[0] == "KS":
                    p = step[1]
                    consumed(sp, ("K0", p))
                    for part, src in enumerate((K_h, K_l)):
                        sp.dma_start(k_dram[p][part], src[:, p % 2, :, :].rearrange("p b t -> p (b t)").bitcast(F32)).then_inc(k_spilled, 16)
                elif step[0] == "KL":
                    p = step[1]
                    sp.wait_ge(k_spilled, 32 * (p + 1))
                    if p:
                        sp.wait_ge(ks_ready, 2 * p)
                    for n, part in enumerate((0, 0, 1)):
                        sp.dma_start(KR[32 * n:32 * n + 32, :, :, :].rearrange("p g b t -> p g (b t)"),
                                     k_dram[p][part].rearrange("(g p) n -> p g n", p=32)).then_inc(kr_loaded, 16)
                elif step[0] == "QS":
                    p = step[1]
                    consumed(sp, ("Q0", p, 0))
                    consumed(sp, ("Q0", p, 1))
                    for part, src in enumerate((Q_h, Q_l)):
                        sp.dma_start(q_dram[p][part], src[:, :, :, :].rearrange("p b r q -> p b (r q)").bitcast(F32)).then_inc(q_spilled, 16)
                elif step[0] == "QL":
                    b = step[1]
                    sp.wait_ge(q_spilled, 32 * (b // 2 + 1))
                    if b >= 2:
                        stacks_read(sp, b - 2)
                    for n, part in enumerate((0, 1, 0)):
                        sp.dma_start(QS[32 * n:32 * n + 32, b % 2, :, :].bitcast(F32),
                                     q_dram[b // 2][part, :, b % 2, :].rearrange("(g p) n -> p g n", p=32)).then_inc(qs_loaded[b % 2], 16)
                elif step[0] == "DM":
                    b = step[1]
                    consumed(sp, ("MT", b))
                    sp.dma_start(max_dram[b], negmax[0:KVH, b % 2, :].bitcast(F32)).then_inc(max_spilled, 16)
                    sp.wait_ge(max_spilled, 16 * (b + 1))
                    if b == 0:
                        sp.wait_ge(consts_pool, 4)
                    if b >= 2:
                        stacks_read(sp, b - 2)
                    sp.dma_start(QS[LAST:LAST + 2, b % 2, :, :].bitcast(F32),
                                 max_dram[b].rearrange("(g e) n -> e g n", e=2)).then_inc(max_loaded[b % 2], 16)
                elif step[0] == "PH2":
                    filled(sp, ("OX", B - 1))
                    sp.dma_start(cf[:, :, :, :], coefs).then_inc(late_loaded, 16)
                    sp.dma_start(mk[:, :], masks).then_inc(late_loaded, 16)
                    sp.dma_start(enc_sb[0:ENC, :], enc).then_inc(late_loaded, 16)
                    sp.dma_start(bias_out[:, :], bbase.partition_broadcast(P)).then_inc(late_loaded, 16)
                    sp.dma_start(bias_v[:, :], bv1.partition_broadcast(P)).then_inc(late_loaded, 16)
                elif step[0] == "WM":
                    n_w += C
                    while done_chunks < len(CHUNKS):
                        load_chunk(done_chunks)
                        done_chunks += 1
                elif step[0] == "F1":
                    b = step[1]
                    consumed(sp, step)
                    sp.dma_start(out[b], XB[:, b % 2, :]).then_inc(out_stored[b % 2], 16)
            for k in range(2):
                sp.wait_ge(out_stored[k], 16 * (B // 2))

        @block.tensor
        def _(pe):
            pe.wait_ge(ident_loaded, 16)
            for step in ORDER:
                kind = step[0]
                if kind == "XT":
                    layer, b = step[1:]
                    n = NORMED[("LNn", layer, b)]
                    dst = take_bank(pe, step)
                    pe.wait_ge(xn_ready, n + 1)
                    for c in range(C):
                        last = pe.transpose(dst[:, c * P:(c + 1) * P], xn[:, n % 2, c * P:(c + 1) * P],
                                            ident[:, :])
                    last.then_inc(bank_full, 1)
                elif kind == "V0":
                    b = step[1]
                    dst = take_bank(pe, step)
                    weight_ready(pe, "wkv")
                    ctx_split(pe, ("CT", 0, b))
                    last = project(pe, dst[:, 0:2 * P],
                                   lambda c: (ctxT_h[:, c, b % 2, :], ctxT_l[:, c, b % 2, :]),
                                   lambda c: (wkv_h[:, c, :], wkv_l[:, c, :]))
                    last.then_inc(bank_full, 1)
                elif kind == "K0":
                    p = step[1]
                    dst = take_bank(pe, step)
                    for k in range(2):
                        consumed(pe, ("V0", 2 * p + k))
                        last = pe.transpose(dst[:, k * P:(k + 1) * P], K_raw[:, k, :], ident[:, :])
                    last.then_inc(bank_full, 1)
                elif kind == "Q0":
                    p, half = step[1:]
                    dst = take_bank(pe, step)
                    weight_ready(pe, "wq0")
                    consumed(pe, ("XT", 0, 2 * p))
                    consumed(pe, ("XT", 0, 2 * p + 1))
                    for k in range(2):
                        r = 2 * half + k
                        last = project(pe, dst[:, k * 2 * P:(k + 1) * 2 * P],
                                       lambda c: (slot_h[0][:, c, r * P:(r + 1) * P],
                                                  slot_l[0][:, c, r * P:(r + 1) * P]),
                                       lambda c: (xT_h[:, c, :, :].rearrange("p b t -> p (b t)"),
                                                  xT_l[:, c, :, :].rearrange("p b t -> p (b t)")))
                    last.then_inc(bank_full, 1)
                elif kind == "MX":
                    b, r = step[1:]
                    p = b // 2
                    dst = take_wide(pe, step)
                    consumed(pe, ("Q0", p, r // 2))
                    pe.wait_ge(km_ready, b + 1)
                    for k in range(2):
                        last = pe.matmul(dst[:, k, :], Q_h[:, b % 2, r, :],
                                         KM_h[:, b % 2, 4 * k:4 * k + 4, :].rearrange("p g k -> p (g k)"),
                                         start=True, stop=True)
                    last.then_inc(wide_full, 1)
                elif kind == "MT":
                    b = step[1]
                    dst = take_bank(pe, step)
                    for r in range(REP):
                        wide_consumed(pe, ("MX", b, r))
                    for r in range(REP):
                        last = pe.transpose(dst[0:KVH, r * P:(r + 1) * P], mx[:, b % 2, r, :], ident[:, :])
                    last.then_inc(bank_full, 1)
                elif kind == "ST":
                    b, g2 = step[1:]
                    p = b // 2
                    dst = take_wide(pe, step)
                    if (b, g2) == (0, 0):
                        pe.wait_ge(consts_dve, 2)
                        pe.wait_ge(consts_pool, 4)
                    pe.wait_ge(ks_ready, b + 1)
                    pe.wait_ge(qs_loaded[b % 2], 16 * 3 * (b // 2 + 1))
                    pe.wait_ge(max_loaded[b % 2], 16 * (b // 2 + 1))
                    for k in range(2):
                        last = pe.matmul(dst[:, k, :], KS[:, b % 2, 2 * g2 + k, :], QS[:, b % 2, g2, :],
                                         start=True, stop=True)
                    last.then_inc(wide_full, 1)
                elif kind == "PV":
                    b, gq = step[1:]
                    dst = take_bank(pe, step)
                    consumed(pe, ("V0", b))
                    wide_consumed(pe, ("ST", b, 2 * gq))
                    wide_consumed(pe, ("ST", b, 2 * gq + 1))
                    for j in range(4):
                        n = 4 * b + 2 * gq + j // 2
                        last = pe.matmul(dst[32 * j:32 * j + 32, :], V0[:, b % 4, 4 * gq + j, :],
                                         PT[:, n % 4, (j % 2) * D:(j % 2 + 1) * D], start=True, stop=True)
                    last.then_inc(bank_full, 1)
                elif kind == "OB":
                    b, gq = step[1:]
                    dst = take_bank(pe, step)
                    consumed(pe, ("PV", b, gq))
                    for r in range(REP):
                        last = pe.transpose(dst[:, r * P:(r + 1) * P], OTs[:, gq, r * P:(r + 1) * P],
                                            ident[:, :])
                    last.then_inc(bank_full, 1)
                elif kind == "OX":
                    b = step[1]
                    dst = take_bank(pe, step)
                    consumed(pe, ("OB", b, 0))
                    consumed(pe, ("OB", b, 1))
                    for c in range(C):
                        last = pe.transpose(dst[:, c * P:(c + 1) * P], O[:, c * P:(c + 1) * P],
                                            ident[:, :])
                    last.then_inc(bank_full, 1)
                elif kind == "WO":
                    b = step[1]
                    dst = take_bank(pe, step)
                    weight_ready(pe, "wo")
                    consumed(pe, ("OX", b))
                    last = project(pe, dst, lambda c: (OT_h[:, c, :], OT_l[:, c, :]),
                                   lambda c: (slot_h[1][:, c, :], slot_l[1][:, c, :]))
                    last.then_inc(bank_full, 1)
                elif kind == "LT":
                    p = step[1]
                    dst = take_bank(pe, step)
                    weight_ready(pe, "la")
                    consumed(pe, ("XT", 1, 2 * p))
                    consumed(pe, ("XT", 1, 2 * p + 1))
                    last = project(pe, dst[:, 0:2 * P], lambda c: (la_h[:, c, :], la_l[:, c, :]),
                                   lambda c: (fT_h[:, c, :, :].rearrange("p b t -> p (b t)"),
                                              fT_l[:, c, :, :].rearrange("p b t -> p (b t)")))
                    last.then_inc(bank_full, 1)
                elif kind == "F0":
                    b = step[1]
                    dst = take_bank(pe, step)
                    weight_ready(pe, "w0")
                    consumed(pe, ("LT", b // 2))
                    for c in range(C):
                        passes(pe, dst, (fT_h[:, c, b % 2, :], fT_l[:, c, b % 2, :]),
                               (slot_h[2][:, c, :], slot_l[2][:, c, :]), start=(c == 0), stop=False)
                    pe.matmul(dst, lora_t[:, b % 2, :], lb_h[:, :], start=False, stop=False)
                    pe.matmul(dst, lora_t[:, b % 2, :], lb_l[:, :], start=False, stop=True).then_inc(bank_full, 1)
                elif kind in ("K1", "Q1"):
                    g = step[1]
                    p, c1 = g // C, g % C
                    dst = take_bank(pe, step)
                    src, k = ((ctxT_h, ctxT_l), 0) if kind == "K1" else ((xT_h, xT_l), 1)
                    weight_ready(pe, "wk1" if kind == "K1" else "wq1")
                    for b in (2 * p, 2 * p + 1):
                        if kind == "K1":
                            ctx_split(pe, ("CT", 1, b))
                        else:
                            consumed(pe, ("XT", 2, b))
                    last = project(pe, dst[:, 0:2 * P],
                                   lambda c: (slot_h[k][:, c, c1 * P:(c1 + 1) * P],
                                              slot_l[k][:, c, c1 * P:(c1 + 1) * P]),
                                   lambda c: [t[:, c, :, :].rearrange("p b t -> p (b t)") for t in src])
                    last.then_inc(bank_full, 1)
                elif kind == "S1":
                    g = step[1]
                    dst = take_wide(pe, step)
                    consumed(pe, ("K1", g))
                    consumed(pe, ("Q1", g))
                    for b in range(2):
                        last = passes(pe, dst[:, b, :], (K1_h[:, g % 2, b, :], K1_l[:, g % 2, b, :]),
                                      [t[:, g % 2, b, :, :].rearrange("p j q -> p (j q)") for t in (Q1_h, Q1_l)])
                    last.then_inc(wide_full, 1)
                elif kind == "SM":
                    g = step[1]
                    dst = wide(("S1", g))
                    pe.wait_ge(m1_ready, g + 1)
                    pe.wait_ge(consts_dve, 3)
                    for b in range(2):
                        last = pe.matmul(dst[:, b, :], ident_r[:, :],
                                         mneg[:, g, :].unsqueeze(1).broadcast_to([P, JH, P]),
                                         start=False, stop=True, skip_group_check=True)
                    last.then_inc(shifted, 1)
                elif kind == "V1":
                    b = step[1]
                    dst = take_bank(pe, step)
                    weight_ready(pe, "wv1")
                    ctx_split(pe, ("CT", 2, b))
                    last = project(pe, dst, lambda c: (ctxT_h[:, c, b % 2, :], ctxT_l[:, c, b % 2, :]),
                                   lambda c: (slot_h[2][:, c, :], slot_l[2][:, c, :]))
                    last.then_inc(bank_full, 1)
                elif kind == "PV1":
                    b = step[1]
                    dst = take_bank(pe, step)
                    pe.wait_ge(v1_ready, b + 1)
                    pe.wait_ge(nm_dve, 3 * (b // 2 + 1))
                    pe.wait_ge(nm_pool, b // 2 + 1)
                    for c in range(C):
                        for j in range(JH):
                            h = c * JH + j
                            last = pe.matmul(dst[32 * j:32 * j + 32, c * P:(c + 1) * P],
                                             V1[:, b, h * HD1:(h + 1) * HD1],
                                             P1[:, b // 2 * C + c, (b % 2) * JH + j, :], start=True, stop=True)
                    last.then_inc(bank_full, 1)
                elif kind == "OX1":
                    b = step[1]
                    dst = take_bank(pe, step)
                    consumed(pe, ("PV1", b))
                    for c in range(C):
                        last = pe.transpose(dst[:, c * P:(c + 1) * P], O1T[:, b % 2, c * P:(c + 1) * P], ident[:, :])
                    last.then_inc(bank_full, 1)
                elif kind == "F1":
                    b = step[1]
                    dst = take_bank(pe, step)
                    weight_ready(pe, "wbase")
                    consumed(pe, ("XT", 3, b))
                    last = project(pe, dst, lambda c: (xT_h[:, c, b % 2, :], xT_l[:, c, b % 2, :]),
                                   lambda c: (slot_h[1][:, c, :], slot_l[1][:, c, :]))
                    last.then_inc(bank_full, 1)
                elif kind == "WM":
                    dst = take_bank(pe, step)
                    pe.wait_ge(cs_step, 3)
                    for c in range(C):
                        stage_loaded(pe, ("dft", c))
                        last = pe.matmul(dst[0:ENC, :], cs[:, c, :], stage(("dft", c)),
                                         start=(c == 0), stop=(c == C - 1))
                    last.then_inc(bank_full, 1)
                elif kind == "WE":
                    c = step[1]
                    dst = take_bank(pe, step)
                    consumed(pe, ("WM",))
                    pe.wait_ge(late_loaded, 80)
                    pe.matmul(dst, enc_sb[0:ENC, c * P:(c + 1) * P], mt[0:ENC, :],
                              start=True, stop=True).then_inc(bank_full, 1)

        @block.scalar
        def _(act):
            for step in ORDER:
                kind = step[0]
                if kind == "W":
                    key = step[1:]
                    hi, _, src = parts(key)
                    stage_loaded(act, key)
                    for reader in last_readers.get(key[0], []):
                        filled(act, reader)
                    act.activation(hi, src, ACT.Copy).then_inc(w_hi, 1)
                elif kind == "WE":
                    key = ("wbase", step[1])
                    hi, _, src = parts(key)
                    consumed(act, step)
                    for reader in last_readers["wbase"]:
                        filled(act, reader)
                    act.activation(hi, src, ACT.Copy).then_inc(w_hi, 1)
                elif kind == "CT":
                    n, old = CTX[step], previous_ctx(step)
                    act.wait_ge(ctx_loaded[n % 2], 16 * (n // 2 + 1))
                    if old:
                        ctx_read(act, old)
                    act.activation(ctxT_h[:, :, step[2] % 2, :],
                                   ctx_in[:, n % 2, :].rearrange("p (c t) -> p c t", c=C), ACT.Copy).then_inc(split_hi, 1)
                elif kind == "XT":
                    filled(act, step)
                    dst = fT_h if step[1] == 1 else xT_h
                    act.activation(dst[:, :, step[2] % 2, :],
                                   bank(step).rearrange("p (c t) -> p c t", c=C), ACT.Copy).then_inc(split_hi, 1)
                elif kind == "K0":
                    p = step[1]
                    filled(act, step)
                    if p >= 2:
                        act.wait_ge(km_ready, 2 * (p - 1))
                        act.wait_ge(k_spilled, 32 * (p - 1))
                    act.activation(K_h[:, p % 2, :, :], bank(step)[:, 0:2 * P].rearrange("p (b t) -> p b t", b=2),
                                   ACT.Copy).then_inc(split_hi, 1)
                elif kind == "V0":
                    b = step[1]
                    filled(act, step)
                    act.wait_ge(consts_pool, 4)
                    act.activation(K_raw[:, b % 2, :], bank(step)[:, 0:P], ACT.Copy)
                    act.activation(V0[:, b % 4, :, 0:HD0],
                                   bank(step)[:, P:2 * P].rearrange("p (g d) -> p g d", g=KVH),
                                   ACT.Copy).then_inc(free(step), 1)
                elif kind == "Q0":
                    p, half = step[1:]
                    filled(act, step)
                    if p:
                        act.wait_ge(q_spilled, 32 * p)
                    act.activation(Q_h[:, :, 2 * half:2 * half + 2, :],
                                   bank(step).rearrange("p (r b q) -> p b r q", r=2, b=2),
                                   ACT.Copy).then_inc(split_hi, 1)
                elif kind == "ST":
                    b, g2 = step[1:]
                    n = 4 * b + g2
                    wide_filled(act, step)
                    if n >= 4:
                        filled(act, ("PV", (n - 4) // 4, (n - 4) % 4 // 2))
                    act.activation(PT[:, n % 4, :], wide(step).rearrange("p k n -> p (k n)"), ACT.Exp,
                                   scale=SCALE0).then_inc(wide_free[WIDE[step] % 2], 1)
                elif kind == "PV":
                    b, gq = step[1:]
                    filled(act, step)
                    act.activation(OTs[:, gq, :], bank(step), ACT.Copy).then_inc(free(step), 1)
                elif kind == "OX":
                    b = step[1]
                    filled(act, step)
                    act.activation(OT_h[:, :, :], bank(step).rearrange("p (c t) -> p c t", c=C),
                                   ACT.Copy).then_inc(split_hi, 1)
                elif kind == "LT":
                    p = step[1]
                    filled(act, step)
                    act.wait_ge(small_loaded, 16 * 3)
                    act.wait_ge(lora_ready, 5)
                    for k in range(2):
                        b = 2 * p + k
                        last = act.activation(lora_t[:, k, :], bank(step)[:, k * P:(k + 1) * P], ACT.Identity,
                                              scale=use_lora[:, b:b + 1], bias=tab[:, KVH + B + 1:KVH + B + 2])
                    last.then_inc(split_hi, 1)
                elif kind == "K1":
                    g = step[1]
                    filled(act, step)
                    act.activation(K1_h[:, g % 2, :, :], bank(step)[:, 0:2 * P].rearrange("p (b t) -> p b t", b=2),
                                   ACT.Identity, bias=bias_qk[:, 0, g % C:g % C + 1]).then_inc(split_hi, 1)
                elif kind == "Q1":
                    g = step[1]
                    filled(act, step)
                    act.wait_ge(zero_q1, 4)
                    for j in range(JH):
                        rows = slice(j * HD1, (j + 1) * HD1)
                        last = act.activation(Q1_h[rows, g % 2, :, j, :],
                                              bank(step)[rows, 0:2 * P].rearrange("p (b t) -> p b t", b=2),
                                              ACT.Identity, bias=bias_qk[rows, 1, g % C:g % C + 1])
                    last.then_inc(split_hi, 1)
                elif kind == "SM":
                    g = step[1]
                    act.wait_ge(shifted, g + 1)
                    act.activation(P1[:, g, :, :].rearrange("p t q -> p (t q)"),
                                   wide(("S1", g)).rearrange("p k n -> p (k n)"),
                                   ACT.Exp, scale=SCALE1).then_inc(wide_free[WIDE[("S1", g)] % 2], 1)
                elif kind == "FA" and step[1] == 0:
                    act.wait_ge(fac_dve, 1)
                    act.activation(fac[:, :, :], fac[:, :, :], ACT.Exp, scale=SCALE1).then_inc(fac_act, 1)
                elif kind == "V1":
                    b = step[1]
                    filled(act, step)
                    for c in range(C):
                        filled(act, ("K1", GROUPS - 1 - c))
                    act.activation(V1[:, b, :], bank(step), ACT.Copy).then_inc(free(step), 1)
                elif kind == "PV1":
                    b = step[1]
                    filled(act, step)
                    act.activation(O1T[:, b % 2, :], bank(step), ACT.Copy).then_inc(free(step), 1)

        @block.vector
        def _(dve):
            for step in ORDER:
                kind = step[0]
                if kind == "C0":
                    dve.wait_ge(small_loaded, 16 * 3)
                    for k in range(2):
                        dve.tensor_copy(KS[LAST:P, k, :, :],
                                        tab[LAST:P, KVH + B + 2:KVH + B + 2 + KVH].unsqueeze(2).broadcast_to([P - LAST, KVH, P])).then_inc(consts_dve, 1)
                    dve.wait_ge(ident_loaded, 16)
                    dve.tensor_copy(ident_r[:, :], ident[:, :]).then_inc(consts_dve, 1)
                    dve.tensor_copy(starts_f[:, :], starts_i[:, :]).then_inc(lora_ready, 1)
                    dve.wait_ge(lora_ready, 1)
                    dve.tensor_tensor(started[:, :, :], starts_f[:, :].unsqueeze(1).broadcast_to([P, B, 4]),
                                      tab[:, KVH:KVH + B].unsqueeze(2).broadcast_to([P, B, 4]),
                                      ALU.is_le).then_inc(lora_ready, 1)
                    dve.wait_ge(lora_ready, 2)
                    dve.tensor_reduce(n_started[:, :], started[:, :, :], AX_X, ALU.add).then_inc(lora_ready, 1)
                    dve.wait_ge(lora_ready, 3)
                    dve.tensor_scalar(use_lora[:, :], n_started[:, :], tab[:, KVH + B:KVH + B + 1], None,
                                      ALU.is_equal).then_inc(lora_ready, 1)
                    dve.wait_ge(lora_ready, 4)
                    dve.memset(lb_l[TOP:P, :].bitcast(F32), 0.0).then_inc(lora_ready, 1)
                elif kind == "W" and step[1] not in BY_POOL:
                    key = step[1:]
                    hi, lo, src = parts(key)
                    if key[0] == "lb":
                        hi, src = hi[0:TOP, :], src[0:TOP, :]
                    dve.wait_ge(w_hi, hi_count(key))
                    dve.tensor_tensor(lo, src, hi.bitcast(F32), ALU.subtract).then_inc(w_lo, 1)
                elif kind == "WE":
                    key = ("wbase", step[1])
                    filled(dve, step)
                    stage_loaded(dve, key)
                    hi, lo, src = parts(key)
                    dve.tensor_tensor(src, bank(step), src, ALU.add).then_inc(free(step), 1)
                elif kind == "LNs":
                    layer, b = step[1:]
                    n = NORM[step]
                    if layer == 0:
                        dve.wait_ge(x_loaded[b], 16)
                    else:
                        consumed(dve, [None, ("WO", b), ("F0", b), ("OX1", b)][layer])
                    if n >= 4:
                        dve.wait_ge(rstd_ready, n - 3)
                    dve.bn_stats(stats[:, n % 4, :], X[:, b, :]).then_inc(stat_done, 1)
                    dve.wait_ge(stat_done, n + 1)
                    dve.bn_aggr(moments[:, n % 4, :], stats[:, n % 4, :]).then_inc(moments_ready, 1)
                elif kind == "LNn":
                    layer, b = step[1:]
                    n, m = NORM[("LNs", layer, b)], NORMED[step]
                    if m >= 2:
                        filled(dve, ("XT",) + turn_of(NORMED, m - 2)[1:])
                    dve.wait_ge(rstd_ready, n + 1)
                    dve.tensor_scalar(xn[:, m % 2, :], X[:, b, :], moments[:, n % 4, 0:1], rstd[:, n % 4, 0:1],
                                      ALU.subtract, ALU.mult).then_inc(xn_ready, 1)
                elif kind == "CT" and step not in CT_BY_POOL:
                    hi_written(dve, step)
                    dve.tensor_tensor(ctxT_l[:, :, step[2] % 2, :],
                                      ctx_in[:, CTX[step] % 2, :].rearrange("p (c t) -> p c t", c=C),
                                      ctxT_h[:, :, step[2] % 2, :].bitcast(F32), ALU.subtract).then_inc(ctx_lo, 1)
                elif kind in ("XT", "OX"):
                    hi_written(dve, step)
                    if kind == "OX":
                        lo, hi = [t[:, :, :] for t in (OT_l, OT_h)]
                    else:
                        ts = (fT_l, fT_h) if step[1] == 1 else (xT_l, xT_h)
                        lo, hi = [t[:, :, step[2] % 2, :] for t in ts]
                    dve.tensor_tensor(lo, bank(step).rearrange("p (c t) -> p c t", c=C), hi.bitcast(F32),
                                      ALU.subtract).then_inc(free(step), 1)
                elif kind == "K0":
                    p = step[1]
                    hi_written(dve, step)
                    dve.tensor_tensor(K_l[:, p % 2, :, :], bank(step)[:, 0:2 * P].rearrange("p (b t) -> p b t", b=2),
                                      K_h[:, p % 2, :, :].bitcast(F32), ALU.subtract).then_inc(free(step), 1)
                elif kind == "Q0":
                    p, half = step[1:]
                    rs = slice(2 * half, 2 * half + 2)
                    hi_written(dve, step)
                    dve.tensor_tensor(Q_l[:, :, rs, :], bank(step).rearrange("p (r b q) -> p b r q", r=2, b=2),
                                      Q_h[:, :, rs, :].bitcast(F32), ALU.subtract).then_inc(free(step), 1)
                elif kind == "MX":
                    b, r = step[1:]
                    wide_filled(dve, step)
                    dve.tensor_reduce(mx[:, b % 2, r, :], wide(step).rearrange("p k (g t) -> p (k g) t", g=4),
                                      AX_X, ALU.max).then_inc(wide_free[WIDE[step] % 2], 1)
                elif kind == "MT":
                    b = step[1]
                    filled(dve, step)
                    if b >= 2:
                        dve.wait_ge(max_spilled, 16 * (b - 1))
                    dve.tensor_scalar(negmax[0:KVH, b % 2, :], bank(step)[0:KVH, :], -1.0, None,
                                      ALU.mult).then_inc(free(step), 1)
                elif kind == "OB":
                    b, gq = step[1:]
                    filled(dve, step)
                    src = bank(step).rearrange("p (r j e) -> p r j e", r=REP, j=4)
                    dve.reciprocal(rec[:, gq, :, :], src[:, :, :, HD0]).then_inc(rec_ready, 1)
                    dve.wait_ge(rec_ready, 2 * b + gq + 1)
                    dst = O[:, :].rearrange("p (g r d) -> p r g d", g=KVH, r=REP)[:, :, 4 * gq:4 * gq + 4, :]
                    dve.tensor_tensor(dst, src[:, :, :, 0:HD0],
                                      rec[:, gq, :, :].unsqueeze(3).broadcast_to([P, REP, 4, HD0]),
                                      ALU.mult).then_inc(free(step), 1)
                elif kind in ("WO", "F0"):
                    b = step[1]
                    filled(dve, step)
                    dve.tensor_tensor(X[:, b, :], bank(step), X[:, b, :], ALU.add).then_inc(free(step), 1)
                elif kind == "LT":
                    p = step[1]
                    hi_written(dve, step)
                    for k in range(2):
                        b = 2 * p + k
                        last = dve.scalar_tensor_tensor(
                            out=lora_t[TOP:P, k, :], in0=bank(step)[TOP:P, k * P:(k + 1) * P],
                            scalar=use_lora[TOP:P, b:b + 1], in1=lora_t[TOP:P, k, :].bitcast(F32),
                            op0=ALU.mult, op1=ALU.subtract)
                    last.then_inc(free(step), 1)
                elif kind == "K1":
                    g = step[1]
                    hi_written(dve, step)
                    dve.scalar_tensor_tensor(
                        out=K1_l[:, g % 2, :, :], in0=bank(step)[:, 0:2 * P].rearrange("p (b t) -> p b t", b=2),
                        scalar=bias_qk[:, 0, g % C:g % C + 1], in1=K1_h[:, g % 2, :, :].bitcast(F32),
                        op0=ALU.add, op1=ALU.subtract).then_inc(free(step), 1)
                elif kind == "Q1":
                    g = step[1]
                    hi_written(dve, step)
                    dve.wait_ge(zero_q1, 4)
                    for j in range(JH):
                        rows = slice(j * HD1, (j + 1) * HD1)
                        last = dve.scalar_tensor_tensor(
                            out=Q1_l[rows, g % 2, :, j, :],
                            in0=bank(step)[rows, 0:2 * P].rearrange("p (b t) -> p b t", b=2),
                            scalar=bias_qk[rows, 1, g % C:g % C + 1], in1=Q1_h[rows, g % 2, :, j, :].bitcast(F32),
                            op0=ALU.add, op1=ALU.subtract)
                    last.then_inc(free(step), 1)
                elif kind == "S1":
                    g = step[1]
                    wide_filled(dve, step)
                    dve.tensor_reduce(mneg[:, g, :], wide(step).rearrange("p k (j q) -> p q (k j)", j=JH),
                                      AX_X, ALU.max, negate=True).then_inc(m1_ready, 1)
                elif kind == "SM":
                    g = step[1]
                    dve.wait_ge(m1_ready, g + 1)
                    neg = mneg[:, g, :].bitcast(F32)
                    if g == 0:
                        dve.tensor_copy(nmin[:, :], neg).then_inc(nmin_ready, 1)
                    else:
                        dve.wait_ge(nmin_ready, g)
                        dve.tensor_tensor(nmin[:, :], nmin[:, :], neg, ALU.min).then_inc(nmin_ready, 1)
                elif kind == "FA" and step[1] == 0:
                    dve.wait_ge(nmin_ready, GROUPS)
                    dve.tensor_tensor(fac[:, :, :], nmin[:, :].unsqueeze(1).broadcast_to([P, GROUPS, P]),
                                      mneg[:, :, :].bitcast(F32), ALU.subtract).then_inc(fac_dve, 1)
                elif kind == "FA" and step[1] == 1:
                    dve.wait_ge(z_ready, 3 * GROUPS)
                    dve.wait_ge(fac_act, 1)
                    dve.tensor_tensor(Z[:, :, :], Z[:, :, :], fac[:, :, :], ALU.mult).then_inc(fac_dve, 1)
                elif kind == "FA" and step[1] == 2:
                    dve.wait_ge(fac_dve, 2)
                    dve.tensor_reduce(zsum[:, :], Z[:, :, :].rearrange("p g q -> p q g"), AX_X,
                                      ALU.add).then_inc(fac_dve, 1)
                elif kind == "FA" and step[1] == 3:
                    dve.wait_ge(fac_dve, 3)
                    dve.reciprocal(zsum[:, :], zsum[:, :]).then_inc(fac_dve, 1)
                elif kind == "FA":
                    dve.wait_ge(fac_dve, 4)
                    dve.tensor_tensor(fac[:, :, :], fac[:, :, :], zsum[:, :].unsqueeze(1).broadcast_to([P, GROUPS, P]),
                                      ALU.mult).then_inc(fac_dve, 1)
                elif kind == "NM" and step[1] % C != C - 1:
                    g = step[1]
                    dve.wait_ge(fac_dve, 5)
                    dve.tensor_tensor(P1[:, g, :, :], P1[:, g, :, :],
                                      fac[:, g, :].unsqueeze(1).broadcast_to([P, T, P]),
                                      ALU.mult).then_inc(nm_dve, 1)
                elif kind == "OX1":
                    b = step[1]
                    filled(dve, step)
                    dst = X[:, b, :].rearrange("p (d h) -> p h d", h=H1)
                    dve.tensor_tensor(dst, bank(step).rearrange("p (h d) -> p h d", h=H1), dst,
                                      ALU.add).then_inc(free(step), 1)
                elif kind == "F1":
                    b = step[1]
                    filled(dve, step)
                    dve.wait_ge(xb_ready, b + 1)
                    dve.tensor_tensor(XB[:, b % 2, :], bank(step), XB[:, b % 2, :], ALU.add).then_inc(free(step), 1)
                elif kind == "WC":
                    dve.wait_ge(late_loaded, 80)
                    dve.tensor_tensor(cf[:, :, :, :], cf[:, :, :, :],
                                      mk[:, :].bitcast(U8).rearrange("p (c e r) -> p c e r", c=C, e=EXP),
                                      ALU.mult).then_inc(cs_step, 1)
                    dve.wait_ge(cs_step, 1)
                    dve.tensor_tensor(cs[:, :, :], cf[:, :, 0, :], cf[:, :, 1, :], ALU.add).then_inc(cs_step, 1)
                    dve.wait_ge(cs_step, 2)
                    dve.tensor_tensor(cs[:, :, :], cs[:, :, :], cf[:, :, 2, :], ALU.add).then_inc(cs_step, 1)
                elif kind == "WM":
                    filled(dve, step)
                    consumed(dve, ("F0", B - 2))
                    consumed(dve, ("F0", B - 1))
                    dve.tensor_copy(mt[0:ENC, :], bank(step)[0:ENC, :]).then_inc(free(step), 1)

        @block.gpsimd
        def _(pool):
            pool.memset(minus_half[:, :], -0.5).then_inc(consts_pool, 1)
            pool.memset(V0[:, :, :, :], 0.0).then_inc(consts_pool, 1)
            pool.wait_ge(consts_pool, 2)
            pool.memset(V0[:, :, :, HD0:HD0 + 1], 1.0).then_inc(consts_pool, 1)
            pool.wait_ge(consts_pool, 3)
            pool.memset(QS[LAST:P, :, :, :].bitcast(F32), 0.0).then_inc(consts_pool, 1)
            pool.wait_ge(consts_pool, 4)
            for step in ORDER:
                kind = step[0]
                if kind == "W" and step[1] in BY_POOL or kind == "WE":
                    key = ("wbase", step[1]) if kind == "WE" else step[1:]
                    hi, lo, src = parts(key)
                    pool.wait_ge(w_hi, hi_count(key))
                    pool.tensor_tensor(lo, src, hi.bitcast(F32), ALU.subtract).then_inc(w_lo_pool, 1)
                elif kind == "CT" and step in CT_BY_POOL:
                    hi_written(pool, step)
                    pool.tensor_tensor(ctxT_l[:, :, step[2] % 2, :],
                                       ctx_in[:, CTX[step] % 2, :].rearrange("p (c t) -> p c t", c=C),
                                       ctxT_h[:, :, step[2] % 2, :].bitcast(F32), ALU.subtract).then_inc(ctx_lo_pool, 1)
                elif kind == "LNs":
                    n = NORM[step]
                    pool.wait_ge(moments_ready, n + 1)
                    if n >= 4:
                        pool.wait_ge(xn_ready, NORMED[("LNn",) + turn_of(NORM, n - 4)[1:]] + 1)
                    pool.tensor_scalar(var_eps[:, n % 4, :], moments[:, n % 4, 1:2], EPS, None,
                                       ALU.add).then_inc(eps_done, 1)
                    pool.wait_ge(eps_done, n + 1)
                    pool.tensor_tensor(rstd[:, n % 4, :], var_eps[:, n % 4, :], minus_half[:, :],
                                       ALU.pow).then_inc(rstd_ready, 1)
                elif kind == "KM":
                    b = step[1]
                    consumed(pool, ("K0", b // 2))
                    pool.wait_ge(small_loaded, 16 * 3)
                    if b >= 2:
                        for r in range(REP):
                            wide_consumed(pool, ("MX", b - 2, r))
                    own = tab[:, 0:KVH].unsqueeze(2).broadcast_to([P, KVH, P])
                    pool.tensor_tensor(KM_h[:, b % 2, :, :],
                                       K_h[:, b // 2 % 2, b % 2, :].bitcast(F32).unsqueeze(1).broadcast_to([P, KVH, P]),
                                       own, ALU.mult).then_inc(km_ready, 1)
                elif kind == "KX":
                    b = step[1]
                    pool.wait_ge(kr_loaded, 16 * 3 * (b // 2 + 1))
                    if b >= 2:
                        stacks_read(pool, b - 2)
                    for e in range(2):
                        last = pool.tensor_tensor(
                            KS[0:LAST, b % 2, e:KVH:2, :], KR[0:LAST, :, b % 2, :],
                            tab[0:LAST, KVH + B + 2 + KVH + e:KVH + B + 3 + KVH + e].unsqueeze(2).broadcast_to([LAST, KVH // 2, P]),
                            ALU.mult)
                    last.then_inc(ks_ready, 1)
                elif kind == "SM":
                    g = step[1]
                    wide_consumed(pool, ("S1", g))
                    if g:
                        pool.wait_ge(z_ready, 3 * g)
                    pool.tensor_tensor(zpart[:, :, :], P1[:, g, 0:JH, :], P1[:, g, JH:T, :],
                                       ALU.add).then_inc(z_ready, 1)
                    pool.wait_ge(z_ready, 3 * g + 1)
                    pool.tensor_tensor(zpart[:, 0:2, :], zpart[:, 0:2, :], zpart[:, 2:4, :],
                                       ALU.add).then_inc(z_ready, 1)
                    pool.wait_ge(z_ready, 3 * g + 2)
                    pool.tensor_tensor(Z[:, g, :], zpart[:, 0, :], zpart[:, 1, :], ALU.add).then_inc(z_ready, 1)
                elif kind == "PH2":
                    filled(pool, ("OX", B - 1))
                    for t in (Q1_h, Q1_l):
                        for k in range(2):
                            pool.memset(t[:, k, :, :, :].bitcast(F32), 0.0).then_inc(zero_q1, 1)
                elif kind == "V1":
                    b = step[1]
                    consumed(pool, step)
                    pool.wait_ge(late_loaded, 80)
                    pool.tensor_tensor(V1[:, b, :], V1[:, b, :], bias_v[:, :], ALU.add).then_inc(v1_ready, 1)
                elif kind == "NM" and step[1] % C == C - 1:
                    g = step[1]
                    pool.wait_ge(fac_dve, 5)
                    pool.tensor_tensor(P1[:, g, :, :], P1[:, g, :, :],
                                       fac[:, g, :].unsqueeze(1).broadcast_to([P, T, P]),
                                       ALU.mult).then_inc(nm_pool, 1)
                elif kind == "OX1":
                    b = step[1]
                    consumed(pool, step)
                    pool.wait_ge(late_loaded, 80)
                    if b >= 2:
                        pool.wait_ge(out_stored[b % 2], 16 * (b // 2))
                    pool.tensor_tensor(XB[:, b % 2, :], X[:, b, :], bias_out[:, :], ALU.add).then_inc(xb_ready, 1)


def kernel(**inputs):
    import numpy as np
    import concourse.bacc as bacc
    from concourse import mybir as _mybir
    from concourse.bass_utils import run_bass_kernel_spmd as run

    a = {k: np.asarray(v) for k, v in inputs.items()}
    f = np.float32
    wq0 = a["L0_xattn_Wq"].reshape(D, KVH, REP, HD0).transpose(0, 2, 1, 3).reshape(D, D)
    lora_a = a["L0_ffn_lora_A"].reshape(RANK, D).T
    la = np.zeros((D, P), f)
    la[:, 0:RANK] = lora_a
    la[:, TOP:TOP + RANK] = lora_a
    lora_b = a["L0_ffn_lora_B"].transpose(0, 2, 1).reshape(RANK, D)
    lb = np.zeros((P, D), f)
    lb[0:RANK] = lora_b
    lb[RANK] = a["L0_ffn_bias"]
    lb[TOP:TOP + RANK] = lora_b
    packed = lambda u, v: np.concatenate([u, v], axis=2).reshape(EXP, C, P, ENC).transpose(2, 1, 0, 3)
    n = np.arange(D)
    k = np.arange(1, (D - 1) // 2 + 1)[:, None]
    dft = np.zeros((D, D))
    dft[0] = D ** -0.5
    dft[1:D - 1:2] = np.sqrt(2.0 / D) * np.cos(2 * np.pi * (k * n % D) / D)
    dft[2:D:2][:len(k)] = np.sqrt(2.0 / D) * np.sin(2 * np.pi * (k * n % D) / D)
    dft[D - 1] = np.where(n % 2 == 0, 1.0, -1.0) * D ** -0.5
    dft = (0.5 * dft).astype(f)
    row = np.arange(P)
    table = np.zeros((P, KVH + B + 2 + KVH + 2), f)
    table[:, 0:KVH] = row[:, None] // HD0 == np.arange(KVH)[None]
    table[:, KVH:KVH + B] = np.arange(B)[None]
    table[:, KVH + B] = np.where(row % TOP < RANK, row % TOP // 16 + 2, -1)
    table[:, KVH + B + 1] = row == RANK
    table[:, KVH + B + 2:KVH + B + 2 + KVH] = row[:, None] == LAST + np.arange(KVH)[None] % 2
    table[:, KVH + B + 2 + KVH:] = row[:, None] // HD0 % 2 == np.arange(2)[None]
    arrays = {
        "x": a["x"],
        "ctx": a["ctx_4096"].transpose(0, 2, 1).reshape(B, C, P, S).transpose(0, 2, 1, 3).reshape(B, P, C * S),
        "wkv": np.concatenate([a["L0_xattn_Wk"], a["L0_xattn_Wv"]], axis=1), "wq0": wq0,
        "wo": a["L0_xattn_Wo"], "la": la, "lb": lb, "w0": a["L0_ffn_weight"].T,
        "starts": a["L0_ffn_lora_start_indices"],
        "wk1": a["L1_xattn_Wk"].T, "wq1": a["L1_xattn_Wq"].T, "wv1": a["L1_xattn_Wv"].T,
        "biases": np.stack([a["L1_xattn_bk"], a["L1_xattn_bq"]]).reshape(2, C, P).transpose(2, 0, 1),
        "bv1": a["L1_xattn_bv"],
        "wbase": a["L1_ffn_W_base"].T, "bbase": a["L1_ffn_b_base"],
        "enc": np.concatenate([a["L1_ffn_enc0"], a["L1_ffn_enc1"]], axis=0),
        "coefs": packed(a["L1_ffn_coefs0"], a["L1_ffn_coefs1"]),
        "masks": packed(a["L1_ffn_mask0"], a["L1_ffn_mask1"]).reshape(P, -1).view(np.int32),
        "dft": dft, "eye": np.eye(P, dtype=f), "table": table,
    }
    nc = bacc.Bacc("TRN2", target_bir_lowering=False, num_devices=1)
    feeds, args = {}, []
    for name, v in arrays.items():
        v = np.ascontiguousarray(v)
        feeds[f"in_{name}"] = v
        args.append(nc.dram_tensor(f"in_{name}", v.shape, _mybir.dt.from_np(v.dtype), kind="ExternalInput").ap())
    args.append(nc.dram_tensor("out_0", (B, S, D), F32, kind="ExternalOutput").ap())
    build(nc, *args)
    r = run(nc, [feeds], core_ids=[0])
    return r.results[0]["out_0"]
```
